# Optimizing a Trainium2 kernel written in Bass

```python
import numpy as np
import jax
import jax.numpy as jnp

def _softmax(x, axis=-1):
    return jax.nn.softmax(x, axis=axis)

def _gelu(x):
    return jax.nn.gelu(x, approximate=True)

def _silu(x):
    return jax.nn.silu(x)

def _sigmoid(x):
    return jax.nn.sigmoid(x)

def _layernorm(x, axis=-1, eps=1e-05):
    m = jnp.mean(x, axis=axis, keepdims=True)
    v = jnp.var(x, axis=axis, keepdims=True)
    return (x - m) / jnp.sqrt(v + eps)

def _scatter_add(tgt, idx, src, axis=0):
    return tgt.at[idx].add(src)

def _segment_sum(src, seg, n):
    return jax.ops.segment_sum(src, seg, n)
kernel_name = 'mk_conv_preact_d4_conv_nchw512_r2_b0df36'

def setup_inputs(seed: int=0):
    np.random.seed(seed)
    _w = jnp.asarray

    def _rec_inputs():
        import jax
        import jax.numpy as jnp
        _gk = jax.random.key(seed)
        x = -0.0002928 + 1 * jax.random.normal(jax.random.fold_in(_gk, 1), (2, 256, 32, 32), jnp.float32)
        return x
    x = _rec_inputs()

    def _L0_conv_setup():
        import jax, jax.numpy as jnp
        import numpy as np
        C = 256
        G = 16
        Cg = C // G
        K = 3
        P = K * K
        PAD = 1
        STRIDE = 1
        DIL = 1
        DWK = 3
        OFFSET_SCALE = 1.0
        LN_EPS = 1e-05

        def _dcnv3_core(x, offset, mask):
            N, H, W, _ = x.shape
            Hin, Win = (H + 2 * PAD, W + 2 * PAD)
            Hout, Wout = (H, W)
            xpad = jnp.pad(x, ((0, 0), (PAD, PAD), (PAD, PAD), (0, 0)))
            base = DIL * (K - 1) // 2 + 0.5
            ref_y = (base + jnp.arange(Hout, dtype=jnp.float32) * STRIDE) / Hin
            ref_x = (base + jnp.arange(Wout, dtype=jnp.float32) * STRIDE) / Win
            ref = jnp.stack(jnp.broadcast_arrays(ref_x[None, :], ref_y[:, None]), -1)
            g1 = jnp.arange(K, dtype=jnp.float32) * DIL - DIL * (K - 1) // 2
            gxx, gyy = jnp.meshgrid(g1 / Win, g1 / Hin, indexing='ij')
            grid = jnp.stack([gxx, gyy], -1).reshape(P, 2)
            off = offset.reshape(N, Hout, Wout, G, P, 2)
            norm = jnp.array([Win, Hin], jnp.float32)
            loc = ref[None, :, :, None, None, :] + grid * OFFSET_SCALE + off * OFFSET_SCALE / norm
            px = loc[..., 0] * Win - 0.5
            py = loc[..., 1] * Hin - 0.5
            xg = xpad.reshape(N, Hin, Win, G, Cg).transpose(0, 3, 1, 2, 4).reshape(N * G, Hin, Win, Cg)
            pxg = px.transpose(0, 3, 1, 2, 4).reshape(N * G, Hout, Wout, P)
            pyg = py.transpose(0, 3, 1, 2, 4).reshape(N * G, Hout, Wout, P)
            mg = mask.transpose(0, 3, 1, 2, 4).reshape(N * G, Hout, Wout, P)

            def bilin(img, bx, by, m):
                x0 = jnp.floor(bx)
                y0 = jnp.floor(by)
                wx = (bx - x0)[..., None]
                wy = (by - y0)[..., None]
                x0i = x0.astype(jnp.int32)
                y0i = y0.astype(jnp.int32)

                def g(yy, xx):
                    valid = (yy >= 0) & (yy < Hin) & (xx >= 0) & (xx < Win)
                    v = img[jnp.clip(yy, 0, Hin - 1), jnp.clip(xx, 0, Win - 1)]
                    return v * valid[..., None]
                v00 = g(y0i, x0i)
                v01 = g(y0i, x0i + 1)
                v10 = g(y0i + 1, x0i)
                v11 = g(y0i + 1, x0i + 1)
                samp = (v00 * (1 - wx) + v01 * wx) * (1 - wy) + (v10 * (1 - wx) + v11 * wx) * wy
                return jnp.einsum('hwpc,hwp->hwc', samp, m)
            out = jax.vmap(bilin)(xg, pxg, pyg, mg)
            return out.reshape(N, G, Hout, Wout, Cg).transpose(0, 2, 3, 1, 4).reshape(N, Hout, Wout, C)
        key = jax.random.key(seed)
        ks = jax.random.split(key, 10)
        N, H, W = (2, 32, 32)
        sc = 1.0 / np.sqrt(C)
        return {'x': jax.random.normal(ks[0], (N, C, H, W), jnp.float32), 'dw_w': jax.random.normal(ks[1], (C, 1, DWK, DWK), jnp.float32) * 0.1, 'dw_b': jax.random.normal(ks[2], (C,), jnp.float32) * 0.02, 'ln_g': jnp.ones((C,), jnp.float32), 'ln_b': jnp.zeros((C,), jnp.float32), 'off_w': jax.random.normal(ks[3], (C, G * P * 2), jnp.float32) * 0.01, 'off_b': jax.random.normal(ks[4], (G * P * 2,), jnp.float32) * 0.01, 'mask_w': jax.random.normal(ks[5], (C, G * P), jnp.float32) * 0.01, 'mask_b': jnp.zeros((G * P,), jnp.float32), 'in_w': jax.random.normal(ks[6], (C, C), jnp.float32) * sc, 'in_b': jnp.zeros((C,), jnp.float32), 'out_w': jax.random.normal(ks[7], (C, C), jnp.float32) * sc, 'out_b': jnp.zeros((C,), jnp.float32)}
    _L0_conv_all = _L0_conv_setup()
    _L0_conv_in = {k: v for k, v in _L0_conv_all.items() if k in ('dw_w', 'dw_b', 'ln_g', 'ln_b', 'off_w', 'off_b', 'mask_w', 'mask_b', 'in_w', 'in_b', 'out_w', 'out_b')}
    del _L0_conv_all

    def _L1_conv_setup():
        import jax, jax.numpy as jnp
        import numpy as np
        from jax import lax
        DIM = 256
        MED = 2 * DIM
        NF = 4
        SIZE = 32
        FS = SIZE // 2 + 1
        HR = int(0.5 * DIM)
        HS = int(0.5 * DIM)
        B = 16

        def _conv1x1(x, w, b):
            return jnp.einsum('bchw,oc->bohw', x, w[:, :, 0, 0]) + b[None, :, None, None]

        def _conv3x3(x, w, b):
            return lax.conv_general_dilated(x, w, (1, 1), 'SAME') + b[None, :, None, None]
        key = jax.random.key(seed)
        ks = jax.random.split(key, 12)
        n = lambda k, shape, s=0.02: jax.random.normal(k, shape, jnp.float32) * s
        return dict(x=jax.random.normal(ks[0], (B, DIM, SIZE, SIZE), jnp.float32), w_pw1=n(ks[1], (MED, DIM)), w_pw2=n(ks[2], (DIM, MED)), star_scale=jnp.ones((1,), jnp.float32), star_bias=jnp.zeros((1,), jnp.float32), rw_fc1_w=n(ks[3], (HR, DIM, 1, 1)), rw_fc1_b=jnp.zeros((HR,), jnp.float32), rw_conv_w=n(ks[4], (HR, HR, 1, 1)), rw_conv_b=jnp.zeros((HR,), jnp.float32), rw_fc2_w=n(ks[5], (NF * MED, HR, 1, 1)), rw_fc2_b=jnp.zeros((NF * MED,), jnp.float32), sp_fc1_w=n(ks[6], (HS, DIM, 3, 3)), sp_fc1_b=jnp.zeros((HS,), jnp.float32), sp_fc2_w=n(ks[7], (NF * MED, HS, 3, 3)), sp_fc2_b=jnp.zeros((NF * MED,), jnp.float32), complex_weights=n(ks[8], (SIZE, FS, NF, 2), 0.02), spatial_weights=n(ks[9], (SIZE, SIZE, NF), 0.03))
    _L1_conv_all = _L1_conv_setup()
    _L1_conv_in = {k: v for k, v in _L1_conv_all.items() if k in ('w_pw1', 'w_pw2', 'star_scale', 'star_bias', 'rw_fc1_w', 'rw_fc1_b', 'rw_conv_w', 'rw_conv_b', 'rw_fc2_w', 'rw_fc2_b', 'sp_fc1_w', 'sp_fc1_b', 'sp_fc2_w', 'sp_fc2_b', 'complex_weights', 'spatial_weights')}
    del _L1_conv_all

    def _L2_conv_setup():
        import jax, jax.numpy as jnp
        from jax import lax
        import numpy as np
        DIM = 8
        BN_EPS = 1e-05
        ATT_EPS = 1e-15
        key = jax.random.key(seed)
        ks = jax.random.split(key, 6)
        B, C, H, W = (2, 256, 64, 64)
        total_dim = 256
        c3 = 3 * total_dim
        x = jax.random.normal(ks[0], (B, C, H, W), dtype=jnp.float32)
        w_qkv = jax.random.normal(ks[1], (c3, C), dtype=jnp.float32) * 0.02
        w_dw = jax.random.normal(ks[2], (c3, 1, 5, 5), dtype=jnp.float32) * 0.05
        w_pw = jax.random.normal(ks[3], (c3, 8, 1, 1), dtype=jnp.float32) * 0.1
        w_proj = jax.random.normal(ks[4], (256, 2 * total_dim), dtype=jnp.float32) * 0.02
        bn_gamma = jnp.ones((256,), jnp.float32)
        bn_beta = jnp.zeros((256,), jnp.float32)
        bn_mean = jnp.zeros((256,), jnp.float32)
        bn_var = jnp.ones((256,), jnp.float32)
        return {'x': x, 'w_qkv': w_qkv, 'w_dw': w_dw, 'w_pw': w_pw, 'w_proj': w_proj, 'bn_gamma': bn_gamma, 'bn_beta': bn_beta, 'bn_mean': bn_mean, 'bn_var': bn_var}
    _L2_conv_all = _L2_conv_setup()
    _L2_conv_in = {k: v for k, v in _L2_conv_all.items() if k in ('w_qkv', 'w_dw', 'w_pw', 'w_proj', 'bn_gamma', 'bn_beta', 'bn_mean', 'bn_var')}
    del _L2_conv_all

    def _L3_conv_setup():
        import jax, jax.numpy as jnp
        import numpy as np
        from jax import lax
        EPS = 1e-05
        DW_THRESH = 4.0
        PW_THRESH = 0.001
        C_IN = 256
        C_OUT = 256

        def _bn(x, g, b, m, v):
            inv = g * lax.rsqrt(v + EPS)
            return x * inv[None, :, None, None] + (b - m * inv)[None, :, None, None]

        def _prune(x, thresh):
            amax = jnp.max(jnp.abs(x), axis=(2, 3), keepdims=True)
            return jnp.where(amax < thresh, jnp.zeros_like(x), x)
        key = jax.random.key(seed)
        ks = jax.random.split(key, 8)
        B, H, W = (32, 28, 28)
        x = jax.random.normal(ks[0], (B, C_IN, H, W), dtype=jnp.float32)
        dw_w = jax.random.normal(ks[1], (C_IN, 1, 3, 3), dtype=jnp.float32) * 0.1
        dw_b = jax.random.normal(ks[2], (C_IN,), dtype=jnp.float32) * 0.1
        bn1_g = jnp.ones((C_IN,), jnp.float32)
        bn1_b = jnp.zeros((C_IN,), jnp.float32)
        bn1_m = jnp.zeros((C_IN,), jnp.float32)
        bn1_v = jnp.ones((C_IN,), jnp.float32)
        pw_w = jax.random.normal(ks[3], (C_OUT, C_IN, 1, 1), dtype=jnp.float32) * 0.05
        pw_b = jax.random.normal(ks[4], (C_OUT,), dtype=jnp.float32) * 0.1
        bn2_g = jnp.ones((C_OUT,), jnp.float32)
        bn2_b = jnp.zeros((C_OUT,), jnp.float32)
        bn2_m = jnp.zeros((C_OUT,), jnp.float32)
        bn2_v = jnp.ones((C_OUT,), jnp.float32)
        return dict(x=x, dw_w=dw_w, dw_b=dw_b, bn1_g=bn1_g, bn1_b=bn1_b, bn1_m=bn1_m, bn1_v=bn1_v, pw_w=pw_w, pw_b=pw_b, bn2_g=bn2_g, bn2_b=bn2_b, bn2_m=bn2_m, bn2_v=bn2_v)
    _L3_conv_all = _L3_conv_setup()
    _L3_conv_in = {k: v for k, v in _L3_conv_all.items() if k in ('dw_w', 'dw_b', 'bn1_g', 'bn1_b', 'bn1_m', 'bn1_v', 'pw_w', 'pw_b', 'bn2_g', 'bn2_b', 'bn2_m', 'bn2_v')}
    del _L3_conv_all
    return {'x': x, 'L0_conv_dw_w': _L0_conv_in['dw_w'], 'L0_conv_dw_b': _L0_conv_in['dw_b'], 'L0_conv_ln_g': _L0_conv_in['ln_g'], 'L0_conv_ln_b': _L0_conv_in['ln_b'], 'L0_conv_off_w': _L0_conv_in['off_w'], 'L0_conv_off_b': _L0_conv_in['off_b'], 'L0_conv_mask_w': _L0_conv_in['mask_w'], 'L0_conv_mask_b': _L0_conv_in['mask_b'], 'L0_conv_in_w': _L0_conv_in['in_w'], 'L0_conv_in_b': _L0_conv_in['in_b'], 'L0_conv_out_w': _L0_conv_in['out_w'], 'L0_conv_out_b': _L0_conv_in['out_b'], 'L1_conv_w_pw1': _L1_conv_in['w_pw1'], 'L1_conv_w_pw2': _L1_conv_in['w_pw2'], 'L1_conv_star_scale': _L1_conv_in['star_scale'], 'L1_conv_star_bias': _L1_conv_in['star_bias'], 'L1_conv_rw_fc1_w': _L1_conv_in['rw_fc1_w'], 'L1_conv_rw_fc1_b': _L1_conv_in['rw_fc1_b'], 'L1_conv_rw_conv_w': _L1_conv_in['rw_conv_w'], 'L1_conv_rw_conv_b': _L1_conv_in['rw_conv_b'], 'L1_conv_rw_fc2_w': _L1_conv_in['rw_fc2_w'], 'L1_conv_rw_fc2_b': _L1_conv_in['rw_fc2_b'], 'L1_conv_sp_fc1_w': _L1_conv_in['sp_fc1_w'], 'L1_conv_sp_fc1_b': _L1_conv_in['sp_fc1_b'], 'L1_conv_sp_fc2_w': _L1_conv_in['sp_fc2_w'], 'L1_conv_sp_fc2_b': _L1_conv_in['sp_fc2_b'], 'L1_conv_complex_weights': _L1_conv_in['complex_weights'], 'L1_conv_spatial_weights': _L1_conv_in['spatial_weights'], 'L2_conv_w_qkv': _L2_conv_in['w_qkv'], 'L2_conv_w_dw': _L2_conv_in['w_dw'], 'L2_conv_w_pw': _L2_conv_in['w_pw'], 'L2_conv_w_proj': _L2_conv_in['w_proj'], 'L2_conv_bn_gamma': _L2_conv_in['bn_gamma'], 'L2_conv_bn_beta': _L2_conv_in['bn_beta'], 'L2_conv_bn_mean': _L2_conv_in['bn_mean'], 'L2_conv_bn_var': _L2_conv_in['bn_var'], 'L3_conv_dw_w': _L3_conv_in['dw_w'], 'L3_conv_dw_b': _L3_conv_in['dw_b'], 'L3_conv_bn1_g': _L3_conv_in['bn1_g'], 'L3_conv_bn1_b': _L3_conv_in['bn1_b'], 'L3_conv_bn1_m': _L3_conv_in['bn1_m'], 'L3_conv_bn1_v': _L3_conv_in['bn1_v'], 'L3_conv_pw_w': _L3_conv_in['pw_w'], 'L3_conv_pw_b': _L3_conv_in['pw_b'], 'L3_conv_bn2_g': _L3_conv_in['bn2_g'], 'L3_conv_bn2_b': _L3_conv_in['bn2_b'], 'L3_conv_bn2_m': _L3_conv_in['bn2_m'], 'L3_conv_bn2_v': _L3_conv_in['bn2_v']}

def reference(x, L0_conv_dw_w, L0_conv_dw_b, L0_conv_ln_g, L0_conv_ln_b, L0_conv_off_w, L0_conv_off_b, L0_conv_mask_w, L0_conv_mask_b, L0_conv_in_w, L0_conv_in_b, L0_conv_out_w, L0_conv_out_b, L1_conv_w_pw1, L1_conv_w_pw2, L1_conv_star_scale, L1_conv_star_bias, L1_conv_rw_fc1_w, L1_conv_rw_fc1_b, L1_conv_rw_conv_w, L1_conv_rw_conv_b, L1_conv_rw_fc2_w, L1_conv_rw_fc2_b, L1_conv_sp_fc1_w, L1_conv_sp_fc1_b, L1_conv_sp_fc2_w, L1_conv_sp_fc2_b, L1_conv_complex_weights, L1_conv_spatial_weights, L2_conv_w_qkv, L2_conv_w_dw, L2_conv_w_pw, L2_conv_w_proj, L2_conv_bn_gamma, L2_conv_bn_beta, L2_conv_bn_mean, L2_conv_bn_var, L3_conv_dw_w, L3_conv_dw_b, L3_conv_bn1_g, L3_conv_bn1_b, L3_conv_bn1_m, L3_conv_bn1_v, L3_conv_pw_w, L3_conv_pw_b, L3_conv_bn2_g, L3_conv_bn2_b, L3_conv_bn2_m, L3_conv_bn2_v):
    import jax
    import jax.numpy as jnp

    def _L0_conv_ref(x, dw_w, dw_b, ln_g, ln_b, off_w, off_b, mask_w, mask_b, in_w, in_b, out_w, out_b):
        import jax, jax.numpy as jnp
        import numpy as np
        C = 256
        G = 16
        Cg = C // G
        K = 3
        P = K * K
        PAD = 1
        STRIDE = 1
        DIL = 1
        DWK = 3
        OFFSET_SCALE = 1.0
        LN_EPS = 1e-05

        def _dcnv3_core(x, offset, mask):
            N, H, W, _ = x.shape
            Hin, Win = (H + 2 * PAD, W + 2 * PAD)
            Hout, Wout = (H, W)
            xpad = jnp.pad(x, ((0, 0), (PAD, PAD), (PAD, PAD), (0, 0)))
            base = DIL * (K - 1) // 2 + 0.5
            ref_y = (base + jnp.arange(Hout, dtype=jnp.float32) * STRIDE) / Hin
            ref_x = (base + jnp.arange(Wout, dtype=jnp.float32) * STRIDE) / Win
            ref = jnp.stack(jnp.broadcast_arrays(ref_x[None, :], ref_y[:, None]), -1)
            g1 = jnp.arange(K, dtype=jnp.float32) * DIL - DIL * (K - 1) // 2
            gxx, gyy = jnp.meshgrid(g1 / Win, g1 / Hin, indexing='ij')
            grid = jnp.stack([gxx, gyy], -1).reshape(P, 2)
            off = offset.reshape(N, Hout, Wout, G, P, 2)
            norm = jnp.array([Win, Hin], jnp.float32)
            loc = ref[None, :, :, None, None, :] + grid * OFFSET_SCALE + off * OFFSET_SCALE / norm
            px = loc[..., 0] * Win - 0.5
            py = loc[..., 1] * Hin - 0.5
            xg = xpad.reshape(N, Hin, Win, G, Cg).transpose(0, 3, 1, 2, 4).reshape(N * G, Hin, Win, Cg)
            pxg = px.transpose(0, 3, 1, 2, 4).reshape(N * G, Hout, Wout, P)
            pyg = py.transpose(0, 3, 1, 2, 4).reshape(N * G, Hout, Wout, P)
            mg = mask.transpose(0, 3, 1, 2, 4).reshape(N * G, Hout, Wout, P)

            def bilin(img, bx, by, m):
                x0 = jnp.floor(bx)
                y0 = jnp.floor(by)
                wx = (bx - x0)[..., None]
                wy = (by - y0)[..., None]
                x0i = x0.astype(jnp.int32)
                y0i = y0.astype(jnp.int32)

                def g(yy, xx):
                    valid = (yy >= 0) & (yy < Hin) & (xx >= 0) & (xx < Win)
                    v = img[jnp.clip(yy, 0, Hin - 1), jnp.clip(xx, 0, Win - 1)]
                    return v * valid[..., None]
                v00 = g(y0i, x0i)
                v01 = g(y0i, x0i + 1)
                v10 = g(y0i + 1, x0i)
                v11 = g(y0i + 1, x0i + 1)
                samp = (v00 * (1 - wx) + v01 * wx) * (1 - wy) + (v10 * (1 - wx) + v11 * wx) * wy
                return jnp.einsum('hwpc,hwp->hwc', samp, m)
            out = jax.vmap(bilin)(xg, pxg, pyg, mg)
            return out.reshape(N, G, Hout, Wout, Cg).transpose(0, 2, 3, 1, 4).reshape(N, Hout, Wout, C)
        N, _, H, W = x.shape
        inp = jnp.transpose(x, (0, 2, 3, 1))
        xproj = inp @ in_w + in_b
        x1 = jax.lax.conv_general_dilated(x, dw_w, (1, 1), [((DWK - 1) // 2, (DWK - 1) // 2)] * 2, feature_group_count=C, dimension_numbers=('NCHW', 'OIHW', 'NCHW'))
        x1 = jnp.transpose(x1, (0, 2, 3, 1)) + dw_b
        mu = x1.mean(-1, keepdims=True)
        var = ((x1 - mu) ** 2).mean(-1, keepdims=True)
        x1 = (x1 - mu) / jnp.sqrt(var + LN_EPS) * ln_g + ln_b
        x1 = jax.nn.gelu(x1, approximate=False)
        offset = x1 @ off_w + off_b
        mask = jax.nn.softmax((x1 @ mask_w + mask_b).reshape(N, H, W, G, P), -1)
        out = _dcnv3_core(xproj, offset, mask)
        out = out @ out_w + out_b
        return jnp.transpose(out, (0, 3, 1, 2))

    def _L1_conv_ref(x, w_pw1, w_pw2, star_scale, star_bias, rw_fc1_w, rw_fc1_b, rw_conv_w, rw_conv_b, rw_fc2_w, rw_fc2_b, sp_fc1_w, sp_fc1_b, sp_fc2_w, sp_fc2_b, complex_weights, spatial_weights):
        import jax, jax.numpy as jnp
        import numpy as np
        from jax import lax
        DIM = 256
        MED = 2 * DIM
        NF = 4
        SIZE = 32
        FS = SIZE // 2 + 1
        HR = int(0.5 * DIM)
        HS = int(0.5 * DIM)
        B = 16

        def _conv1x1(x, w, b):
            return jnp.einsum('bchw,oc->bohw', x, w[:, :, 0, 0]) + b[None, :, None, None]

        def _conv3x3(x, w, b):
            return lax.conv_general_dilated(x, w, (1, 1), 'SAME') + b[None, :, None, None]
        Bn, _, H, W = x.shape
        r = jax.nn.relu(_conv1x1(x, rw_fc1_w, rw_fc1_b))
        r = jax.nn.relu(_conv1x1(r, rw_conv_w, rw_conv_b))
        r = _conv1x1(r, rw_fc2_w, rw_fc2_b)
        routeing = jax.nn.softmax(r.mean(axis=(2, 3)).reshape(Bn, NF, MED), axis=1)
        s = jax.nn.relu(_conv3x3(x, sp_fc1_w, sp_fc1_b))
        s = _conv3x3(s, sp_fc2_w, sp_fc2_b)
        spatial_routeing = jax.nn.softmax(s.mean(axis=(2, 3)).reshape(Bn, NF, MED), axis=1)
        xc = jnp.transpose(x, (0, 2, 3, 1))
        xp = jnp.einsum('bhwc,mc->bhwm', xc, w_pw1)
        xp = star_scale * jnp.square(jax.nn.relu(xp)) + star_bias
        xf = jnp.fft.rfft2(xp, axes=(1, 2), norm='ortho')
        cw = lax.complex(complex_weights[..., 0], complex_weights[..., 1])
        weight = jnp.einsum('bfc,hwf->bhwc', routeing.astype(cw.dtype), cw)
        spatial_weight = jnp.einsum('bfc,hwf->bhwc', spatial_routeing, spatial_weights)
        xs = jnp.fft.irfft2(xf * weight, s=(H, W), axes=(1, 2), norm='ortho')
        out = xp * spatial_weight + xs
        out = jnp.einsum('bhwm,dm->bhwd', out, w_pw2)
        return jnp.transpose(out, (0, 3, 1, 2))

    def _L2_conv_ref(x, w_qkv, w_dw, w_pw, w_proj, bn_gamma, bn_beta, bn_mean, bn_var):
        import jax, jax.numpy as jnp
        from jax import lax
        import numpy as np
        DIM = 8
        BN_EPS = 1e-05
        ATT_EPS = 1e-15
        B, C, H, W = x.shape
        dn = ('NCHW', 'OIHW', 'NCHW')
        qkv = jnp.einsum('bchw,oc->bohw', x, w_qkv)
        y = lax.conv_general_dilated(qkv, w_dw, (1, 1), [(2, 2), (2, 2)], feature_group_count=w_dw.shape[0], dimension_numbers=dn)
        y = lax.conv_general_dilated(y, w_pw, (1, 1), [(0, 0), (0, 0)], feature_group_count=w_pw.shape[0] // w_pw.shape[1], dimension_numbers=dn)
        mqkv = jnp.concatenate([qkv, y], axis=1)
        N = H * W
        mqkv = mqkv.reshape(B, -1, 3 * DIM, N)
        q = jax.nn.relu(mqkv[:, :, :DIM])
        k = jax.nn.relu(mqkv[:, :, DIM:2 * DIM])
        v = mqkv[:, :, 2 * DIM:]
        v = jnp.pad(v, ((0, 0), (0, 0), (0, 1), (0, 0)), constant_values=1.0)
        vk = jnp.einsum('bhdn,bhen->bhde', v, k)
        out = jnp.einsum('bhde,bhen->bhdn', vk, q)
        out = out[:, :, :-1] / (out[:, :, -1:] + ATT_EPS)
        out = out.reshape(B, -1, H, W)
        out = jnp.einsum('bchw,oc->bohw', out, w_proj)
        inv = bn_gamma / jnp.sqrt(bn_var + BN_EPS)
        out = out * inv[None, :, None, None] + (bn_beta - bn_mean * inv)[None, :, None, None]
        return out

    def _L3_conv_ref(x, dw_w, dw_b, bn1_g, bn1_b, bn1_m, bn1_v, pw_w, pw_b, bn2_g, bn2_b, bn2_m, bn2_v):
        import jax, jax.numpy as jnp
        import numpy as np
        from jax import lax
        EPS = 1e-05
        DW_THRESH = 4.0
        PW_THRESH = 0.001
        C_IN = 256
        C_OUT = 256

        def _bn(x, g, b, m, v):
            inv = g * lax.rsqrt(v + EPS)
            return x * inv[None, :, None, None] + (b - m * inv)[None, :, None, None]

        def _prune(x, thresh):
            amax = jnp.max(jnp.abs(x), axis=(2, 3), keepdims=True)
            return jnp.where(amax < thresh, jnp.zeros_like(x), x)
        dn = ('NCHW', 'OIHW', 'NCHW')
        h = lax.conv_general_dilated(x, dw_w, window_strides=(1, 1), padding=((1, 1), (1, 1)), feature_group_count=C_IN, dimension_numbers=dn)
        h = h + dw_b[None, :, None, None]
        h = jax.nn.relu(_bn(h, bn1_g, bn1_b, bn1_m, bn1_v))
        h = _prune(h, DW_THRESH)
        h = lax.conv_general_dilated(h, pw_w, window_strides=(1, 1), padding=((0, 0), (0, 0)), dimension_numbers=dn)
        h = h + pw_b[None, :, None, None]
        h = jax.nn.relu(_bn(h, bn2_g, bn2_b, bn2_m, bn2_v))
        h = _prune(h, PW_THRESH)
        return h

    def _gn(v, G=32, eps=1e-05):
        B_, C_, H_, W_ = v.shape
        g = v.reshape(B_, G, C_ // G, H_, W_)
        m = jnp.mean(g, axis=(2, 3, 4), keepdims=True)
        s = jnp.var(g, axis=(2, 3, 4), keepdims=True)
        return ((g - m) / jnp.sqrt(s + eps)).reshape(v.shape)

    def _ln_c(v, eps=1e-06):
        m = jnp.mean(v, axis=1, keepdims=True)
        s = jnp.var(v, axis=1, keepdims=True)
        return (v - m) / jnp.sqrt(s + eps)

    def _ln_t(v, eps=1e-05):
        m = jnp.mean(v, axis=-1, keepdims=True)
        s = jnp.var(v, axis=-1, keepdims=True)
        return (v - m) / jnp.sqrt(s + eps)

    def _to_tokens(v):
        B_, C_, H_, W_ = v.shape
        return v.reshape(B_, C_, H_ * W_).transpose(0, 2, 1)

    def _from_tokens(t, like):
        B_, C_, H_, W_ = like.shape
        return t.transpose(0, 2, 1).reshape(B_, C_, H_, W_)
    x = x + _L0_conv_ref(_gn(x), L0_conv_dw_w, L0_conv_dw_b, L0_conv_ln_g, L0_conv_ln_b, L0_conv_off_w, L0_conv_off_b, L0_conv_mask_w, L0_conv_mask_b, L0_conv_in_w, L0_conv_in_b, L0_conv_out_w, L0_conv_out_b)
    x = x + _L1_conv_ref(_gn(x), L1_conv_w_pw1, L1_conv_w_pw2, L1_conv_star_scale, L1_conv_star_bias, L1_conv_rw_fc1_w, L1_conv_rw_fc1_b, L1_conv_rw_conv_w, L1_conv_rw_conv_b, L1_conv_rw_fc2_w, L1_conv_rw_fc2_b, L1_conv_sp_fc1_w, L1_conv_sp_fc1_b, L1_conv_sp_fc2_w, L1_conv_sp_fc2_b, L1_conv_complex_weights, L1_conv_spatial_weights)
    x = x + _L2_conv_ref(_gn(x), L2_conv_w_qkv, L2_conv_w_dw, L2_conv_w_pw, L2_conv_w_proj, L2_conv_bn_gamma, L2_conv_bn_beta, L2_conv_bn_mean, L2_conv_bn_var)
    x = x + _L3_conv_ref(_gn(x), L3_conv_dw_w, L3_conv_dw_b, L3_conv_bn1_g, L3_conv_bn1_b, L3_conv_bn1_m, L3_conv_bn1_v, L3_conv_pw_w, L3_conv_pw_b, L3_conv_bn2_g, L3_conv_bn2_b, L3_conv_bn2_m, L3_conv_bn2_v)
    return x

_drawn_inputs = setup_inputs


def setup_inputs(seed=0):
    import zlib

    import numpy as np

    out = dict(_drawn_inputs(seed))
    spreads = {'L0_conv_ln_g': (1.0, 0.6),
     'L0_conv_ln_b': (0.0, 0.8),
     'L0_conv_in_b': (0.0, 0.1),
     'L0_conv_out_b': (0.0, 0.1),
     'L1_conv_rw_fc1_b': (0.0, 0.8),
     'L1_conv_rw_conv_b': (0.0, 0.8),
     'L1_conv_rw_fc2_b': (0.0, 0.8),
     'L1_conv_sp_fc1_b': (0.0, 0.8),
     'L1_conv_sp_fc2_b': (0.0, 0.8),
     'L2_conv_bn_gamma': (1.0, 0.6),
     'L2_conv_bn_beta': (0.0, 0.764),
     'L2_conv_bn_mean': (0.0, 0.408),
     'L2_conv_bn_var': (1.0, 0.6),
     'L3_conv_bn1_g': (1.0, 0.6),
     'L3_conv_bn1_b': (0.0, 0.8),
     'L3_conv_bn1_m': (0.0, 0.8),
     'L3_conv_bn1_v': (1.0, 0.6),
     'L3_conv_bn2_g': (1.0, 0.6),
     'L3_conv_bn2_b': (0.0, 2.0),
     'L3_conv_bn2_m': (0.0, 0.795),
     'L3_conv_bn2_v': (1.0, 0.6)}
    factors = {'L0_conv_dw_b': 8.0,
     'L0_conv_off_b': 8.0,
     'L1_conv_w_pw1': 8.0,
     'L1_conv_w_pw2': 8.0,
     'L1_conv_rw_fc1_w': 8.0,
     'L1_conv_rw_conv_w': 8.0,
     'L1_conv_rw_fc2_w': 8.0,
     'L1_conv_sp_fc1_w': 8.0,
     'L1_conv_sp_fc2_w': 8.0,
     'L1_conv_complex_weights': 8.0,
     'L1_conv_spatial_weights': 8.0,
     'L2_conv_w_qkv': 4.501,
     'L2_conv_w_dw': 8.0,
     'L2_conv_w_pw': 8.0,
     'L2_conv_w_proj': 4.456,
     'L3_conv_dw_w': 8.0,
     'L3_conv_dw_b': 8.0,
     'L3_conv_pw_w': 8.0,
     'L3_conv_pw_b': 4.454}
    for name, (base, spread) in spreads.items():
        noise = np.random.default_rng([zlib.crc32(name.encode()), seed]).standard_normal(out[name].shape)
        drawn = base * np.exp(spread * noise) if base else spread * noise
        out[name] = jnp.asarray(drawn.astype(out[name].dtype))
    for name, factor in factors.items():
        out[name] = (out[name] * factor).astype(out[name].dtype)
    return out
```

```python
from contextlib import ExitStack

import numpy as np
import concourse.bass as bass
from concourse import mybir

F32 = mybir.dt.float32
I32 = mybir.dt.int32
ALU = mybir.AluOpType
ACT = mybir.ActivationFunctionType
AX = mybir.AxisListType

B, C, H, W = 2, 256, 32, 32
PIX = H * W
P = 128
HALVES = C // P
COLS = B * PIX
PAD = 2
HP = H + 2 * PAD
BANK = 512
CHUNKS = COLS // BANK
G, K2 = 16, 9
XX = W // 2
NOM = 3 * G * K2
GH = G // HALVES
CG = C // G
XG = XX * GH
NPT = K2 * XG
ND = 5
MED, NF = 2 * C, 4
KM = MED // P
WT = 8
TILES = B * WT
QKV_TILES = 6
K5 = 25
TENSOR_TAPS = [3, 3, 3, 3, 5, 5]
QROW = H + 4
ATT_EPS = 1e-15
DW_THRESH, PW_THRESH = 4.0, 0.001
GN_EPS = 1e-5
REACH = H
PADDED = H + 2 * REACH
LAST_LAYER = 3


class Steps:

    def __init__(self, engine, sem):
        self.engine, self.sem, self.n = engine, sem, 0

    def add(self, ins):
        ins.then_inc(self.sem, 1)
        self.n += 1
        return self.n

    def link(self, ins):
        self.add(ins)
        self.engine.wait_ge(self.sem, self.n)

    def upto(self, n):
        self.engine.wait_ge(self.sem, n)


def channel_columns():
    names, at = {}, 0
    for name, width in (("dw0_w", 18), ("dw0_b", 2), ("ln_g", 2), ("ln_b", 2), ("out_b", 2),
                        ("star_scale", 1), ("star_bias", 1), ("fc1_b", 1), ("conv_b", 1), ("sp1_b", 1),
                        ("dw2_w", 150), ("dw3_w", 18), ("bn_g", 6), ("bn_b", 6), ("bn_m", 6), ("bn_v", 6),
                        ("l3_b", 4)):
        names[name] = (at, at + width)
        at += width
    return names, at


def mixer_kernel(nc, x_in, out, w, xpad_dram, general_dram, LAST):
    cv_at, cv_n = channel_columns()
    with ExitStack() as ctx:
        def sem(name):
            return ctx.enter_context(nc.semaphore(name))

        arena_words = 53000
        arena = ctx.enter_context(nc.sbuf_tensor("arena", [P, arena_words], F32))
        psum = ctx.enter_context(nc.psum_tensor("psum", [P, 8, BANK], F32))

        def words(at, n):
            assert at + n <= arena_words, (at, n)
            return arena[:, at:at + n]

        top = [0]

        def take(n):
            top[0] += n
            return words(top[0] - n, n)

        X = take(HALVES * COLS).rearrange("p (h b q) -> p h b q", h=HALVES, b=B)
        Z = take(HALVES * B * HP * HP).rearrange("p (i y x) -> p i y x", y=HP, x=HP)
        z_base = HALVES * COLS
        ident = take(P)
        gmean = take(P)
        head_mask = take(P)
        cv = take(cv_n)
        small = take(512)
        L = top[0]

        def col(name, i=0, n=1):
            a, _ = cv_at[name]
            return cv[:, a + i:a + i + n]

        Xi = X.rearrange("p h b (y x) -> p (h b) y x", y=H)

        def z_inner(i):
            return Z[:, i, PAD:PAD + H, PAD:PAD + W]

        st = small[:, 0:48].rearrange("p (i c s) -> p i c s", i=4, c=2)
        mv = small[:, 48:56].rearrange("p (i s) -> p i s", s=2)
        gq = small[:, 56:64].rearrange("p (s i) -> p s i", s=2)
        gm = small[:, 64:72].rearrange("p (s i) -> p s i", s=2)
        gvar, gsd, grs, gt, gnb = (small[:, 72 + 4 * j:76 + 4 * j] for j in range(5))
        amax, amax_all, within = (small[:, 92 + j:93 + j] for j in range(3))
        beyond = small[:, 95:96].bitcast(I32)
        hat_shift = small[:, 96:99]
        valid_halo = small[:, 99:103]
        ln_st = small[:, 104:200].rearrange("p (x s) -> p x s", s=6)
        ln_mv = small[:, 200:232].rearrange("p (x s) -> p x s", s=2)
        ln_var, ln_sd, ln_rs, ln_t, ln_nb = (small[:, 232 + 16 * j:248 + 16 * j] for j in range(5))

        s_x, s_const, s_w0 = sem("x_loaded"), sem("consts_loaded"), sem("l0_weights_loaded")
        s_gn_stats, s_gn_means, s_gn_var = sem("gn_stats"), sem("gn_group_means"), sem("gn_var")
        s_gn_sd, s_gn_coef, s_z = sem("gn_sd"), sem("gn_coef"), sem("z_padded_written")
        s_zc = sem("z_unpadded_written")
        s_zb = sem("z_border_zero")
        s_x_new = sem("x_updated")
        s_dve, s_act, s_pool = sem("dve_steps"), sem("act_steps"), sem("pool_steps")
        s_out = sem("output_stored")

        o = L
        inw = words(o, 512).rearrange("p (k c) -> p k c", k=2); o += 512
        omw = words(o, 2 * NOM).rearrange("p (k c) -> p k c", k=2); o += 2 * NOM
        outw = words(o, 512).rearrange("p (k c) -> p k c", k=2); o += 512
        inb = words(o, C); o += C
        omb = words(o, NOM); o += NOM
        XSc = words(o, (XX + 4) * C).rearrange("p (x c) -> p x c", c=C); o += (XX + 4) * C
        XSd = words(o, 4 * (XX + 4) * P).rearrange("p (d x c) -> p d x c", d=4, c=P); o += 4 * (XX + 4) * P
        r1 = o; o += 2 * HALVES * COLS
        Zc = words(o, HALVES * COLS).rearrange("p (i q) -> p i q", q=PIX)
        OM = words(o, XX * NOM).rearrange("p (x o) -> p x o", o=NOM); o += XX * NOM
        mask = words(o, 2 * NPT).rearrange("p (h k g) -> p h k g", h=2, k=K2); o += 2 * NPT
        wd_at = o
        Wd = words(o, ND * ND * XG).rearrange("p (i j g) -> p i j g", i=ND, j=ND); o += ND * ND * XG
        prod2 = words(o, 2048); o += 2048
        general_scratch_end = o
        x1cm = words(r1, HALVES * COLS).rearrange("p (h q) -> p h q", h=HALVES)
        x1n = words(r1 + HALVES * COLS, HALVES * COLS).rearrange("p (x c) -> p x c", c=C)
        g1cm = words(r1, HALVES * COLS).rearrange("p (h x q) -> p h x q", h=HALVES, x=XX)
        hats = words(r1, 6 * NPT).rearrange("p (a k g) -> p a k g", a=6, k=K2)
        wk = words(r1 + 6 * NPT, NPT)
        prods = [words(z_base, 2048), words(z_base + 2048, 2048), prod2]
        sm_t = words(z_base + 4096, 2 * XG).rearrange("p (h g) -> p h g", h=2)
        sm_r = words(z_base + 4096 + 2 * XG, 2 * XG).rearrange("p (h g) -> p h g", h=2)
        Wds = [Wd, OM.rearrange("p x o -> p (x o)")[:, 0:ND * ND * XG].rearrange("p (i j g) -> p i j g", i=ND, j=ND)]
        outT = words(r1, HALVES * COLS).rearrange("p (h x q) -> p h x q", h=HALVES, x=XX)

        s_xp, s_xpe = sem("xproj_ready"), sem("xproj_evacuated")
        s_shift = [sem(f"xproj_shifted_{j}") for j in range(4)]
        s_shz = sem("shift_border_zero")
        s_x1 = sem("x1_ready")
        s_lnv, s_lnsd = sem("ln_var"), sem("ln_sd")
        s_x1t, s_x1n = sem("x1_turned"), sem("x1_normalised")
        s_back, s_g1 = sem("x1n_turned_back"), sem("gelu_done")
        s_om, s_ome = sem("offset_mask_ready"), sem("offset_mask_evacuated")
        s_lgs, s_exp = sem("mask_logits_shifted"), sem("mask_exp")
        s_amax, s_flag = sem("offset_amax"), sem("offset_flag")
        s_mask, s_general = sem("mask_ready"), sem("general_path_done")
        s_abs, s_wd, s_absfree = sem("hat_distance"), sem("displacement_weights"), sem("hats_used")
        s_pd, s_pp = sem("product_by_dve"), sem("product_by_pool")
        s_acc = sem("product_accumulated")
        s_outT, s_op, s_halo = sem("sampled_evacuated"), sem("out_projected"), sem("halo_columns")
        s_gen, s_gstep = sem("general_dma"), sem("general_step")

        o = L
        fc1w = words(o, 2 * P).rearrange("p (k c) -> p k c", k=2); o += 2 * P
        convw = words(o, P); o += P
        pw1w = words(o, 2 * MED).rearrange("p (k c) -> p k c", k=2); o += 2 * MED
        sp1w = words(o, 18 * P).rearrange("p (k t c) -> p k t c", k=2, t=9)
        sm_tmp = words(o, 2 * MED)[0:4].rearrange("p (a c) -> p a c", a=2); o += 18 * P
        pw2w = words(o, KM * C).rearrange("p (k c) -> p k c", k=KM); o += KM * C
        dft = words(o, 8 * P).rearrange("p (a m) -> p a m", a=8); o += 8 * P
        cwe = words(o, 2 * 1024)[0:NF].rearrange("p (a m) -> p a m", a=2); o += 2048
        spw = words(o, 1024)[0:NF]; o += 1024
        stream = [words(o + 2048 * j, 2048) for j in range(3)]; o += 3 * 2048
        route = stream[2][0:NF].rearrange("p (r c) -> p r c", r=4)
        sr_act = words(o, COLS)
        route_sm = sr_act[0:4, :]; o += COLS
        Zc1 = words(o, HALVES * COLS).rearrange("p (i q) -> p i q", q=PIX)
        V = [words(o + 4096 * b, 4096).rearrange("p (t c) -> p t c", t=WT) for b in range(B)]; o += 8192
        craw = words(o, 4096)[0:NF].rearrange("p (a m) -> p a m", a=4)
        ccoef = words(o + 4096, 2048)[0:NF].rearrange("p (a m) -> p a m", a=2)
        U = [words(o + 4096 * b, 4096).rearrange("p (t c) -> p t c", t=WT) for b in range(B)]; o += 8192
        OT = [u.rearrange("p t c -> p (t c)").rearrange("p (k t j) -> p k t j", k=KM, t=WT) for u in U]
        xp = words(o, TILES * MED).rearrange("p (t c) -> p t c", t=TILES); o += TILES * MED
        racc = small[:, 322:326]
        rmean = small[:, 326:330]
        lhs_u = small[:, 330:366].rearrange("p (t m) -> p t m", t=9)
        rsum2 = words(o, 256); o += 256
        rsums = rsum2[:, 0:192].rearrange("p (v b y) -> p v b y", v=3, b=2)

        s_w1, s_w1b, s_craw = sem("l1_weights_loaded"), sem("l1_late_weights"), sem("l1_spectra_loaded")
        s_cwe, s_cols0 = sem("l1_spectra_ready"), sem("l1_zero_columns")
        s_str = [sem(f"l1_stream_{j}") for j in range(3)]
        s_fc1, s_fc1r, s_cv, s_cvr = sem("fc1"), sem("fc1_relu"), sem("conv"), sem("conv_relu")
        s_pw1, s_pw1r, s_sq, s_xpd = sem("pw1"), sem("pw1_relu"), sem("pw1_squared"), sem("xp_ready")
        s_f1, s_f1e = sem("rows_dft"), sem("rows_dft_evacuated")
        s_uo = [sem(f"bounce_out_{b}") for b in range(B)]
        s_vi = [sem(f"bounce_in_{j}") for j in range(TILES)]
        s_sp, s_spr, s_u = sem("sp_conv"), sem("sp_relu"), sem("sp_tap_means")
        s_fc2, s_fc2c, s_rmean = sem("fc2"), sem("fc2_chunk"), sem("route_mean")
        s_rl, s_re, s_rd, s_rt = sem("route_logits"), sem("route_exp"), sem("route_done"), sem("route_moved")
        s_f2, s_f2e, s_wri = sem("spectrum"), sem("spectrum_evacuated"), sem("spectrum_weights")
        s_ya, s_yb, s_y = sem("weighted_a"), sem("weighted_b"), sem("weighted")
        s_i2, s_i2e = sem("columns_inverse"), sem("columns_inverse_evacuated")
        s_sw, s_xw, s_o1, s_o1e = sem("spatial_weight"), sem("spatially_weighted"), sem("filtered"), sem("filtered_evacuated")
        s_p2 = sem("pw2")
        ya = [words(z_base + 512 * j, 512) for j in range(2)]
        yb = [words(z_base + 1024 + 512 * j, 512) for j in range(2)]
        y_w = [words(z_base + 2048 + 512 * j, 512) for j in range(2)]
        spec = [words(z_base + 3072 + 1024 * j, 1024).rearrange("p (a c) -> p a c", a=2) for j in range(2)]

        o = L
        Zc2 = words(z_base, HALVES * COLS).rearrange("p (i q) -> p i q", q=PIX)
        rden = words(z_base + HALVES * COLS, 1024)
        qkvw = words(o, 2 * 768).rearrange("p (k c) -> p k c", k=2)
        num_s = [words(o + 512 * j, 512) for j in range(2)]; o += 1536
        pwm = words(o, 768).rearrange("p (t m) -> p t m", t=QKV_TILES); o += 768
        pwt = [words(o + sum(TENSOR_TAPS[:t]) * P, TENSOR_TAPS[t] * P).rearrange("p (a m) -> p a m", m=P)
               for t in range(QKV_TILES)]; o += sum(TENSOR_TAPS) * P
        projw = words(o, 1024).rearrange("p (k c) -> p k c", k=4); o += 1024
        head_cols = words(o, 32); o += 32
        head_rows = words(o, P); o += P
        vkm = words(o, 1024).rearrange("p (s b g m) -> p s b g m", s=2, b=B, g=2); o += 1024
        denw = words(o, 256).rearrange("p (s b g m) -> p s b g m", s=2, b=B, g=2); o += 256
        turned = [words(o + 512 * j, 512) for j in range(2)]
        proj_s = turned; o += 1024
        padq_at = o
        padq = words(o, QKV_TILES * B * QROW * QROW).rearrange("p (t b y x) -> p t b y x", t=QKV_TILES, b=B, y=QROW); o += QKV_TILES * B * QROW * QROW
        flat = [words(o + COLS * t, COLS) for t in range(QKV_TILES)]; o += QKV_TILES * COLS
        tile_pad = B * QROW * QROW
        local = [words(o, COLS), flat[0], words(o + COLS, COLS), words(o + 2 * COLS, COLS), flat[1],
                 words(padq_at, COLS)]; o += 3 * COLS
        att = [flat[2], flat[3], words(padq_at + 2 * tile_pad, COLS), words(padq_at + 3 * tile_pad, COLS)]
        kacc = small[:, 370:386].rearrange("p (s g c) -> p s g c", s=2, g=2)
        ksum = small[:, 386:394].rearrange("p (s g b) -> p s g b", s=2, g=2)
        bnv, bnsd, bn_inv, bnt, bn_off = (small[:, 394 + 6 * j:400 + 6 * j] for j in range(5))
        s_w2, s_w2b, s_bnv, s_bnsd, s_bn = sem("l2_weights_loaded"), sem("l2_late_weights"), sem("bn_var"), sem("bn_sd"), sem("bn_ready")
        s_qb, s_qkv, s_qp, s_qf = sem("qkv_border_zero"), sem("qkv"), sem("qkv_padded"), sem("qkv_flat")
        s_pwm = sem("pointwise_ready")
        s_tr, s_trc, s_vk, s_vkm = sem("kv_turned"), sem("kv_turned_copied"), sem("vk"), sem("vk_masked")
        s_den, s_rc, s_num, s_rb, s_ns, s_att = (sem("denominators"), sem("denominators_inverted"), sem("numerators"),
                                                 sem("inverse_spread"), sem("numerators_copied"), sem("attended"))
        s_dwd, s_yq, s_yqe = sem("filtered_by_dve"), sem("local_qkv"), sem("local_qkv_copied")
        s_pj, s_pje = sem("proj"), sem("proj_scaled")
        Y_ORDER = [0, 1, 2, 4, 3, 5]
        POOL_TILES = [4, 5]
        DVE_TILES = [0, 1, 2, 3]

        pool_taps = [(t, a, b) for t in POOL_TILES for a in range(TENSOR_TAPS[t], K5) for b in range(B)]
        tap_tmp = [Zc2[:, j, :] for j in range(4)]
        s_tp = sem("tap_product")
        s_ta = sem("tap_product_added")

        def tap_view(t, a, b):
            dy, dx = divmod(a, 5)
            return padq[:, t, b, dy:dy + H, dx:dx + W]

        def filter_tap(eng, step, t, a):
            for b in range(B):
                dst = local[t][:, b * PIX:(b + 1) * PIX].rearrange("p (y x) -> p y x", y=H)
                wt = col("dw2_w", t * K5 + a)
                if a == TENSOR_TAPS[t]:
                    ins = eng.tensor_scalar(dst, tap_view(t, a, b), wt, None, ALU.mult)
                else:
                    ins = eng.scalar_tensor_tensor(dst, tap_view(t, a, b), wt, dst, ALU.mult, ALU.add)
                if a == K5 - 1:
                    ins.then_inc(s_dwd, 1)
                    n = step.n
                else:
                    n = step.add(ins)
            return n

        o = L
        pw3w = words(o, 512).rearrange("p (k c) -> p k c", k=2); o += 512
        tap3 = words(o, 9 * P).rearrange("p (a m) -> p a m", a=9); o += 9 * P
        h3 = words(o, HALVES * COLS).rearrange("p (i q) -> p i q", q=PIX); o += HALVES * COLS
        o3 = words(o, HALVES * COLS).rearrange("p (i q) -> p i q", q=PIX); o += HALVES * COLS
        pk = small[:, 424:440].rearrange("p (a i) -> p a i", a=4)
        tap3_tmp = [words(o + 1024 * j, 1024) for j in range(2)]; o += 2048
        s_tp3 = sem("l3_tap_product")
        s_w3, s_d3, s_dw3, s_dw3p, s_h3 = sem("l3_weights_loaded"), sem("l3_taps_ready"), sem("l3_dw_by_dve"), sem("l3_dw_by_pool"), sem("l3_hidden")
        s_dw3t, s_kept, s_pw3, s_o3 = sem("l3_dw_by_tensor"), sem("l3_pruned"), sem("l3_pointwise"), sem("l3_result")

        def filter3(eng, step, i, tap, last):
            dy, dx = divmod(tap, 3)
            src = Z[:, i, PAD - 1 + dy:PAD - 1 + dy + H, PAD - 1 + dx:PAD - 1 + dx + W]
            dst = h3[:, i, :].rearrange("p (y x) -> p y x", y=H)
            wt = col("dw3_w", i // 2 * 9 + tap)
            if tap == 0:
                ins = eng.tensor_scalar(dst, src, wt, None, ALU.mult)
            else:
                ins = eng.scalar_tensor_tensor(dst, src, wt, dst, ALU.mult, ALU.add)
            if tap < 8:
                return step.add(ins)
            ins.then_inc(last, 1)
            return step.n

        DISP = [(i, j) for j in range(ND) for i in range(ND)]
        ORDER = [2, 1, 3, 0, 4]
        plan = []
        for hf in range(HALVES):
            for a, j in enumerate(ORDER):
                for i in range(ND):
                    plan.append((hf, j, i))
        by_pool = [n % 3 == 1 for n in range(len(plan))]
        last_of_half = [len(plan) // 2 - 1, len(plan) - 1]
        for n in last_of_half:
            by_pool[n] = True
        upto_dve = np.cumsum([not b for b in by_pool]).tolist()
        upto_pool = np.cumsum(by_pool).tolist()

        def shifted(hf, j, i):
            src = XSc[:, i:i + XX, hf * P:(hf + 1) * P] if j == 2 else XSd[:, j - (j > 2), i:i + XX, :]
            return src.rearrange("p x (g c) -> p x g c", c=CG)

        def product(eng, n):
            hf, j, i = plan[n]
            weight = Wds[hf][:, i, j, :].rearrange("p (x g) -> p x g", g=GH).unsqueeze(3).to_broadcast([P, XX, GH, CG])
            return eng.tensor_tensor(prods[n % 3].rearrange("p (x g c) -> p x g c", g=GH, c=CG),
                                     shifted(hf, j, i), weight, ALU.mult)

        def await_product_inputs(eng, n):
            hf, j, i = plan[n]
            eng.wait_ge(s_wd, hf + 1)
            if j == 2:
                eng.wait_ge(s_halo, 32)
            else:
                eng.wait_ge(s_shift[j - (j > 2)], 32 * (hf + 1))
            if n >= 3:
                eng.wait_ge(s_acc, n - 2)

        gen_x, gen_y, gen_hy, gen_w = (words(wd_at + NPT * j, NPT).rearrange("p (k g) -> p k g", k=K2) for j in range(4))
        gen_src, gen_acc = prods[0], prods[1]
        gen_tmp = gen_src[:, 0:NPT].rearrange("p (k g) -> p k g", k=K2)
        gen_dy, gen_dx = small[:, 440:441], small[:, 441:442]

        def restart(pool):
            pool.dma_reset(range(s_gen.num, s_gen.num + 1))
            pool.sem_clear(s_gen)

        def hat(me, g, out_, at, centre):
            me.link(g.tensor_scalar(out_, at, centre, None, ALU.subtract))
            me.link(g.tensor_scalar(gen_tmp, out_, 0.0, None, ALU.max))
            me.link(g.tensor_scalar(out_, out_, 0.0, None, ALU.min))
            me.link(g.tensor_tensor(out_, out_, gen_tmp, ALU.subtract))
            me.link(g.tensor_scalar(out_, out_, 1.0, 0.0, ALU.add, ALU.max))

        def general_path(pool, g, any_beyond):
            with pool.If(any_beyond > 0):
                me = Steps(pool, s_gstep)
                me.link(g.memset(gen_acc, 0.0))
                blank = xpad_dram.rearrange("b y x c -> (b y x c)").rearrange("(n p q) -> n p q", p=P, q=XX * P)
                for n in range(blank.shape[0]):
                    g.dma_start(blank[n], gen_acc).then_inc(s_gen, 16)
                    pool.wait_ge(s_gen, 16 * (n + 1))
                for b in range(B):
                    for s_ in range(2):
                        rows = XSc[b * 64 + s_:(b + 1) * 64:2, PAD:PAD + XX, :]
                        g.dma_start(xpad_dram[b, REACH:REACH + H, REACH + XX * s_:REACH + XX * (s_ + 1), :], rows).then_inc(s_gen, 16)
                        pool.wait_ge(s_gen, 16 * (blank.shape[0] + 1 + 2 * b + s_))
                restart(pool)
                pool.sem_clear(s_gstep)
                offs = OM[:, :, 0:2 * G * K2].rearrange("p x (h g k a) -> p h a k x g", h=2, g=GH, k=K2)
                for hf in range(HALVES):
                    me = Steps(pool, s_gstep)
                    for k in range(K2):
                        for a_, dst in ((0, gen_x), (1, gen_y)):
                            shift = float((k // 3, k % 3)[a_] - 1)
                            me.add(g.tensor_scalar(dst[:, k].rearrange("p (x g) -> p x g", g=GH), offs[:, hf, a_, k], shift, None, ALU.add))
                    me.add(g.memset(gen_acc, 0.0))
                    me.link(g.memset(gen_dy, -float(REACH)))
                    pool.sem_clear(s_gstep)
                    with pool.Fori(0, 2 * REACH) as i:
                        me = Steps(pool, s_gstep)
                        hat(me, g, gen_hy, gen_y, gen_dy)
                        me.link(g.tensor_tensor(gen_hy, gen_hy, mask[:, hf], ALU.mult))
                        me.add(g.tensor_scalar(gen_dy, gen_dy, 1.0, None, ALU.add))
                        me.link(g.memset(gen_dx, -float(REACH)))
                        pool.sem_clear(s_gstep)
                        with pool.Fori(0, 2 * REACH) as j:
                            me = Steps(pool, s_gstep)
                            hat(me, g, gen_w, gen_x, gen_dx)
                            me.link(g.tensor_tensor(gen_w, gen_w, gen_hy, ALU.mult))
                            me.add(g.tensor_scalar(gen_dx, gen_dx, 1.0, None, ALU.add))
                            for k in range(1, K2):
                                me.link(g.tensor_tensor(gen_w[:, 0], gen_w[:, 0], gen_w[:, k], ALU.add))
                            for b in range(B):
                                for s_ in range(2):
                                    src = xpad_dram[b, bass.ds(i, H), bass.ds(j + XX * s_, XX), hf * P:(hf + 1) * P]
                                    dst = gen_src.rearrange("p (x c) -> p x c", c=P)[b * 64 + s_:(b + 1) * 64:2]
                                    g.dma_start(dst, src).then_inc(s_gen, 16)
                                    pool.wait_ge(s_gen, 16 * (2 * b + s_ + 1))
                            weight = gen_w[:, 0].rearrange("p (x g) -> p x g", g=GH).unsqueeze(3).to_broadcast([P, XX, GH, CG])
                            term = gen_src.rearrange("p (x g c) -> p x g c", g=GH, c=CG)
                            me.link(g.tensor_tensor(term, term, weight, ALU.mult))
                            me.link(g.tensor_tensor(gen_acc, gen_acc, gen_src, ALU.add))
                            restart(pool)
                            pool.sem_clear(s_gstep)
                    g.dma_start(general_dram[hf], gen_acc).then_inc(s_gen, 16)
                    pool.wait_ge(s_gen, 16)
                    restart(pool)

        def add_general(pool, g, any_beyond, n):
            with pool.If(any_beyond > 0):
                g.dma_start(prods[n % 3], general_dram[plan[n][0]], accum_op=ALU.add).then_inc(s_gen, 16)
                pool.wait_ge(s_gen, 16)
                restart(pool)

        block = ctx.enter_context(nc.Block())

        @block.sync
        def _(sp):
            for i in range(4):
                h, b = divmod(i, 2)
                sp.dma_start(X[:, h, b, :], x_in[b, h * P:(h + 1) * P]).then_inc(s_x, 16)
            sp.dma_start(cv, w["chan_vecs"]).then_inc(s_const, 16)
            sp.dma_start(ident, w["ident"]).then_inc(s_const, 16)
            sp.dma_start(gmean, w["gmean"]).then_inc(s_const, 16)
            sp.dma_start(head_mask, w["head_mask"]).then_inc(s_const, 16)
            sp.dma_start(small[:, 96:103], w["small_consts"]).then_inc(s_const, 16)
            sp.dma_start(inw, w["in_w"].rearrange("(k p) c -> p k c", p=P)).then_inc(s_w0, 16)
            sp.dma_start(inb, w["in_b"].partition_broadcast(P)).then_inc(s_w0, 16)
            sp.dma_start(omw[:, :, 0:2 * G * K2], w["off_w"].rearrange("(k p) c -> p k c", p=P)).then_inc(s_w0, 16)
            sp.dma_start(omw[:, :, 2 * G * K2:], w["mask_w"].rearrange("(k p) c -> p k c", p=P)).then_inc(s_w0, 16)
            sp.dma_start(omb[:, 0:2 * G * K2], w["off_b"].partition_broadcast(P)).then_inc(s_w0, 16)
            sp.dma_start(omb[:, 2 * G * K2:], w["mask_b"].partition_broadcast(P)).then_inc(s_w0, 16)
            sp.dma_start(outw, w["out_w"].rearrange("(k p) c -> p k c", p=P)).then_inc(s_w0, 16)
            sp.wait_ge(s_xpe, 8)
            sp.wait_ge(s_shz, 2)
            sp.dma_start(XSc[1::2, 0:PAD], XSc[0::2, XX:XX + PAD]).then_inc(s_halo, 16)
            sp.dma_start(XSc[0::2, PAD + XX:], XSc[1::2, PAD:2 * PAD]).then_inc(s_halo, 16)
            sp.wait_ge(s_halo, 32)
            for hf in range(HALVES):
                for a, j in enumerate(ORDER[1:]):
                    if hf:
                        sp.wait_ge(s_acc, ND * (a + 2))
                    d = 2 * (j - 2)
                    for b in range(B):
                        lo, hi = b * 64 + max(0, -d), b * 64 + 64 - max(0, d)
                        sp.dma_start(XSd[lo:hi, j - (j > 2)], XSc[lo + d:hi + d, :, hf * P:(hf + 1) * P]).then_inc(s_shift[j - (j > 2)], 16)
            sp.wait_ge(s_x_new, 8)
            for dst, name in ((fc1w, "fc1_w"), (pw1w, "pw1_w")):
                sp.dma_start(dst, w[name].rearrange("(k p) c -> p k c", p=P)).then_inc(s_w1, 16)
            sp.dma_start(convw, w["conv_w"]).then_inc(s_w1, 16)
            sp.dma_start(dft, w["dft"]).then_inc(s_w1, 16)
            sp.dma_start(craw, w["spectra"]).then_inc(s_craw, 16)
            sp.dma_start(ccoef, w["spectra_coef"]).then_inc(s_craw, 16)
            sp.dma_start(sp1w, w["sp1_w"].rearrange("(k p) t c -> p k t c", p=P)).then_inc(s_w1b, 16)
            sp.dma_start(spw, w["spatial_w"]).then_inc(s_w1b, 16)
            sp.dma_start(pw2w, w["pw2_w"].rearrange("(k p) c -> p k c", p=P)).then_inc(s_w1b, 16)
            for c in range(3):
                sp.dma_start(stream[c], w["fc2_w"][c]).then_inc(s_str[c], 16)
            for b in range(B):
                for t in range(WT):
                    sp.wait_ge(s_f1e, WT * b + t + 1)
                    sp.dma_start(w["bounce"][0, b, :, t, :], U[b][:, t, :]).then_inc(s_uo[b], 16)
            for b in range(B):
                sp.wait_ge(s_uo[b], 16 * WT)
                if b == 0:
                    sp.wait_ge(s_pw1, TILES)
                for t in range(WT):
                    rows = w["bounce"][0, b].rearrange("s w c -> (s w) c")[t * P:(t + 1) * P, :]
                    sp.dma_start(V[b][:, t, :], rows).then_inc(s_vi[WT * b + t], 16)
            for c in range(3, 11):
                sp.wait_ge(s_fc2c, c - 2)
                dst, src = (stream[c % 3], w["fc2_w"][c]) if c < 10 else (stream[1][0:4, :], w["fc2_b"])
                sp.dma_start(dst, src).then_inc(s_str[c % 3], 16)
            sp.wait_ge(s_rd, 1)
            for r_ in range(4):
                sp.dma_start(route[:, r_, :], route_sm[r_:r_ + 1, :]).then_inc(s_rt, 16)
            for b in range(B):
                for t in range(WT):
                    sp.wait_ge(s_i2e, WT * b + t + 1)
                    rows = w["bounce"][1, b].rearrange("s w c -> (s w) c")[t * P:(t + 1) * P, :]
                    sp.dma_start(rows, U[b][:, t, :]).then_inc(s_uo[b], 16)
                sp.wait_ge(s_uo[b], 32 * WT)
                for t in range(WT):
                    sp.dma_start(V[b][:, t, :], w["bounce"][1, b, :, t, :]).then_inc(s_vi[WT * b + t], 16)
            if LAST >= 2:
                sp.wait_ge(s_x_new, 16)
                sp.dma_start(qkvw, w["qkv_w"].rearrange("(k p) c -> p k c", p=P)).then_inc(s_w2, 16)
                sp.dma_start(pwm.rearrange("p t m -> p (t m)"), w["pointwise_w"]).then_inc(s_w2b, 16)
                sp.dma_start(projw, w["proj_w"].rearrange("(k p) c -> p k c", p=P)).then_inc(s_w2b, 16)
                sp.dma_start(head_cols, w["head_cols"]).then_inc(s_w2b, 16)
                sp.dma_start(head_rows, w["head_rows"]).then_inc(s_w2b, 16)
            if LAST >= 3:
                sp.wait_ge(s_x_new, 24)
                sp.dma_start(pw3w, w["pw3_w"].rearrange("(k p) c -> p k c", p=P)).then_inc(s_w3, 16)
            for n, i in enumerate((0, 2, 1, 3)):
                h, b = divmod(i, 2)
                sp.wait_ge(s_x_new, 8 * (LAST + 1) if LAST < 3 else 24 + n + 1)
                sp.dma_start(out[b, h * P:(h + 1) * P], X[:, h, b, :]).then_inc(s_out, 16)
            sp.wait_ge(s_out, 64)

        @block.tensor
        def _(pe):
            def group_means(layer):
                pe.wait_ge(s_gn_stats, layer + 1)
                pe.matmul(psum[:, 7, 0:8], gmean, small[:, 56:64], start=True, stop=True).then_inc(s_gn_means, 1)

            pe.wait_ge(s_const, 80)
            group_means(0)
            pe.wait_ge(s_zc, 4)
            pe.wait_ge(s_w0, 112)
            for n in range(8):
                for u in range(2):
                    for k in range(HALVES):
                        lhs = Zc[:, 2 * k:2 * k + 2, :].rearrange("p b q -> p (b q)")[:, 2 * n + u::XX]
                        m = pe.matmul(psum[:, n, u * C:(u + 1) * C], lhs, inw[:, k], start=(k == 0 and u == 0),
                                      stop=(k == 1), skip_group_check=True)
                m.then_inc(s_xp, 1)
            for t in range(8):
                if t == 0:
                    pe.wait_ge(s_x1, 4)
                    pe.wait_ge(s_xpe, 8)
                for u in range(2):
                    for k in range(HALVES):
                        m = pe.transpose(psum[:, t, u * C + k * P:u * C + (k + 1) * P],
                                         x1cm[:, k, 2 * t + u::XX], ident)
                m.then_inc(s_x1t, 1)
            for t in range(8):
                q, k = divmod(t, 2)
                pe.wait_ge(s_x1n, 4 * (q + 1))
                for u in range(4):
                    m = pe.transpose(psum[:, t, u * P:(u + 1) * P], x1n[:, 4 * q + u, k * P:(k + 1) * P], ident)
                m.then_inc(s_back, 1)
            for t in range(XX):
                pe.wait_ge(s_g1, max(2 * (t // 4 + 1), t % 8 + 1))
                if t >= 8:
                    pe.wait_ge(s_ome, t - 7)
                for k in range(HALVES):
                    m = pe.matmul(psum[:, t % 8, 0:NOM], g1cm[:, k, t, :], omw[:, k], start=(k == 0), stop=(k == 1))
                m.then_inc(s_om, 1)
            for n, (hf, j, i) in enumerate(plan):
                first, last = n % (ND * ND) == 0, n % (ND * ND) == ND * ND - 1
                if by_pool[n]:
                    pe.wait_ge(s_pp, upto_pool[n])
                else:
                    pe.wait_ge(s_pd, upto_dve[n])
                for xx in range(XX):
                    m = pe.matmul(psum[:, 4 * hf + xx // 4, xx % 4 * P:(xx % 4 + 1) * P], prods[n % 3][:, xx * P:(xx + 1) * P],
                                  ident, start=(first and xx % 4 == 0), stop=last, is_transpose=True, skip_group_check=True)
                m.then_inc(s_acc, 1)
            pe.wait_ge(s_outT, 8)
            for t in range(8):
                q, mh = divmod(t, 2)
                for k in range(HALVES):
                    m = pe.matmul(psum[:, t, :], outw[:, k, mh * P:(mh + 1) * P],
                                  outT[:, k, 4 * q:4 * q + 4, :], start=(k == 0), stop=(k == 1))
                m.then_inc(s_op, 1)

            if LAST < 1:
                return
            group_means(1)
            pe.wait_ge(s_zc, 8)
            pe.wait_ge(s_w1, 64)
            z2 = Zc1.rearrange("p (k b) q -> p k (b q)", k=2)
            for c in range(CHUNKS):
                for k in range(HALVES):
                    m = pe.matmul(psum[:, c, :], fc1w[:, k], z2[:, k, c * BANK:(c + 1) * BANK], start=(k == 0), stop=(k == 1))
                m.then_inc(s_fc1, 1)
            for c in range(CHUNKS):
                pe.wait_ge(s_fc1r, c + 1)
                pe.matmul(psum[:, 4 + c, :], convw, sr_act[:, c * BANK:(c + 1) * BANK], start=True, stop=True).then_inc(s_cv, 1)
            for i in range(TILES + 3):
                if i < TILES:
                    if i < 4:
                        pe.wait_ge(s_fc1r, i + 1)
                    else:
                        pe.wait_ge(s_pw1r, i - 3)
                    b, t = divmod(i, WT)
                    for k in range(HALVES):
                        m = pe.matmul(psum[:, i % 4, :], Zc1[:, 2 * k + b, t::WT], pw1w[:, k], start=(k == 0), stop=(k == 1))
                    m.then_inc(s_pw1, 1)
                if i >= 3:
                    n = i - 3
                    pe.wait_ge(s_xpd, n + 1)
                    if n < 4:
                        pe.wait_ge(s_cvr, 4)
                    else:
                        pe.wait_ge(s_f1e, n - 3)
                    pe.matmul(psum[:, 4 + n % 4, :], dft[:, 0], xp[:, n, :], start=True, stop=True).then_inc(s_f1, 1)
            pe.wait_ge(s_z, 8)
            pe.wait_ge(s_zb, 2)
            pe.wait_ge(s_w1b, 48)
            pe.wait_ge(s_pw1r, TILES)
            for c in range(CHUNKS):
                b, yh = divmod(c, 2)
                for k in range(HALVES):
                    for tap in range(9):
                        dy, dx = divmod(tap, 3)
                        y0 = PAD - 1 + dy + 16 * yh
                        m = pe.matmul(psum[:, c, :], sp1w[:, k, tap], Z[:, 2 * k + b, y0:y0 + 16, PAD - 1 + dx:PAD - 1 + dx + W],
                                      start=(k == 0 and tap == 0), stop=(k == 1 and tap == 8))
                m.then_inc(s_sp, 1)
            for c in range(10):
                pe.wait_ge(s_str[c % 3], 16 * (c // 3 + 1))
                if c == 0:
                    pe.wait_ge(s_rmean, 1)
                    pe.wait_ge(s_f1e, TILES)
                if c == 1:
                    pe.wait_ge(s_u, 1)
                for f in range(4):
                    m = pe.matmul(psum[0:4, 4 + f, :], rmean if c == 0 else lhs_u[:, c - 1, :],
                                  stream[c % 3][:, f * BANK:(f + 1) * BANK], start=(c == 0), stop=(c == 9))
                m.then_inc(s_fc2c, 1)
            for i in range(TILES + 1):
                if i < TILES:
                    b, t = divmod(i, WT)
                    sel = 1 if t == 0 else 2
                    pe.wait_ge(s_vi[i], 16)
                    if i == 0:
                        pe.wait_ge(s_spr, 4)
                    if i >= 2:
                        pe.wait_ge(s_f2e, i - 1)
                    pe.matmul(psum[:, 2 * (i % 2), :], dft[:, sel], V[b][:, t, :], start=True, stop=True)
                    pe.matmul(psum[:, 2 * (i % 2) + 1, :], dft[:, sel + 2], V[b][:, t, :], start=True, stop=True).then_inc(s_f2, 1)
                    if i == 0:
                        pe.wait_ge(s_rt, 64)
                        pe.wait_ge(s_cwe, 1)
                    else:
                        pe.wait_ge(s_ya, i)
                        pe.wait_ge(s_yb, i)
                    pe.matmul(psum[:, 4, :], cwe[:, 0, t * P:(t + 1) * P], route[:, b, :], start=True, stop=True)
                    pe.matmul(psum[:, 5, :], cwe[:, 1, t * P:(t + 1) * P], route[:, b, :], start=True, stop=True).then_inc(s_wri, 1)
                if i >= 1:
                    n = i - 1
                    pe.wait_ge(s_y, n + 1)
                    if n >= 2:
                        pe.wait_ge(s_i2e, n - 1)
                    pe.matmul(psum[:, 6 + n % 2, :], dft[:, 5 if n % WT == 0 else 6], y_w[n % 2], start=True, stop=True).then_inc(s_i2, 1)
            for i in range(TILES + 1):
                if i < TILES:
                    b, t = divmod(i, WT)
                    if i == 0:
                        pe.wait_ge(s_f2e, TILES)
                    if i >= 2:
                        pe.wait_ge(s_xw, i - 1)
                    pe.matmul(psum[:, i % 2, :], spw[:, t * P:(t + 1) * P], route[:, 2 + b, :], start=True, stop=True).then_inc(s_sw, 1)
                if i >= 1:
                    n = i - 1
                    b, t = divmod(n, WT)
                    pe.wait_ge(s_vi[n], 32)
                    pe.wait_ge(s_xw, n + 1)
                    if n < 2:
                        pe.wait_ge(s_yb, TILES)
                    else:
                        pe.wait_ge(s_o1e, n - 1)
                    for k in range(KM):
                        pe.matmul(psum[:, 2 + n % 2, k * P:(k + 1) * P], V[b][:, t, k * P:(k + 1) * P], dft[:, 7],
                                  start=(k == 0), stop=False, skip_group_check=True)
                    for k in range(KM):
                        m = pe.matmul(psum[:, 2 + n % 2, k * P:(k + 1) * P], xp[:, n, k * P:(k + 1) * P], ident,
                                      start=False, stop=True, is_transpose=True, skip_group_check=True)
                    m.then_inc(s_o1, 1)
                    if n % 4 == 3:
                        pe.wait_ge(s_o1e, n + 1)
                        pe.wait_ge(s_i2e, TILES)
                        for mh in range(HALVES):
                            j = n // 4 * 2 + mh
                            if j >= 4:
                                pe.wait_ge(s_x_new, 8 + j - 3)
                            for k in range(KM):
                                m = pe.matmul(psum[:, 4 + j % 4, :], pw2w[:, k, mh * P:(mh + 1) * P],
                                              OT[b][:, k, t - 3:t + 1, :], start=(k == 0), stop=(k == KM - 1))
                            m.then_inc(s_p2, 1)

            if LAST < 2:
                return
            group_means(2)
            pe.wait_ge(s_zc, 12)
            pe.wait_ge(s_w2, 16)
            z2 = Zc2.rearrange("p (k b) q -> p k (b q)", k=2)
            for i in range(QKV_TILES * CHUNKS):
                t, c = divmod(i, CHUNKS)
                if i >= 4:
                    pe.wait_ge(s_qp, i - 3)
                    pe.wait_ge(s_qf, i - 3)
                for k in range(HALVES):
                    m = pe.matmul(psum[:, i % 4, :], qkvw[:, k, t * P:(t + 1) * P], z2[:, k, c * BANK:(c + 1) * BANK],
                                  start=(k == 0), stop=(k == 1))
                m.then_inc(s_qkv, 1)

            def key_value_products(src, tiles):
                for i in range(TILES + 1):
                    if i < TILES:
                        b, t = divmod(i, WT)
                        n = src * TILES + i
                        if n >= 2:
                            pe.wait_ge(s_trc, n - 1)
                        for u in range(4):
                            m = pe.transpose(psum[:, 4 + n % 2, u * P:(u + 1) * P], tiles[u][:, i * P:(i + 1) * P], ident)
                        m.then_inc(s_tr, 1)
                    if i >= 1:
                        b, t = divmod(i - 1, WT)
                        n = src * TILES + i - 1
                        pe.wait_ge(s_trc, n + 1)
                        if src and t == 0:
                            pe.wait_ge(s_vkm, 2)
                        for gr in range(2):
                            tk, tv = 2 * gr, 2 * gr + 1
                            m = pe.matmul(psum[:, 6 + b, gr * P:(gr + 1) * P], turned[n % 2][:, tk * P:(tk + 1) * P],
                                          turned[n % 2][:, tv * P:(tv + 1) * P], start=(t == 0 and gr == 0), stop=(t == WT - 1),
                                          skip_group_check=True)
                        m.then_inc(s_vk, 1)

            def attend(src, queries):
                pe.wait_ge(s_vkm, 2 * src + 2)
                for c in range(2):
                    for b in range(B):
                        for gr in range(2):
                            j = 2 * gr + b
                            m = pe.matmul(psum[32 * j:32 * j + 32, c, :], denw[:, src, b, gr, :],
                                          queries[gr][:, b * PIX + c * BANK:b * PIX + (c + 1) * BANK], start=True, stop=True)
                    m.then_inc(s_den, 1)
                for s_ in range(8):
                    b, gr, c = s_ // 4, s_ // 2 % 2, s_ % 2
                    n, j = 8 * src + s_, 2 * gr + b
                    if n >= 2:
                        pe.wait_ge(s_ns, n - 1)
                    pe.matmul(psum[:, 2 + n % 2, :], vkm[:, src, b, gr, :], queries[gr][:, b * PIX + c * BANK:b * PIX + (c + 1) * BANK],
                              start=True, stop=True).then_inc(s_num, 1)
                    if s_ == 0:
                        pe.wait_ge(s_rc, src + 1)
                    if n >= 2:
                        pe.wait_ge(s_att, n - 1)
                    pe.matmul(psum[:, 4 + n % 2, :], head_rows[32 * j:32 * j + 32, :],
                              rden[32 * j:32 * j + 32, c * BANK:(c + 1) * BANK], start=True, stop=True).then_inc(s_rb, 1)

            def local_qkv(a):
                t = Y_ORDER[a]
                if t in POOL_TILES:
                    pe.wait_ge(s_ta, len([p for p in pool_taps if p[0] <= t]))
                else:
                    pe.wait_ge(s_dwd, 2 * (DVE_TILES.index(t) + 1))
                for c in range(CHUNKS):
                    if a:
                        pe.wait_ge(s_yqe, 4 * a + c - 3)
                    else:
                        pe.wait_ge(s_pwm, 1)
                    b, yh = divmod(c, 2)
                    for tap in range(TENSOR_TAPS[t]):
                        dy, dx = divmod(tap, 5)
                        pe.matmul(psum[:, c, :], pwt[t][:, tap, :], padq[:, t, b, dy + 16 * yh:dy + 16 * yh + 16, dx:dx + W],
                                  start=(tap == 0), stop=False)
                    pe.matmul(psum[:, c, :], pwm[:, t, :], local[t][:, c * BANK:(c + 1) * BANK], start=False, stop=True).then_inc(s_yq, 1)

            pe.wait_ge(s_qf, 24)
            pe.wait_ge(s_qp, 24)
            key_value_products(0, flat[0:4])
            pe.wait_ge(s_w2b, 64)
            local_qkv(0)
            pe.wait_ge(s_yqe, 4)
            attend(0, flat[4:6])
            pe.wait_ge(s_ns, 8)
            for a in range(1, 5):
                local_qkv(a)
            pe.wait_ge(s_att, 8)
            pe.wait_ge(s_yqe, 20)
            key_value_products(1, local[0:4])
            local_qkv(5)
            pe.wait_ge(s_yqe, 24)
            attend(1, local[4:6])
            pe.wait_ge(s_ns, 16)
            pe.wait_ge(s_att, 16)
            for i in range(8):
                c, mh = divmod(i, 2)
                if i >= 4:
                    pe.wait_ge(s_pje, i - 3)
                for k in range(4):
                    m = pe.matmul(psum[:, i % 4, :], projw[:, k, mh * P:(mh + 1) * P], att[k][:, c * BANK:(c + 1) * BANK],
                                  start=(k == 0), stop=(k == 3))
                m.then_inc(s_pj, 1)
            if LAST < 3:
                return
            group_means(3)
            pe.wait_ge(s_z, 16 - 4)
            pe.wait_ge(s_zb, 3)
            pe.wait_ge(s_d3, 1)
            for c in range(2):
                for tap in range(9):
                    dy, dx = divmod(tap, 3)
                    y0 = PAD - 1 + dy + 16 * c
                    m = pe.matmul(psum[:, c, :], tap3[:, tap, :], Z[:, 3, y0:y0 + 16, PAD - 1 + dx:PAD - 1 + dx + W],
                                  start=(tap == 0), stop=(tap == 8))
            m.then_inc(s_dw3t, 1)
            pe.wait_ge(s_w3, 16)
            for b in range(B):
                pe.wait_ge(s_kept, 2 * (b + 1))
                for mh in range(HALVES):
                    for c in range(2):
                        for k in range(HALVES):
                            m = pe.matmul(psum[:, (2 + 4 * b + 2 * mh + c) % 8, :], pw3w[:, k, mh * P:(mh + 1) * P],
                                          h3[:, 2 * k + b, c * BANK:(c + 1) * BANK], start=(k == 0), stop=(k == 1))
                    m.then_inc(s_pw3, 1)

        @block.vector
        def _(dve):
            v = nc.vector
            me = Steps(dve, s_dve)

            def group_norm(layer):
                for i in range(4):
                    for c in range(2):
                        n = me.add(v.bn_stats(st[:, i, c, :], X.rearrange("p h b q -> p (h b) q")[:, i, c * BANK:(c + 1) * BANK]))
                me.upto(n)
                for i in range(4):
                    n = me.add(v.bn_aggr(mv[:, i, :], st[:, i, :, :]))
                me.upto(n)
                me.link(v.tensor_tensor(gq[:, 1, :], mv[:, :, 0], mv[:, :, 0], ALU.mult))
                me.link(v.tensor_tensor(gq[:, 1, :], gq[:, 1, :], mv[:, :, 1], ALU.add))
                v.tensor_copy(gq[:, 0, :], mv[:, :, 0]).then_inc(s_gn_stats, 1)
                dve.wait_ge(s_gn_means, layer + 1)
                me.link(v.tensor_copy(small[:, 64:72], psum[:, 7, 0:8]))
                me.link(v.tensor_tensor(gt, gm[:, 0, :], gm[:, 0, :], ALU.mult))
                me.link(v.tensor_tensor(gvar, gm[:, 1, :], gt, ALU.subtract))
                v.tensor_scalar(gvar, gvar, GN_EPS, None, ALU.add).then_inc(s_gn_var, 1)
                dve.wait_ge(s_gn_sd, layer + 1)
                me.link(v.reciprocal(grs, gsd))
                newton(grs, gvar, gt)
                me.link(v.tensor_tensor(gnb, gm[:, 0, :], grs, ALU.mult))
                v.tensor_scalar(gnb, gnb, -1.0, None, ALU.mult).then_inc(s_gn_coef, 1)
                dve.wait_ge(s_gn_coef, layer + 1)
                if layer == 2:
                    return
                for i in range(4):
                    v.tensor_scalar(z_inner(i), Xi[:, i], grs[:, i:i + 1], gnb[:, i:i + 1], ALU.mult, ALU.add).then_inc(s_z, 1)

            def newton(r, var, t):
                me.link(v.tensor_tensor(t, r, r, ALU.mult))
                me.link(v.tensor_tensor(t, t, var, ALU.mult))
                me.link(v.tensor_scalar(t, t, -0.5, 1.5, ALU.mult, ALU.add))
                me.link(v.tensor_tensor(r, r, t, ALU.mult))

            dve.wait_ge(s_x, 64)
            dve.wait_ge(s_const, 80)
            group_norm(0)
            v.tensor_scalar(bnv, col("bn_v", 0, 6), GN_EPS, None, ALU.add).then_inc(s_bnv, 1)
            dve.wait_ge(s_z, 4)
            dve.wait_ge(s_zb, 1)
            dve.wait_ge(s_w0, 112)
            dve.wait_ge(s_bnsd, 1)
            me.link(v.reciprocal(bn_inv, bnsd))
            newton(bn_inv, bnv, bnt)
            me.link(v.tensor_tensor(bn_inv, bn_inv, col("bn_g", 0, 6), ALU.mult))
            me.link(v.tensor_tensor(bn_off, col("bn_m", 0, 6), bn_inv, ALU.mult))
            me.link(v.tensor_tensor(bn_off, col("bn_b", 0, 6), bn_off, ALU.subtract))
            me.link(v.tensor_tensor(bnt[:, 0:4], col("l3_b", 0, 4), bn_inv[:, 2:6], ALU.mult))
            v.tensor_tensor(bn_off[:, 2:6], bn_off[:, 2:6], bnt[:, 0:4], ALU.add).then_inc(s_bn, 1)

            def depthwise3(k, acc, tap, wname, bname, last):
                dy, dx = divmod(tap, 3)
                for b in range(B):
                    src = Z[:, 2 * k + b, PAD - 1 + dy:PAD - 1 + dy + H, PAD - 1 + dx:PAD - 1 + dx + W]
                    dst = acc[:, k, b * PIX:(b + 1) * PIX].rearrange("p (y x) -> p y x", y=H)
                    wt = col(wname, k * 9 + tap)
                    if tap == 0:
                        ins = v.tensor_scalar(dst, src, wt, col(bname, k), ALU.mult, ALU.add)
                    else:
                        ins = v.scalar_tensor_tensor(dst, src, wt, dst, ALU.mult, ALU.add)
                    if tap < 8:
                        n = me.add(ins)
                    else:
                        ins.then_inc(last, 1)
                        n = me.n
                return n

            def evacuate_xproj(n):
                dve.wait_ge(s_xp, n + 1)
                v.tensor_tensor(XSc[:, PAD + 2 * n:PAD + 2 * n + 2, :], psum[:, n, :].rearrange("p (x c) -> p x c", c=C),
                                inb.unsqueeze(1).to_broadcast([P, 2, C]), ALU.add).then_inc(s_xpe, 1)

            tap_done = [0, 0]
            for tap in range(9):
                for k in range(HALVES):
                    if tap:
                        me.upto(tap_done[k])
                    tap_done[k] = depthwise3(k, x1cm, tap, "dw0_w", "dw0_b", s_x1)
                if 1 <= tap:
                    evacuate_xproj(tap - 1)
            tiles = psum[:].rearrange("p t (u c) -> p (t u) c", c=C)
            for t in range(XX):
                dve.wait_ge(s_x1t, t // 2 + 1)
                n = me.add(v.bn_stats(ln_st[:, t, :], tiles[:, t, :]))
            me.upto(n)
            for t in range(XX):
                n = me.add(v.bn_aggr(ln_mv[:, t, :], ln_st[:, t, :]))
            me.upto(n)
            v.tensor_scalar(ln_var, ln_mv[:, :, 1], GN_EPS, None, ALU.add).then_inc(s_lnv, 1)
            dve.wait_ge(s_lnsd, 1)
            me.link(v.reciprocal(ln_rs, ln_sd))
            newton(ln_rs, ln_var, ln_t)
            me.link(v.tensor_tensor(ln_nb, ln_mv[:, :, 0], ln_rs, ALU.mult))
            me.link(v.tensor_scalar(ln_nb, ln_nb, -1.0, None, ALU.mult))
            for t in range(XX):
                v.tensor_scalar(x1n[:, t, :], tiles[:, t, :], ln_rs[:, t:t + 1], ln_nb[:, t:t + 1],
                                ALU.mult, ALU.add).then_inc(s_x1n, 1)
            for t in range(XX):
                dve.wait_ge(s_om, t + 1)
                v.tensor_tensor(OM[:, t, :], psum[:, t % 8, 0:NOM], omb, ALU.add).then_inc(s_ome, 1)
            dve.wait_ge(s_ome, XX)
            v.tensor_reduce(amax, OM[:, :, 0:2 * G * K2], AX.XY, ALU.max, apply_absolute_value=True).then_inc(s_amax, 1)
            logits = OM[:, :, 2 * G * K2:].rearrange("p x (h g k) -> p h x g k", h=2, k=K2)
            for hf in range(2):
                n = me.add(v.tensor_reduce(sm_t[:, hf].rearrange("p (x g) -> p x g", g=GH), logits[:, hf], AX.X, ALU.max))
            me.upto(n)
            for hf in range(2):
                v.tensor_tensor(mask[:, hf].rearrange("p k (x g) -> p k x g", g=GH), logits[:, hf].rearrange("p x g k -> p k x g"),
                                sm_t[:, hf].rearrange("p (x g) -> p x g", g=GH).unsqueeze(1).to_broadcast([P, K2, XX, GH]),
                                ALU.subtract).then_inc(s_lgs, 1)
            for hf in range(2):
                dve.wait_ge(s_exp, hf + 1)
                me.link(v.tensor_reduce(sm_r[:, hf], mask[:, hf].rearrange("p k g -> p g k"), AX.X, ALU.add))
                me.link(v.reciprocal(sm_t[:, hf], sm_r[:, hf]))
                v.tensor_tensor(mask[:, hf], mask[:, hf], sm_t[:, hf].unsqueeze(1).to_broadcast([P, K2, XG]), ALU.mult).then_inc(s_mask, 1)
            dve.wait_ge(s_mask, 2)

            def displacement_weights(hf):
                dve.wait_ge(s_abs, 6 * (hf + 1))
                allh = hats.rearrange("p a k g -> p (a k g)")
                me.link(v.tensor_scalar(allh, allh, 1.0, 1.0, ALU.min, ALU.subtract))
                if hf == 0:
                    dve.wait_ge(s_general, 1)
                for ky in range(3):
                    n = me.add(v.scalar_tensor_tensor(hats[:, 3 + ky], hats[:, 3 + ky], within, mask[:, hf], ALU.mult, ALU.mult))
                n = me.add(v.memset(Wds[hf], 0.0))
                me.upto(n)
                for ky in range(3):
                    for kx in range(3):
                        me.link(v.tensor_tensor(wk, hats[:, 3 + ky].rearrange("p k g -> p (k g)"),
                                                hats[:, kx].rearrange("p k g -> p (k g)"), ALU.mult))
                        window = Wds[hf][:, kx:kx + 3, ky:ky + 3, :]
                        ins = v.tensor_tensor(window, window, wk.rearrange("p (i j g) -> p i j g", i=3, j=3), ALU.add)
                        if ky == 2 and kx == 2:
                            ins.then_inc(s_wd, 1)
                        else:
                            me.link(ins)

            displacement_weights(0)
            for n in range(len(plan)):
                if n == 12:
                    displacement_weights(1)
                if not by_pool[n]:
                    await_product_inputs(dve, n)
                    product(v, n).then_inc(s_pd, 1)
            for t in range(8):
                q, mh = divmod(t, 2)
                dve.wait_ge(s_op, t + 1)
                xv = X[:, mh].rearrange("p b (r x) -> p x (b r)", x=XX)[:, 4 * q:4 * q + 4, :]
                v.scalar_tensor_tensor(xv, psum[:, t, :].rearrange("p (x r) -> p x r", x=4), col("out_b", mh), xv,
                                       ALU.add, ALU.add).then_inc(s_x_new, 1)

            if LAST < 1:
                return
            dve.wait_ge(s_x_new, 8)
            group_norm(1)
            for i in range(TILES):
                dve.wait_ge(s_pw1r, i + 1)
                v.tensor_tensor(xp[:, i, :], xp[:, i, :], xp[:, i, :], ALU.mult).then_inc(s_sq, 1)
                if i == 3:
                    dve.wait_ge(s_cvr, 4)
                    me.link(v.tensor_tensor(rmean[:, 0:2], racc[:, 0:4:2], racc[:, 1:4:2], ALU.add))
                    n = me.add(v.tensor_scalar(rmean[:, 0:2], rmean[:, 0:2], 1.0 / PIX, None, ALU.mult))
                    v.memset(rmean[:, 2:4], 0.0).then_inc(s_rmean, 1)
                    me.link(v.memset(small[:, 330:366], 0.0))
            dve.wait_ge(s_spr, 4)
            hidden = sr_act.rearrange("p (b y x) -> p b y x", b=B, y=H)
            span = [(0, 31), (0, 32), (1, 32)]
            for dx, (lo, hi) in enumerate(span):
                n = me.add(v.tensor_reduce(rsums[:, dx], hidden[:, :, :, lo:hi], AX.X, ALU.add))
            me.upto(n)
            for dy, (lo, hi) in enumerate(span):
                n = me.add(v.tensor_reduce(lhs_u[:, 3 * dy:3 * dy + 3, 2:4], rsums[:, :, :, lo:hi], AX.X, ALU.add))
            me.upto(n)
            v.tensor_scalar(lhs_u[:, :, 2:4], lhs_u[:, :, 2:4], 1.0 / PIX, None, ALU.mult).then_inc(s_u, 1)
            dve.wait_ge(s_fc2c, 10)
            dve.wait_ge(s_str[1], 64)
            me.link(v.tensor_tensor(route_sm, psum[0:4, 4:8, :].rearrange("p f c -> p (f c)"), stream[1][0:4, :], ALU.add))
            rs_f = route_sm.rearrange("p (f c) -> p f c", f=NF)
            me.link(v.tensor_reduce(sm_tmp[:, 0], rs_f.rearrange("p f c -> p c f"), AX.X, ALU.max))
            v.tensor_tensor(rs_f, rs_f, sm_tmp[:, 0].unsqueeze(1).to_broadcast([4, NF, MED]), ALU.subtract).then_inc(s_rl, 1)
            dve.wait_ge(s_re, 1)
            me.link(v.tensor_reduce(sm_tmp[:, 0], rs_f.rearrange("p f c -> p c f"), AX.X, ALU.add))
            me.link(v.reciprocal(sm_tmp[:, 1], sm_tmp[:, 0]))
            v.tensor_tensor(rs_f, rs_f, sm_tmp[:, 1].unsqueeze(1).to_broadcast([4, NF, MED]), ALU.mult).then_inc(s_rd, 1)
            for i in range(TILES):
                dve.wait_ge(s_f2e, i + 1)
                dve.wait_ge(s_wri, i + 1)
                if i >= 2:
                    dve.wait_ge(s_y, i - 1)
                v.tensor_tensor(ya[i % 2], spec[i % 2][:, 0], psum[:, 4, :], ALU.mult).then_inc(s_ya, 1)
                v.tensor_tensor(yb[i % 2], spec[i % 2][:, 1], psum[:, 5, :], ALU.mult).then_inc(s_yb, 1)

            def update_x1(m):
                b, q = divmod(m, 2)
                for mh in range(HALVES):
                    j = 2 * m + mh
                    dve.wait_ge(s_p2, j + 1)
                    xv = X[:, mh, b].rearrange("p (j o) -> p o j", o=WT)[:, 4 * q:4 * q + 4, :]
                    v.tensor_tensor(xv, psum[:, 4 + j % 4, :].rearrange("p (o j) -> p o j", o=4), xv, ALU.add).then_inc(s_x_new, 1)

            for i in range(TILES):
                dve.wait_ge(s_sw, i + 1)
                v.tensor_tensor(xp[:, i, :], xp[:, i, :], psum[:, i % 2, :], ALU.mult).then_inc(s_xw, 1)
                if i % 4 == 1 and i >= 5:
                    update_x1(i // 4 - 1)
            update_x1(3)

            if LAST < 2:
                return
            dve.wait_ge(s_x_new, 16)
            group_norm(2)
            dve.wait_ge(s_w2b, 64)
            me.link(v.tensor_tensor(pwm, pwm, head_mask.unsqueeze(1).to_broadcast([P, QKV_TILES, P]), ALU.mult))
            for t in range(QKV_TILES):
                for a_ in range(TENSOR_TAPS[t]):
                    ins = v.tensor_scalar(pwt[t][:, a_, :], pwm[:, t, :], col("dw2_w", t * K5 + a_), None, ALU.mult)
                    n = me.add(ins) if (t, a_) != (QKV_TILES - 1, TENSOR_TAPS[-1] - 1) else ins.then_inc(s_pwm, 1)

            def mask_products(src):
                me.link(v.tensor_tensor(ksum[:, src], kacc[:, src, :, 0:4:2], kacc[:, src, :, 1:4:2], ALU.add))
                for b in range(B):
                    for gr in range(2):
                        n = me.add(v.tensor_scalar(denw[:, src, b, gr, :], head_cols, ksum[:, src, gr, b:b + 1], None, ALU.mult))
                me.upto(n)
                for b in range(B):
                    dve.wait_ge(s_vk, src * TILES + WT * (b + 1))
                    v.tensor_tensor(vkm[:, src, b], psum[:, 6 + b, 0:2 * P].rearrange("p (g m) -> p g m", g=2),
                                    head_mask.unsqueeze(1).to_broadcast([P, 2, P]), ALU.mult).then_inc(s_vkm, 1)

            def invert_denominators(src):
                dve.wait_ge(s_den, 2 * src + 2)
                me.link(v.tensor_scalar(rden, psum[:, 0:2, :].rearrange("p c q -> p (c q)"), ATT_EPS, None, ALU.add))
                v.reciprocal(rden, rden).then_inc(s_rc, 1)

            def divide(src, s_):
                b, gr, c = s_ // 4, s_ // 2 % 2, s_ % 2
                n = 8 * src + s_
                dve.wait_ge(s_ns, n + 1)
                dve.wait_ge(s_rb, n + 1)
                v.tensor_tensor(att[2 * src + gr][:, b * PIX + c * BANK:b * PIX + (c + 1) * BANK], num_s[n % 2],
                                psum[:, 4 + n % 2, :], ALU.mult).then_inc(s_att, 1)

            for t in DVE_TILES:
                dve.wait_ge(s_qp, 4 * (t + 1))
                if t == 1:
                    dve.wait_ge(s_tr, TILES)
                for tap in range(TENSOR_TAPS[t], K5):
                    if tap > TENSOR_TAPS[t]:
                        me.upto(tap_n)
                    tap_n = filter_tap(v, me, t, tap)
                    late = tap - TENSOR_TAPS[t] - 6
                    if t == 1 and late == -4:
                        invert_denominators(0)
                    if t == 1 and late >= 0 and late % 2 == 0:
                        divide(0, late // 2)
                if t == 0:
                    dve.wait_ge(s_qf, 12)
                    mask_products(0)
            dve.wait_ge(s_yqe, 12)
            mask_products(1)
            invert_denominators(1)
            for s_ in range(8):
                divide(1, s_)
            for i in range(8):
                c, mh = divmod(i, 2)
                b, q = divmod(c, 2)
                dve.wait_ge(s_pje, i + 1)
                xv = X[:, mh, b, q * BANK:(q + 1) * BANK]
                v.tensor_tensor(xv, xv, proj_s[i % 2], ALU.add).then_inc(s_x_new, 1)
            if LAST < 3:
                return
            dve.wait_ge(s_x_new, 24)
            group_norm(3)
            for tap in range(9):
                ins = v.tensor_scalar(tap3[:, tap, :], ident, col("dw3_w", 9 + tap), None, ALU.mult)
                n = me.add(ins) if tap < 8 else ins.then_inc(s_d3, 1)
            dve.wait_ge(s_z, 12)
            dve.wait_ge(s_zb, 3)
            for tap in range(9):
                if tap:
                    me.upto(tap_n)
                for i in (0, 2):
                    tap_n = filter3(v, me, i, tap, s_dw3)

            def keep_flags(a_, i, data, thresh):
                me.link(v.tensor_reduce(pk[:, 2 * a_, i:i + 1], data, AX.X, ALU.max))
                me.link(v.tensor_scalar(pk[:, 2 * a_ + 1, i:i + 1], pk[:, 2 * a_, i:i + 1], thresh, None, ALU.is_ge))
                return pk[:, 2 * a_ + 1, i:i + 1]

            for a_, i in enumerate((0, 2, 1, 3)):
                dve.wait_ge(s_h3, a_ + 1)
                keep = keep_flags(0, i, h3[:, i, :], DW_THRESH)
                v.tensor_scalar(h3[:, i, :], h3[:, i, :], keep, None, ALU.mult).then_inc(s_kept, 1)
            for a_, i in enumerate((0, 2, 1, 3)):
                dve.wait_ge(s_o3, a_ + 1)
                keep = keep_flags(1, i, o3[:, i, :], PW_THRESH)
                xv = X.rearrange("p h b q -> p (h b) q")[:, i, :]
                v.scalar_tensor_tensor(xv, o3[:, i, :], keep, xv, ALU.mult, ALU.add).then_inc(s_x_new, 1)

        @block.scalar
        def _(act):
            a = nc.scalar

            def group_norm(layer, zc):
                act.wait_ge(s_gn_var, layer + 1)
                a.activation(gsd, gvar, ACT.Sqrt).then_inc(s_gn_sd, 1)
                if layer == 0:
                    act.wait_ge(s_bnv, 1)
                    a.activation(bnsd, bnv, ACT.Sqrt).then_inc(s_bnsd, 1)
                if zc is None:
                    return
                act.wait_ge(s_gn_coef, layer + 1)
                for i in range(4):
                    a.activation(zc[:, i], X.rearrange("p h b q -> p (h b) q")[:, i], ACT.Identity, scale=grs[:, i:i + 1],
                                 bias=gnb[:, i:i + 1]).then_inc(s_zc, 1)

            act.wait_ge(s_const, 80)
            group_norm(0, Zc)
            act.wait_ge(s_lnv, 1)
            a.activation(ln_sd, ln_var, ACT.Sqrt).then_inc(s_lnsd, 1)
            for t in range(8):
                q, k = divmod(t, 2)
                act.wait_ge(s_back, t + 1)
                a.activation(g1cm[:, k, 4 * q:4 * q + 4, :], psum[:, t, :].rearrange("p (x q) -> p x q", x=4), ACT.Gelu,
                             scale=col("ln_g", k), bias=col("ln_b", k)).then_inc(s_g1, 1)
            for hf in range(2):
                act.wait_ge(s_lgs, hf + 1)
                a.activation(mask[:, hf], mask[:, hf], ACT.Exp).then_inc(s_exp, 1)
            offs = OM[:, :, 0:2 * G * K2].rearrange("p x (h g k a) -> p h a k x g", h=2, g=GH, k=K2)
            for hf in range(2):
                if hf == 0:
                    act.wait_ge(s_om, XX)
                    act.wait_ge(s_ome, XX)
                else:
                    act.wait_ge(s_wd, 1)
                for ax in range(2):
                    for k in range(3):
                        a.activation(hats[:, 3 * ax + k].rearrange("p k (x g) -> p k x g", g=GH), offs[:, hf, ax], ACT.Abs,
                                     bias=hat_shift[:, k:k + 1]).then_inc(s_abs, 1)
            act.wait_ge(s_wd, 2)
            for hf in range(2):
                act.wait_ge(s_acc, ND * ND * (hf + 1))
                for q in range(4):
                    a.activation(outT[:, hf, 4 * q:4 * q + 4, :], psum[:, 4 * hf + q, :].rearrange("p (x q) -> p x q", x=4),
                                 ACT.Copy).then_inc(s_outT, 1)

            if LAST < 1:
                return
            group_norm(1, Zc1)
            for c in range(CHUNKS):
                act.wait_ge(s_fc1, c + 1)
                a.activation(sr_act[:, c * BANK:(c + 1) * BANK], psum[:, c, :], ACT.Relu, bias=col("fc1_b")).then_inc(s_fc1r, 1)
            for c in range(CHUNKS):
                act.wait_ge(s_cv, c + 1)
                a.activation(sr_act[:, c * BANK:(c + 1) * BANK], psum[:, 4 + c, :], ACT.Relu, bias=col("conv_b"),
                             accum_out=racc[:, c:c + 1]).then_inc(s_cvr, 1)
            for i in range(TILES + 4):
                if i < TILES:
                    act.wait_ge(s_pw1, i + 1)
                    a.activation(xp[:, i, :], psum[:, i % 4, :], ACT.Relu).then_inc(s_pw1r, 1)
                if i >= 4:
                    n = i - 4
                    b, t = divmod(n, WT)
                    act.wait_ge(s_f1, n + 1)
                    if n == 0:
                        act.wait_ge(s_cwe, 1)
                    a.activation(U[b][:, t, :], psum[:, 4 + n % 4, :], ACT.Copy).then_inc(s_f1e, 1)
            for c in range(CHUNKS):
                act.wait_ge(s_sp, c + 1)
                if c == 0:
                    act.wait_ge(s_cvr, 4)
                a.activation(sr_act[:, c * BANK:(c + 1) * BANK], psum[:, c, :], ACT.Relu, bias=col("sp1_b")).then_inc(s_spr, 1)
            act.wait_ge(s_rl, 1)
            a.activation(route_sm, route_sm, ACT.Exp).then_inc(s_re, 1)
            for i in range(TILES + 2):
                if i < TILES:
                    act.wait_ge(s_f2, i + 1)
                    if i >= 2:
                        act.wait_ge(s_ya, i - 1)
                        act.wait_ge(s_yb, i - 1)
                    a.activation(spec[i % 2], psum[:, 2 * (i % 2):2 * (i % 2) + 2, :], ACT.Copy).then_inc(s_f2e, 1)
                if i >= 2:
                    n = i - 2
                    b, t = divmod(n, WT)
                    act.wait_ge(s_i2, n + 1)
                    if n == 0:
                        act.wait_ge(s_uo[0], 16 * WT)
                        act.wait_ge(s_uo[1], 16 * WT)
                    a.activation(U[b][:, t, :], psum[:, 6 + n % 2, :], ACT.Copy).then_inc(s_i2e, 1)
            for n in range(TILES):
                b, t = divmod(n, WT)
                act.wait_ge(s_o1, n + 1)
                if t == 0:
                    act.wait_ge(s_uo[b], 32 * WT)
                a.activation(OT[b][:, :, t, :], psum[:, 2 + n % 2, :].rearrange("p (k j) -> p k j", k=KM), ACT.Copy).then_inc(s_o1e, 1)

            if LAST < 2:
                return
            group_norm(2, Zc2)
            act.wait_ge(s_qb, 1)
            for i in range(QKV_TILES * CHUNKS):
                t, c = divmod(i, CHUNKS)
                b, yh = divmod(c, 2)
                act.wait_ge(s_qkv, i + 1)
                a.activation(padq[:, t, b, 2 + 16 * yh:18 + 16 * yh, 2:2 + W], psum[:, i % 4, :].rearrange("p (y x) -> p y x", y=16),
                             ACT.Copy).then_inc(s_qp, 1)
                dst = flat[t][:, c * BANK:(c + 1) * BANK]
                if t in (1, 3):
                    a.activation(dst, psum[:, i % 4, :], ACT.Copy).then_inc(s_qf, 1)
                elif t in (0, 2):
                    a.activation(dst, psum[:, i % 4, :], ACT.Relu, accum_out=kacc[:, 0, t // 2, c:c + 1]).then_inc(s_qf, 1)
                else:
                    a.activation(dst, psum[:, i % 4, :], ACT.Relu).then_inc(s_qf, 1)

            def copy_turned(src, between=0):
                for i in range(TILES):
                    n = src * TILES + i
                    act.wait_ge(s_tr, n + 1)
                    if n >= 2:
                        act.wait_ge(s_vk, n - 1)
                    a.activation(turned[n % 2], psum[:, 4 + n % 2, :], ACT.Copy).then_inc(s_trc, 1)
                    if between and i % between == 0:
                        tap_products(1)

            def copy_numerators(src, between):
                for s_ in range(8):
                    n = 8 * src + s_
                    act.wait_ge(s_num, n + 1)
                    if n >= 2:
                        act.wait_ge(s_att, n - 1)
                    a.activation(num_s[n % 2], psum[:, 2 + n % 2, :], ACT.Copy).then_inc(s_ns, 1)
                    tap_products(between)

            def copy_local(tiles):
                for n_ in tiles:
                    t = Y_ORDER[n_]
                    for c in range(CHUNKS):
                        act.wait_ge(s_yq, 4 * n_ + c + 1)
                        dst = local[t][:, c * BANK:(c + 1) * BANK]
                        if t in (1, 3):
                            a.activation(dst, psum[:, c, :], ACT.Copy).then_inc(s_yqe, 1)
                        elif t in (0, 2):
                            a.activation(dst, psum[:, c, :], ACT.Relu, accum_out=kacc[:, 1, t // 2, c:c + 1]).then_inc(s_yqe, 1)
                        else:
                            a.activation(dst, psum[:, c, :], ACT.Relu).then_inc(s_yqe, 1)

            made = [0]

            def tap_products(count):
                for _ in range(min(count, len(pool_taps) - made[0])):
                    n = made[0]
                    t, tap, b = pool_taps[n]
                    if n >= 4:
                        act.wait_ge(s_ta, n - 3)
                    a.activation(tap_tmp[n % 4].rearrange("p (y x) -> p y x", y=H), tap_view(t, tap, b), ACT.Copy,
                                 scale=col("dw2_w", t * K5 + tap)).then_inc(s_tp, 1)
                    made[0] += 1

            copy_turned(0)
            tap_products(2)
            copy_local([0])
            copy_numerators(0, 2)
            tap_products(4)
            copy_local([1])
            tap_products(20)
            copy_local([2])
            tap_products(20)
            copy_local([3])
            tap_products(len(pool_taps) - made[0] - 12)
            copy_local([4])
            copy_turned(1, 2)
            tap_products(len(pool_taps))
            copy_local([5])
            copy_numerators(1, 0)
            act.wait_ge(s_bn, 1)
            act.wait_ge(s_vk, 2 * TILES)
            for i in range(8):
                mh = i % 2
                act.wait_ge(s_pj, i + 1)
                if i >= 2:
                    act.wait_ge(s_x_new, 16 + i - 1)
                a.activation(proj_s[i % 2], psum[:, i % 4, :], ACT.Identity, scale=bn_inv[:, mh:mh + 1], bias=bn_off[:, mh:mh + 1]).then_inc(s_pje, 1)
            if LAST < 3:
                return
            group_norm(3, None)
            act.wait_ge(s_z, 10)
            act.wait_ge(s_zb, 3)
            for tap in range(9):
                dy, dx = divmod(tap, 3)
                if tap >= 2:
                    act.wait_ge(s_dw3p, tap - 1)
                a.activation(tap3_tmp[tap % 2].rearrange("p (y x) -> p y x", y=H), Z[:, 1, PAD - 1 + dy:PAD - 1 + dy + H, PAD - 1 + dx:PAD - 1 + dx + W],
                             ACT.Copy, scale=col("dw3_w", tap)).then_inc(s_tp3, 1)
            for n, i in enumerate((0, 2, 1, 3)):
                h = i // 2
                scale, bias = bn_inv[:, 2 + h:3 + h], bn_off[:, 2 + h:3 + h]
                if i == 3:
                    act.wait_ge(s_dw3t, 1)
                    a.activation(h3[:, i, :].rearrange("p (c q) -> p c q", c=2), psum[:, 0:2, :], ACT.Relu, scale=scale, bias=bias).then_inc(s_h3, 1)
                else:
                    if i == 1:
                        act.wait_ge(s_dw3p, 9)
                    else:
                        act.wait_ge(s_dw3, n + 1)
                    a.activation(h3[:, i, :], h3[:, i, :], ACT.Relu, scale=scale, bias=bias).then_inc(s_h3, 1)
            for n, i in enumerate((0, 2, 1, 3)):
                h, b = divmod(i, 2)
                act.wait_ge(s_pw3, n + 1)
                bank = (2 + 4 * b + 2 * h) % 8
                a.activation(o3[:, i, :].rearrange("p (c q) -> p c q", c=2), psum[:, bank:bank + 2, :], ACT.Relu,
                             scale=bn_inv[:, 4 + h:5 + h], bias=bn_off[:, 4 + h:5 + h]).then_inc(s_o3, 1)

        @block.gpsimd
        def _(pool):
            g = nc.gpsimd
            me = Steps(pool, s_pool)

            def zero_border():
                g.memset(Z[:, :, 0:PAD, :], 0.0)
                g.memset(Z[:, :, PAD + H:, :], 0.0)
                g.memset(Z[:, :, PAD:PAD + H, 0:PAD], 0.0)
                return g.memset(Z[:, :, PAD:PAD + H, PAD + W:], 0.0)

            zero_border().then_inc(s_zb, 1)
            g.memset(XSc[:, 0:PAD], 0.0)
            g.memset(XSc[:, PAD + XX:], 0.0).then_inc(s_shz, 1)
            g.memset(XSd, 0.0).then_inc(s_shz, 1)
            pool.wait_ge(s_amax, 1)
            me.link(g.partition_all_reduce(amax_all, amax, P, bass.bass_isa.ReduceOp.max))
            me.add(g.tensor_scalar(within, amax_all, 1.0, None, ALU.is_le))
            me.link(g.tensor_scalar(beyond, amax_all, 1.0, None, ALU.is_gt))
            pool.wait_ge(s_mask, 2)
            any_beyond = pool.value_load(beyond[0:1, 0:1], min_val=0, max_val=1)
            general_path(pool, g, any_beyond)
            g.memset(small[:, 442:443], 0.0).then_inc(s_general, 1)
            for n in range(len(plan)):
                if by_pool[n]:
                    await_product_inputs(pool, n)
                    if n in last_of_half:
                        me.link(product(g, n))
                        add_general(pool, g, any_beyond, n)
                        g.memset(small[:, 443:444], 0.0).then_inc(s_pp, 1)
                    else:
                        product(g, n).then_inc(s_pp, 1)
            if LAST < 1:
                return
            pool.wait_ge(s_acc, len(plan))
            pool.wait_ge(s_mask, 2)
            zero_border().then_inc(s_zb, 1)
            pool.wait_ge(s_craw, 32)
            n = me.add(g.tensor_tensor(cwe[:, 0], craw[:, 0], craw[:, 1], ALU.add))
            me.add(g.tensor_tensor(craw[:, 2], craw[:, 2], ccoef[:, 0], ALU.mult))
            me.link(g.tensor_tensor(craw[:, 3], craw[:, 3], ccoef[:, 1], ALU.mult))
            me.link(g.tensor_scalar(cwe[:, 0], cwe[:, 0], 0.5, None, ALU.mult))
            g.tensor_tensor(cwe[:, 1], craw[:, 2], craw[:, 3], ALU.add).then_inc(s_cwe, 1)
            for i in range(TILES):
                pool.wait_ge(s_sq, i + 1)
                g.tensor_scalar(xp[:, i, :], xp[:, i, :], col("star_scale"), col("star_bias"), ALU.mult, ALU.add).then_inc(s_xpd, 1)
            for i in range(TILES):
                pool.wait_ge(s_ya, i + 1)
                pool.wait_ge(s_yb, i + 1)
                if i >= 2:
                    pool.wait_ge(s_i2, i - 1)
                g.tensor_tensor(y_w[i % 2], ya[i % 2], yb[i % 2], ALU.add).then_inc(s_y, 1)
            if LAST < 2:
                return
            pool.wait_ge(s_x_new, 16)
            borders = padq.rearrange("p t b y x -> p (t b) y x")
            g.memset(borders[:, :, 0:2, :], 0.0)
            g.memset(borders[:, :, 2 + H:, :], 0.0)
            g.memset(borders[:, :, 2:2 + H, 0:2], 0.0)
            g.memset(borders[:, :, 2:2 + H, 2 + W:], 0.0).then_inc(s_qb, 1)
            for n, (t, tap, b) in enumerate(pool_taps):
                if n == 0:
                    pool.wait_ge(s_tr, TILES)
                if tap == TENSOR_TAPS[t] and t == 5:
                    pool.wait_ge(s_yq, 4)
                pool.wait_ge(s_tp, n + 1)
                dst = local[t][:, b * PIX:(b + 1) * PIX]
                if tap == TENSOR_TAPS[t]:
                    g.tensor_copy(dst, tap_tmp[n % 4]).then_inc(s_ta, 1)
                else:
                    pool.wait_ge(s_ta, n - 1)
                    g.tensor_tensor(dst, dst, tap_tmp[n % 4], ALU.add).then_inc(s_ta, 1)
            if LAST < 3:
                return
            pool.wait_ge(s_x_new, 24)
            zero_border().then_inc(s_zb, 1)
            for tap in range(9):
                pool.wait_ge(s_tp3, tap + 1)
                if tap == 0:
                    g.tensor_copy(h3[:, 1, :], tap3_tmp[0]).then_inc(s_dw3p, 1)
                else:
                    pool.wait_ge(s_dw3p, tap)
                    g.tensor_tensor(h3[:, 1, :], h3[:, 1, :], tap3_tmp[tap % 2], ALU.add).then_inc(s_dw3p, 1)


def host_arrays(**i):
    at, n = channel_columns()
    cv = np.zeros((P, n), np.float32)

    def put(name, a):
        a = np.asarray(a, np.float32).reshape(-1, P, *np.shape(a)[1:]).reshape(-1, P, int(np.prod(np.shape(a)[1:]) or 1))
        lo, hi = at[name]
        cv[:, lo:hi] = a.transpose(1, 0, 2).reshape(P, hi - lo)

    put("dw0_w", i["L0_conv_dw_w"].reshape(C, 9))
    for name, src in (("dw0_b", "dw_b"), ("ln_g", "ln_g"), ("ln_b", "ln_b"), ("out_b", "out_b")):
        put(name, i["L0_conv_" + src])
    r = {"chan_vecs": cv, "ident": np.eye(P, dtype=np.float32)}
    blocks = np.kron(np.eye(16, dtype=np.float32), np.ones((8, 8), np.float32))
    r["gmean"] = blocks / 8
    r["head_mask"] = blocks
    sc = np.zeros((P, 7), np.float32)
    sc[:, 0:3] = [1, 0, -1]
    xh = np.arange(P) % 2
    sc[:, 3:5] = (xh == 1)[:, None]
    sc[:, 5:7] = (xh == 0)[:, None]
    r["small_consts"] = sc
    for name in ("in_w", "in_b", "off_w", "off_b", "mask_w", "mask_b", "out_w"):
        r[name] = np.ascontiguousarray(i["L0_conv_" + name])
    put("star_scale", np.broadcast_to(i["L1_conv_star_scale"], (P,)))
    put("star_bias", np.broadcast_to(i["L1_conv_star_bias"], (P,)))
    put("fc1_b", i["L1_conv_rw_fc1_b"])
    put("conv_b", i["L1_conv_rw_conv_b"])
    put("sp1_b", i["L1_conv_sp_fc1_b"])
    r["fc1_w"] = i["L1_conv_rw_fc1_w"][:, :, 0, 0].T
    r["conv_w"] = i["L1_conv_rw_conv_w"][:, :, 0, 0].T
    r["pw1_w"] = i["L1_conv_w_pw1"].T
    r["pw2_w"] = i["L1_conv_w_pw2"].T
    r["sp1_w"] = i["L1_conv_sp_fc1_w"].reshape(P, C, 9).transpose(1, 2, 0)
    r["fc2_w"] = np.concatenate([i["L1_conv_rw_fc2_w"][:, :, 0, 0].T[None], i["L1_conv_sp_fc2_w"].reshape(-1, P, 9).transpose(2, 1, 0)])
    r["fc2_b"] = np.stack([i["L1_conv_rw_fc2_b"]] * 2 + [i["L1_conv_sp_fc2_b"]] * 2)
    r["dft"] = dft_constants()
    first, second, sign = spectra_maps()
    cw = i["L1_conv_complex_weights"].transpose(2, 3, 0, 1)
    r["spectra"] = np.stack([cw[:, part, m[:, 0], m[:, 1]] for part in (0, 1) for m in (first, second)], 1)
    r["spectra_coef"] = np.broadcast_to(sign, (NF, 2, 1024))
    r["spatial_w"] = i["L1_conv_spatial_weights"].reshape(P, WT, NF).transpose(2, 1, 0).reshape(NF, PIX)
    chan = np.concatenate([[24 * (16 * gr + m // 8) + off + m % 8 for m in range(P)]
                           for gr, off in ((0, 8), (0, 16), (1, 8), (1, 16), (0, 0), (1, 0))])
    r["qkv_w"] = i["L2_conv_w_qkv"][chan].T
    put("dw2_w", i["L2_conv_w_dw"].reshape(-1, K5)[chan])
    r["pointwise_w"] = np.tile(i["L2_conv_w_pw"].reshape(-1, 8)[chan].T, (16, 1))
    r["proj_w"] = i["L2_conv_w_proj"].T
    hc = np.zeros((P, 32), np.float32)
    hc[np.arange(P), np.arange(P) // 8] = 1
    r["head_cols"] = hc
    hr = np.zeros((4, 32, P), np.float32)
    hr[:, np.arange(P) // 8, np.arange(P)] = 1
    r["head_rows"] = hr.reshape(P, P)
    for name, l2, l3 in (("bn_g", "gamma", "g"), ("bn_b", "beta", "b"), ("bn_m", "mean", "m"), ("bn_v", "var", "v")):
        put(name, np.concatenate([i["L2_conv_bn_" + l2], i["L3_conv_bn1_" + l3], i["L3_conv_bn2_" + l3]]))
    put("dw3_w", i["L3_conv_dw_w"].reshape(C, 9))
    put("l3_b", np.concatenate([i["L3_conv_dw_b"], i["L3_conv_pw_b"]]))
    r["pw3_w"] = i["L3_conv_pw_w"][:, :, 0, 0].T
    return {k: np.ascontiguousarray(a) for k, a in r.items()}


def dft_rows():
    rows = []
    for t in range(WT):
        if t == 0:
            for ky in (0, H // 2):
                rows += [(ky, kx, 0) for kx in range(17)] + [(ky, kx, 1) for kx in range(1, 16)]
        for ky in ([1] if t == 0 else [2 * t, 2 * t + 1]):
            rows += [(ky, kx, part) for part in (0, 1) for kx in range(W)]
    return rows


def dft_constants():
    comps = []
    for t in range(WT):
        comps.append([(0, 0), (H // 2, 0), (1, 0), (1, 1)] if t == 0 else [(2 * t, 0), (2 * t, 1), (2 * t + 1, 0), (2 * t + 1, 1)])
    f1 = np.zeros((P, P))
    for t in range(WT):
        for j, (ky, part) in enumerate(comps[t]):
            for y in range(H):
                ang = 2 * np.pi * ky * y / H
                val = (np.cos(ang) if part == 0 else -np.sin(ang)) / np.sqrt(H)
                for i in range(4):
                    f1[16 * t + 4 * j + i, 4 * y + i] = val
    rows = dft_rows()
    f2, f2s = np.zeros((2, P, P)), np.zeros((2, P, P))
    for a, t in enumerate((0, 1)):
        for m in range(P):
            ky, kx, part = rows[t * P + m]
            for j, (cy, cpart) in enumerate(comps[t]):
                if cy != ky:
                    continue
                for x in range(W):
                    q = 8 * (4 * j + x // 8) + x % 8
                    e = np.exp(-2j * np.pi * kx * x / W) / np.sqrt(W) * (1j if cpart else 1)
                    f2[a, m, q] = e.imag if part else e.real
                    f2s[a, m, q] = e.real if part else -e.imag
    mats = [f1.T, f2[0].T, f2[1].T, f2s[0].T, f2s[1].T, np.linalg.inv(f2[0]).T, np.linalg.inv(f2[1]).T,
            np.linalg.inv(f1).T]
    return np.stack(mats, 1).astype(np.float32)


def spectra_maps():
    first, second, sign = [], [], np.zeros((2, 1024), np.float32)
    for n, (ky, kx, part) in enumerate(dft_rows()):
        if kx in (0, W // 2):
            first.append((ky, kx)); second.append((-ky % H, kx)); sign[:, n] = 0.5, -0.5
        elif kx < W // 2:
            first.append((ky, kx)); second.append((ky, kx)); sign[:, n] = 0.5, 0.5
        else:
            first.append((-ky % H, W - kx)); second.append(first[-1]); sign[:, n] = -0.5, -0.5
    return np.array(first), np.array(second), sign


def kernel(**inputs):
    import concourse.bacc as bacc
    from concourse.bass_utils import run_bass_kernel_spmd

    inputs = {k: np.asarray(a) for k, a in inputs.items()}
    nc = bacc.Bacc("TRN2", target_bir_lowering=False, num_devices=1)
    arrays = {"x_dram": np.ascontiguousarray(inputs.pop("x").reshape(B, C, PIX))}
    arrays.update({k + "_dram": a for k, a in host_arrays(**inputs).items()})
    aps = {k[:-5]: nc.dram_tensor(k, a.shape, mybir.dt.from_np(a.dtype), kind="ExternalInput").ap() for k, a in arrays.items()}
    out = nc.dram_tensor("out_dram", (B, C, PIX), F32, kind="ExternalOutput").ap()
    pad_image = nc.dram_tensor("xproj_padded", (B, PADDED, PADDED, C), F32).ap()
    general = nc.dram_tensor("general_sample", (HALVES, P, XX * P), F32).ap()
    aps["bounce"] = nc.dram_tensor("bounce", (2, B, P, WT, MED), F32).ap()
    mixer_kernel(nc, aps.pop("x"), out, aps, pad_image, general, LAST_LAYER)
    r = run_bass_kernel_spmd(nc, [arrays], core_ids=[0])
    return r.results[0]["out_dram"].reshape(B, C, H, W)
```

```python
from contextlib import ExitStack

import numpy as np
import concourse.bass as bass
from concourse import mybir

F32 = mybir.dt.float32
I32 = mybir.dt.int32
ALU = mybir.AluOpType
ACT = mybir.ActivationFunctionType
AX = mybir.AxisListType

B, C, H, W = 2, 256, 32, 32
PIX = H * W
P = 128
HALVES = C // P
COLS = B * PIX
PAD = 2
HP = H + 2 * PAD
BANK = 512
CHUNKS = COLS // BANK
G, K2 = 16, 9
XX = W // 2
NOM = 3 * G * K2
GH = G // HALVES
CG = C // G
XG = XX * GH
NPT = K2 * XG
ND = 5
MED, NF = 2 * C, 4
KM = MED // P
WT = 8
TILES = B * WT
QKV_TILES = 6
K5 = 25
TENSOR_TAPS = [4, 4, 4, 5, 5, 5]
EARLY_PRODUCTS = 18
QROW = H + 4
ATT_EPS = 1e-15
DW_THRESH, PW_THRESH = 4.0, 0.001
GN_EPS = 1e-5
DW_TAPS = 5
POOL_FROM = 25
REACH = H
PADDED = H + 2 * REACH
LAST_LAYER = 3


class Steps:

    def __init__(self, engine, sem):
        self.engine, self.sem, self.n = engine, sem, 0

    def add(self, ins):
        ins.then_inc(self.sem, 1)
        self.n += 1
        return self.n

    def link(self, ins):
        self.add(ins)
        self.engine.wait_ge(self.sem, self.n)

    def upto(self, n):
        self.engine.wait_ge(self.sem, n)


def channel_columns():
    names, at = {}, 0
    for name, width in (("dw0_w", 18), ("dw0_b", 2), ("ln_g", 2), ("ln_b", 2), ("out_b", 2),
                        ("star_scale", 1), ("star_bias", 1), ("fc1_b", 1), ("conv_b", 1), ("sp1_b", 1),
                        ("dw2_w", 150), ("dw3_w", 18), ("bn_g", 6), ("bn_b", 6), ("bn_m", 6), ("bn_v", 6),
                        ("l3_b", 4)):
        names[name] = (at, at + width)
        at += width
    return names, at


def mixer_kernel(nc, x_in, out, w, xpad_dram, general_dram, LAST):
    cv_at, cv_n = channel_columns()
    with ExitStack() as ctx:
        def sem(name):
            return ctx.enter_context(nc.semaphore(name))

        arena_words = 53000
        arena = ctx.enter_context(nc.sbuf_tensor("arena", [P, arena_words], F32))
        psum = ctx.enter_context(nc.psum_tensor("psum", [P, 8, BANK], F32))

        def words(at, n):
            assert at + n <= arena_words, (at, n)
            return arena[:, at:at + n]

        top = [0]

        def take(n):
            top[0] += n
            return words(top[0] - n, n)

        X = take(HALVES * COLS).rearrange("p (h b q) -> p h b q", h=HALVES, b=B)
        Z = take(HALVES * B * HP * HP).rearrange("p (i y x) -> p i y x", y=HP, x=HP)
        z_base = HALVES * COLS
        ident = take(P)
        gmean = take(P)
        head_mask = take(P)
        cv = take(cv_n)
        small = take(512)
        L = top[0]

        def col(name, i=0, n=1):
            a, _ = cv_at[name]
            return cv[:, a + i:a + i + n]

        Xi = X.rearrange("p h b (y x) -> p (h b) y x", y=H)

        def z_inner(i):
            return Z[:, i, PAD:PAD + H, PAD:PAD + W]

        st = small[:, 0:48].rearrange("p (i c s) -> p i c s", i=4, c=2)
        mv = small[:, 48:56].rearrange("p (i s) -> p i s", s=2)
        gq = small[:, 56:64].rearrange("p (s i) -> p s i", s=2)
        gm = small[:, 64:72].rearrange("p (s i) -> p s i", s=2)
        gvar, gsd, grs, gt, gnb = (small[:, 72 + 4 * j:76 + 4 * j] for j in range(5))
        amax, amax_all, within = (small[:, 92 + j:93 + j] for j in range(3))
        beyond = small[:, 95:96].bitcast(I32)
        hat_shift = small[:, 96:99]
        valid_halo = small[:, 99:103]
        ln_st = small[:, 104:200].rearrange("p (x s) -> p x s", s=6)
        ln_mv = small[:, 200:232].rearrange("p (x s) -> p x s", s=2)
        ln_var, ln_sd, ln_rs, ln_t, ln_nb = (small[:, 232 + 16 * j:248 + 16 * j] for j in range(5))

        s_x, s_const, s_w0 = sem("x_loaded"), sem("consts_loaded"), sem("l0_weights_loaded")
        s_gn_stats, s_gn_means, s_gn_var = sem("gn_stats"), sem("gn_group_means"), sem("gn_var")
        s_gn_sd, s_gn_coef, s_z = sem("gn_sd"), sem("gn_coef"), sem("z_padded_written")
        s_zc = sem("z_unpadded_written")
        s_zb = sem("z_border_zero")
        s_x_new = sem("x_updated")
        s_dve, s_act, s_pool = sem("dve_steps"), sem("act_steps"), sem("pool_steps")
        s_out = sem("output_stored")

        o = L
        inw = words(o, 512).rearrange("p (k c) -> p k c", k=2); o += 512
        omw = words(o, 2 * NOM).rearrange("p (k c) -> p k c", k=2); o += 2 * NOM
        outw = words(o, 512).rearrange("p (k c) -> p k c", k=2); o += 512
        inb = words(o, C); o += C
        omb = words(o, NOM); o += NOM
        XSc = words(o, (XX + 4) * C).rearrange("p (x c) -> p x c", c=C); o += (XX + 4) * C
        XSd = words(o, 4 * (XX + 4) * P).rearrange("p (d x c) -> p d x c", d=4, c=P); o += 4 * (XX + 4) * P
        r1 = o; o += 2 * HALVES * COLS
        Zc = words(o, HALVES * COLS).rearrange("p (i q) -> p i q", q=PIX)
        OM = words(o, XX * NOM).rearrange("p (x o) -> p x o", o=NOM); o += XX * NOM
        mask = words(o, 2 * NPT).rearrange("p (h k g) -> p h k g", h=2, k=K2); o += 2 * NPT
        wd_at = o
        Wd = words(o, ND * ND * XG).rearrange("p (i j g) -> p i j g", i=ND, j=ND); o += ND * ND * XG
        hats1_y = words(o, 3 * NPT).rearrange("p (a k g) -> p a k g", a=3, k=K2); o += 3 * NPT
        x1cm = words(r1, HALVES * COLS).rearrange("p (h q) -> p h q", h=HALVES)
        x1n = words(r1 + HALVES * COLS, HALVES * COLS).rearrange("p (x c) -> p x c", c=C)
        x1_rest = words(r1 + HALVES * COLS, HALVES * COLS).rearrange("p (h q) -> p h q", h=HALVES)
        dw_tmp = [words(wd_at + COLS * j, COLS) for j in range(3)]
        s_dwp, s_dwa = sem("dw_tap_products"), sem("dw_tap_products_added")
        g1cm = words(r1, HALVES * COLS).rearrange("p (h x q) -> p h x q", h=HALVES, x=XX)
        hats = words(r1, 6 * NPT).rearrange("p (a k g) -> p a k g", a=6, k=K2)
        wk = [words(r1 + 6 * NPT, NPT), mask[:, 0].rearrange("p k g -> p (k g)")]
        s_wk, s_wka = sem("weight_terms"), sem("weight_terms_added")
        wk1 = words(L, NPT)
        hats1_x = OM.rearrange("p x o -> p (x o)")[:, XX * NOM - 3 * NPT:].rearrange("p (a k g) -> p a k g", a=3, k=K2)
        prods = [words(at, COLS) for at in (z_base, z_base + COLS, r1 + HALVES * COLS, r1 + (HALVES + 1) * COLS)]
        NB = len(prods)
        sm_t = words(z_base + 4096, 2 * XG).rearrange("p (h g) -> p h g", h=2)
        sm_r = words(z_base + 4096 + 2 * XG, 2 * XG).rearrange("p (h g) -> p h g", h=2)
        Wds = [Wd, OM.rearrange("p x o -> p (x o)")[:, 0:ND * ND * XG].rearrange("p (i j g) -> p i j g", i=ND, j=ND)]
        outT = words(r1, HALVES * COLS).rearrange("p (h x q) -> p h x q", h=HALVES, x=XX)

        s_xp, s_xpe = sem("xproj_ready"), sem("xproj_evacuated")
        s_shift = [sem(f"xproj_shifted_{j}") for j in range(4)]
        s_shz = sem("shift_border_zero")
        s_x1 = sem("x1_ready")
        s_lnv, s_lnsd = sem("ln_var"), sem("ln_sd")
        s_x1t, s_x1n = sem("x1_turned"), sem("x1_normalised")
        s_back, s_g1 = sem("x1n_turned_back"), sem("gelu_done")
        s_om, s_ome = sem("offset_mask_ready"), sem("offset_mask_evacuated")
        s_lgs, s_exp = sem("mask_logits_shifted"), sem("mask_exp")
        s_amax, s_flag = sem("offset_amax"), sem("offset_flag")
        s_habs, s_mask, s_general = sem("hat_values"), sem("mask_ready"), sem("general_path_done")
        s_hat = [sem(f"hats_ready_{hf}") for hf in range(2)]
        s_wd = [sem(f"displacement_weights_{hf}") for hf in range(2)]
        s_offx = sem("offsets_x_copied")
        s_pd, s_pp = sem("product_by_dve"), sem("product_by_pool")
        s_acc = sem("product_accumulated")
        s_outT, s_op, s_halo = sem("sampled_evacuated"), sem("out_projected"), sem("halo_columns")
        s_gen, s_gstep = sem("general_dma"), sem("general_step")

        o = L
        fc1w = words(o, 2 * P).rearrange("p (k c) -> p k c", k=2); o += 2 * P
        convw = words(o, P); o += P
        pw1w = words(o, 2 * MED).rearrange("p (k c) -> p k c", k=2); o += 2 * MED
        sp1w = words(o, 18 * P).rearrange("p (k t c) -> p k t c", k=2, t=9)
        sm_tmp = words(o, 2 * MED)[0:4].rearrange("p (a c) -> p a c", a=2); o += 18 * P
        pw2w = words(o, KM * C).rearrange("p (k c) -> p k c", k=KM); o += KM * C
        dft = words(o, 8 * P).rearrange("p (a m) -> p a m", a=8); o += 8 * P
        cwe = words(o, 2 * 1024)[0:NF].rearrange("p (a m) -> p a m", a=2); o += 2048
        spw = words(o, 1024)[0:NF]; o += 1024
        stream = [words(o + 2048 * j, 2048) for j in range(3)]; o += 3 * 2048
        route = stream[2][0:NF].rearrange("p (r c) -> p r c", r=4)
        sr_act = words(o, COLS)
        route_sm = sr_act[0:4, :]; o += COLS
        Zc1 = words(o, HALVES * COLS).rearrange("p (i q) -> p i q", q=PIX)
        V = [words(o + 4096 * b, 4096).rearrange("p (t c) -> p t c", t=WT) for b in range(B)]; o += 8192
        craw = words(o, 4096)[0:NF].rearrange("p (a m) -> p a m", a=4)
        ccoef = words(o + 4096, 2048)[0:NF].rearrange("p (a m) -> p a m", a=2)
        U = [words(o + 4096 * b, 4096).rearrange("p (t c) -> p t c", t=WT) for b in range(B)]; o += 8192
        OT = [u.rearrange("p t c -> p (t c)").rearrange("p (k t j) -> p k t j", k=KM, t=WT) for u in U]
        xp = words(o, TILES * MED).rearrange("p (t c) -> p t c", t=TILES); o += TILES * MED
        racc = small[:, 322:326]
        rmean = small[:, 326:330]
        lhs_u = small[:, 330:366].rearrange("p (t m) -> p t m", t=9)
        rsum2 = words(o, 256); o += 256
        rsums = rsum2[:, 0:192].rearrange("p (v b y) -> p v b y", v=3, b=2)

        s_w1, s_w1b, s_craw = sem("l1_weights_loaded"), sem("l1_late_weights"), sem("l1_spectra_loaded")
        s_cwe, s_cols0 = sem("l1_spectra_ready"), sem("l1_zero_columns")
        s_str = [sem(f"l1_stream_{j}") for j in range(3)]
        s_fc1, s_fc1r, s_cv, s_cvr = sem("fc1"), sem("fc1_relu"), sem("conv"), sem("conv_relu")
        s_pw1, s_pw1r, s_sq, s_xpd = sem("pw1"), sem("pw1_relu"), sem("pw1_squared"), sem("xp_ready")
        s_f1, s_f1e = sem("rows_dft"), sem("rows_dft_evacuated")
        s_uo = [sem(f"bounce_out_{b}") for b in range(B)]
        s_vi = [sem(f"bounce_in_{j}") for j in range(TILES)]
        s_sp, s_spr, s_u = sem("sp_conv"), sem("sp_relu"), sem("sp_tap_means")
        s_fc2, s_fc2c, s_rmean = sem("fc2"), sem("fc2_chunk"), sem("route_mean")
        s_rl, s_re, s_rd, s_rt = sem("route_logits"), sem("route_exp"), sem("route_done"), sem("route_moved")
        s_f2, s_f2e, s_wri = sem("spectrum"), sem("spectrum_evacuated"), sem("spectrum_weights")
        s_ya, s_yb, s_y = sem("weighted_a"), sem("weighted_b"), sem("weighted")
        s_i2, s_i2e = sem("columns_inverse"), sem("columns_inverse_evacuated")
        s_sw, s_xw, s_o1, s_o1e = sem("spatial_weight"), sem("spatially_weighted"), sem("filtered"), sem("filtered_evacuated")
        s_p2 = sem("pw2")
        ya = [words(z_base + 512 * j, 512) for j in range(2)]
        yb = [words(z_base + 1024 + 512 * j, 512) for j in range(2)]
        y_w = [words(z_base + 2048 + 512 * j, 512) for j in range(2)]
        spec = [words(z_base + 3072 + 1024 * j, 1024).rearrange("p (a c) -> p a c", a=2) for j in range(2)]

        o = L
        Zc2 = words(z_base, HALVES * COLS).rearrange("p (i q) -> p i q", q=PIX)
        rden = words(z_base + HALVES * COLS, 1024)
        qkvw = words(o, 2 * 768).rearrange("p (k c) -> p k c", k=2)
        num_s = [words(at, BANK) for at in (o, o + BANK)]; o += 1536
        num_s1 = num_s + [words(z_base + BANK * j, BANK) for j in range(6)]
        pwm = words(o, 768).rearrange("p (t m) -> p t m", t=QKV_TILES); o += 768
        pwt_at = [o + sum(TENSOR_TAPS[:t]) * P for t in range(QKV_TILES - 1)] + [z_base + 3 * PIX]
        pwt = [words(pwt_at[t], TENSOR_TAPS[t] * P).rearrange("p (a m) -> p a m", m=P) for t in range(QKV_TILES)]
        o += sum(TENSOR_TAPS[:-1]) * P
        projw = words(o, 1024).rearrange("p (k c) -> p k c", k=4); o += 1024
        head_cols = words(o, 32); o += 32
        head_rows = words(o, P); o += P
        vkm = words(o, 1024).rearrange("p (s b g m) -> p s b g m", s=2, b=B, g=2); o += 1024
        denw = words(o, 256).rearrange("p (s b g m) -> p s b g m", s=2, b=B, g=2); o += 256
        turned = [words(o + 512 * j, 512) for j in range(2)]
        proj_s = turned; o += 1024
        padq_at = o
        padq = words(o, QKV_TILES * B * QROW * QROW).rearrange("p (t b y x) -> p t b y x", t=QKV_TILES, b=B, y=QROW); o += QKV_TILES * B * QROW * QROW
        flat = [words(o + COLS * t, COLS) for t in range(QKV_TILES)]; o += QKV_TILES * COLS
        tile_pad = B * QROW * QROW
        local = [words(o, COLS), flat[0], words(o + COLS, COLS), flat[1], words(o + 2 * COLS, COLS),
                 words(padq_at, COLS)]; o += 3 * COLS
        att = [flat[2], flat[3], words(padq_at + 2 * tile_pad, COLS), words(padq_at + 3 * tile_pad, COLS)]
        kacc = small[:, 370:386].rearrange("p (s g c) -> p s g c", s=2, g=2)
        ksum = small[:, 386:394].rearrange("p (s g b) -> p s g b", s=2, g=2)
        bnv, bnsd, bn_inv, bnt, bn_off = (small[:, 394 + 6 * j:400 + 6 * j] for j in range(5))
        s_w2, s_w2b, s_bnv, s_bnsd, s_bn = sem("l2_weights_loaded"), sem("l2_late_weights"), sem("bn_var"), sem("bn_sd"), sem("bn_ready")
        s_qb, s_qkv, s_qp, s_qf = sem("qkv_border_zero"), sem("qkv"), sem("qkv_padded"), sem("qkv_flat")
        s_dnw = sem("denominator_weights")
        s_pwm, s_pwt = sem("pointwise_ready"), sem("late_tap_weights")
        s_tr, s_trc, s_vk, s_vkm = sem("kv_turned"), sem("kv_turned_copied"), sem("vk"), sem("vk_masked")
        s_den, s_rc, s_num, s_rb, s_ns, s_att = (sem("denominators"), sem("denominators_inverted"), sem("numerators"),
                                                 sem("inverse_spread"), sem("numerators_copied"), sem("attended"))
        s_dwd, s_yq, s_yqe = sem("filtered_by_dve"), sem("local_qkv"), sem("local_qkv_copied")
        s_pj, s_pje = sem("proj"), sem("proj_scaled")
        Q_ORDER = [0, 4, 1, 2, 3, 5]
        Y_ORDER = [0, 2, 4, 1, 3, 5]
        y_bank = [0, 0, 0, 0, 4, 0]
        local_free = [0, 4, 8, 12, 16, 16]
        ATTEND_ORDER = [(b, c, gr) for b in range(B) for c in range(2) for gr in range(2)]
        POOL_TILES = [4, 5]
        DVE_TILES = [0, 2, 1, 3]

        pool_taps = [(t, a, b) for t in POOL_TILES for a in range(TENSOR_TAPS[t], K5) for b in range(B)]
        early_tmp = [local[2][:, 0:PIX], local[2][:, PIX:COLS], rden]
        late_tmp = [Zc2[:, j, :] for j in range(3)]

        def tap_tmp(n):
            return (early_tmp if n < EARLY_PRODUCTS else late_tmp)[n % 3]

        s_tp = sem("tap_product")
        s_ta = sem("tap_product_added")

        def tap_view(t, a, b):
            dy, dx = divmod(a, 5)
            return padq[:, t, b, dy:dy + H, dx:dx + W]

        def filter_tap(eng, step, t, a):
            for b in range(B):
                dst = local[t][:, b * PIX:(b + 1) * PIX].rearrange("p (y x) -> p y x", y=H)
                wt = col("dw2_w", t * K5 + a)
                if a == TENSOR_TAPS[t]:
                    ins = eng.tensor_scalar(dst, tap_view(t, a, b), wt, None, ALU.mult)
                else:
                    ins = eng.scalar_tensor_tensor(dst, tap_view(t, a, b), wt, dst, ALU.mult, ALU.add)
                if a == K5 - 1:
                    ins.then_inc(s_dwd, 1)
                    n = step.n
                else:
                    n = step.add(ins)
            return n

        o = L
        pw3w = words(o, 512).rearrange("p (k c) -> p k c", k=2); o += 512
        tap3 = words(o, 9 * P).rearrange("p (a m) -> p a m", a=9); o += 9 * P
        h3 = words(o, HALVES * COLS).rearrange("p (i q) -> p i q", q=PIX); o += HALVES * COLS
        o3 = words(o, HALVES * COLS).rearrange("p (i q) -> p i q", q=PIX); o += HALVES * COLS
        pk = small[:, 424:440].rearrange("p (a i) -> p a i", a=4)
        tap3_tmp = [words(o + 1024 * j, 1024) for j in range(2)]; o += 2048
        s_tp3 = sem("l3_tap_product")
        s_w3, s_d3, s_dw3, s_dw3p, s_h3 = sem("l3_weights_loaded"), sem("l3_taps_ready"), sem("l3_dw_by_dve"), sem("l3_dw_by_pool"), sem("l3_hidden")
        s_dw3t, s_kept, s_pw3, s_o3 = sem("l3_dw_by_tensor"), sem("l3_pruned"), sem("l3_pointwise"), sem("l3_result")

        def filter3(eng, step, i, tap, last):
            dy, dx = divmod(tap, 3)
            src = Z[:, i, PAD - 1 + dy:PAD - 1 + dy + H, PAD - 1 + dx:PAD - 1 + dx + W]
            dst = h3[:, i, :].rearrange("p (y x) -> p y x", y=H)
            wt = col("dw3_w", i // 2 * 9 + tap)
            if tap == 0:
                ins = eng.tensor_scalar(dst, src, wt, None, ALU.mult)
            else:
                ins = eng.scalar_tensor_tensor(dst, src, wt, dst, ALU.mult, ALU.add)
            if tap < 8:
                return step.add(ins)
            ins.then_inc(last, 1)
            return step.n

        DISP = [(i, j) for j in range(ND) for i in range(ND)]
        ORDER = [2, 1, 3, 0, 4]
        plan = []
        for hf in range(HALVES):
            for a, j in enumerate(ORDER):
                for i in range(ND):
                    plan.append((hf, j, i))
        by_pool = [n >= POOL_FROM and n % 3 == 1 for n in range(len(plan))]
        last_of_half = [len(plan) // 2 - 1, len(plan) - 1]
        for n in last_of_half:
            by_pool[n] = True
        upto_dve = np.cumsum([not b for b in by_pool]).tolist()
        upto_pool = np.cumsum(by_pool).tolist()

        def shifted(hf, j, i):
            src = XSc[:, i:i + XX, hf * P:(hf + 1) * P] if j == 2 else XSd[:, j - (j > 2), i:i + XX, :]
            return src.rearrange("p x (g c) -> p x g c", c=CG)

        def product(eng, n):
            hf, j, i = plan[n]
            weight = Wds[hf][:, i, j, :].rearrange("p (x g) -> p x g", g=GH).unsqueeze(3).to_broadcast([P, XX, GH, CG])
            return eng.tensor_tensor(prods[n % NB].rearrange("p (x g c) -> p x g c", g=GH, c=CG),
                                     shifted(hf, j, i), weight, ALU.mult)

        def await_product_inputs(eng, n):
            hf, j, i = plan[n]
            eng.wait_ge(s_wd[hf], (2, 1)[hf])
            if j == 2:
                eng.wait_ge(s_halo, 32)
            else:
                eng.wait_ge(s_shift[j - (j > 2)], 32 * (hf + 1))
            if n >= NB:
                eng.wait_ge(s_acc, n - NB + 1)

        gen_x, gen_y, gen_hy, gen_w = (words(wd_at + NPT * j, NPT).rearrange("p (k g) -> p k g", k=K2) for j in range(4))
        gen_src, gen_acc = prods[0], prods[1]
        gen_tmp = gen_src[:, 0:NPT].rearrange("p (k g) -> p k g", k=K2)
        gen_dy, gen_dx = small[:, 440:441], small[:, 441:442]

        def restart(pool):
            pool.dma_reset(range(s_gen.num, s_gen.num + 1))
            pool.sem_clear(s_gen)

        def hat(me, g, out_, at, centre):
            me.link(g.tensor_scalar(out_, at, centre, None, ALU.subtract))
            me.link(g.tensor_scalar(gen_tmp, out_, 0.0, None, ALU.max))
            me.link(g.tensor_scalar(out_, out_, 0.0, None, ALU.min))
            me.link(g.tensor_tensor(out_, out_, gen_tmp, ALU.subtract))
            me.link(g.tensor_scalar(out_, out_, 1.0, 0.0, ALU.add, ALU.max))

        def general_path(pool, g, any_beyond):
            with pool.If(any_beyond > 0):
                me = Steps(pool, s_gstep)
                me.link(g.memset(gen_acc, 0.0))
                blank = xpad_dram.rearrange("b y x c -> (b y x c)").rearrange("(n p q) -> n p q", p=P, q=XX * P)
                for n in range(blank.shape[0]):
                    g.dma_start(blank[n], gen_acc).then_inc(s_gen, 16)
                    pool.wait_ge(s_gen, 16 * (n + 1))
                for b in range(B):
                    for s_ in range(2):
                        rows = XSc[b * 64 + s_:(b + 1) * 64:2, PAD:PAD + XX, :]
                        g.dma_start(xpad_dram[b, REACH:REACH + H, REACH + XX * s_:REACH + XX * (s_ + 1), :], rows).then_inc(s_gen, 16)
                        pool.wait_ge(s_gen, 16 * (blank.shape[0] + 1 + 2 * b + s_))
                restart(pool)
                pool.sem_clear(s_gstep)
                offs = OM[:, :, 0:2 * G * K2].rearrange("p x (h g k a) -> p h a k x g", h=2, g=GH, k=K2)
                for hf in range(HALVES):
                    me = Steps(pool, s_gstep)
                    for k in range(K2):
                        for a_, dst in ((0, gen_x), (1, gen_y)):
                            shift = float((k // 3, k % 3)[a_] - 1)
                            me.add(g.tensor_scalar(dst[:, k].rearrange("p (x g) -> p x g", g=GH), offs[:, hf, a_, k], shift, None, ALU.add))
                    me.add(g.memset(gen_acc, 0.0))
                    me.link(g.memset(gen_dy, -float(REACH)))
                    pool.sem_clear(s_gstep)
                    with pool.Fori(0, 2 * REACH) as i:
                        me = Steps(pool, s_gstep)
                        hat(me, g, gen_hy, gen_y, gen_dy)
                        me.link(g.tensor_tensor(gen_hy, gen_hy, mask[:, hf], ALU.mult))
                        me.add(g.tensor_scalar(gen_dy, gen_dy, 1.0, None, ALU.add))
                        me.link(g.memset(gen_dx, -float(REACH)))
                        pool.sem_clear(s_gstep)
                        with pool.Fori(0, 2 * REACH) as j:
                            me = Steps(pool, s_gstep)
                            hat(me, g, gen_w, gen_x, gen_dx)
                            me.link(g.tensor_tensor(gen_w, gen_w, gen_hy, ALU.mult))
                            me.add(g.tensor_scalar(gen_dx, gen_dx, 1.0, None, ALU.add))
                            for k in range(1, K2):
                                me.link(g.tensor_tensor(gen_w[:, 0], gen_w[:, 0], gen_w[:, k], ALU.add))
                            for b in range(B):
                                for s_ in range(2):
                                    src = xpad_dram[b, bass.ds(i, H), bass.ds(j + XX * s_, XX), hf * P:(hf + 1) * P]
                                    dst = gen_src.rearrange("p (x c) -> p x c", c=P)[b * 64 + s_:(b + 1) * 64:2]
                                    g.dma_start(dst, src).then_inc(s_gen, 16)
                                    pool.wait_ge(s_gen, 16 * (2 * b + s_ + 1))
                            weight = gen_w[:, 0].rearrange("p (x g) -> p x g", g=GH).unsqueeze(3).to_broadcast([P, XX, GH, CG])
                            term = gen_src.rearrange("p (x g c) -> p x g c", g=GH, c=CG)
                            me.link(g.tensor_tensor(term, term, weight, ALU.mult))
                            me.link(g.tensor_tensor(gen_acc, gen_acc, gen_src, ALU.add))
                            restart(pool)
                            pool.sem_clear(s_gstep)
                    g.dma_start(general_dram[hf], gen_acc).then_inc(s_gen, 16)
                    pool.wait_ge(s_gen, 16)
                    restart(pool)

        def add_general(pool, g, any_beyond, n):
            with pool.If(any_beyond > 0):
                g.dma_start(prods[n % NB], general_dram[plan[n][0]], accum_op=ALU.add).then_inc(s_gen, 16)
                pool.wait_ge(s_gen, 16)
                restart(pool)

        block = ctx.enter_context(nc.Block())

        @block.sync
        def _(sp):
            for i in range(4):
                h, b = divmod(i, 2)
                sp.dma_start(X[:, h, b, :], x_in[b, h * P:(h + 1) * P]).then_inc(s_x, 16)
            sp.dma_start(cv, w["chan_vecs"]).then_inc(s_const, 16)
            sp.dma_start(ident, w["ident"]).then_inc(s_const, 16)
            sp.dma_start(gmean, w["gmean"]).then_inc(s_const, 16)
            sp.dma_start(head_mask, w["head_mask"]).then_inc(s_const, 16)
            sp.dma_start(small[:, 96:103], w["small_consts"]).then_inc(s_const, 16)
            sp.dma_start(inw, w["in_w"].rearrange("(k p) c -> p k c", p=P)).then_inc(s_w0, 16)
            sp.dma_start(inb, w["in_b"].partition_broadcast(P)).then_inc(s_w0, 16)
            sp.dma_start(omw[:, :, 0:2 * G * K2], w["off_w"].rearrange("(k p) c -> p k c", p=P)).then_inc(s_w0, 16)
            sp.dma_start(omw[:, :, 2 * G * K2:], w["mask_w"].rearrange("(k p) c -> p k c", p=P)).then_inc(s_w0, 16)
            sp.dma_start(omb[:, 0:2 * G * K2], w["off_b"].partition_broadcast(P)).then_inc(s_w0, 16)
            sp.dma_start(omb[:, 2 * G * K2:], w["mask_b"].partition_broadcast(P)).then_inc(s_w0, 16)
            sp.dma_start(outw, w["out_w"].rearrange("(k p) c -> p k c", p=P)).then_inc(s_w0, 16)
            sp.wait_ge(s_xpe, 8)
            sp.wait_ge(s_shz, 2)
            sp.dma_start(XSc[1::2, 0:PAD], XSc[0::2, XX:XX + PAD]).then_inc(s_halo, 16)
            sp.dma_start(XSc[0::2, PAD + XX:], XSc[1::2, PAD:2 * PAD]).then_inc(s_halo, 16)
            sp.wait_ge(s_halo, 32)
            for hf in range(HALVES):
                for a, j in enumerate(ORDER[1:]):
                    if hf:
                        sp.wait_ge(s_acc, ND * (a + 2))
                    d = 2 * (j - 2)
                    for b in range(B):
                        lo, hi = b * 64 + max(0, -d), b * 64 + 64 - max(0, d)
                        sp.dma_start(XSd[lo:hi, j - (j > 2)], XSc[lo + d:hi + d, :, hf * P:(hf + 1) * P]).then_inc(s_shift[j - (j > 2)], 16)
            sp.wait_ge(s_x_new, 8)
            for dst, name in ((fc1w, "fc1_w"), (pw1w, "pw1_w")):
                sp.dma_start(dst, w[name].rearrange("(k p) c -> p k c", p=P)).then_inc(s_w1, 16)
            sp.dma_start(convw, w["conv_w"]).then_inc(s_w1, 16)
            sp.dma_start(dft, w["dft"]).then_inc(s_w1, 16)
            sp.dma_start(craw, w["spectra"]).then_inc(s_craw, 16)
            sp.dma_start(ccoef, w["spectra_coef"]).then_inc(s_craw, 16)
            sp.dma_start(sp1w, w["sp1_w"].rearrange("(k p) t c -> p k t c", p=P)).then_inc(s_w1b, 16)
            sp.dma_start(spw, w["spatial_w"]).then_inc(s_w1b, 16)
            sp.dma_start(pw2w, w["pw2_w"].rearrange("(k p) c -> p k c", p=P)).then_inc(s_w1b, 16)
            for c in range(3):
                sp.dma_start(stream[c], w["fc2_w"][c]).then_inc(s_str[c], 16)
            for b in range(B):
                for t in range(WT):
                    sp.wait_ge(s_f1e, WT * b + t + 1)
                    sp.dma_start(w["bounce"][0, b, :, t, :], U[b][:, t, :]).then_inc(s_uo[b], 16)
            for b in range(B):
                sp.wait_ge(s_uo[b], 16 * WT)
                if b == 0:
                    sp.wait_ge(s_pw1, TILES)
                for t in range(WT):
                    rows = w["bounce"][0, b].rearrange("s w c -> (s w) c")[t * P:(t + 1) * P, :]
                    sp.dma_start(V[b][:, t, :], rows).then_inc(s_vi[WT * b + t], 16)
            for c in range(3, 11):
                sp.wait_ge(s_fc2c, c - 2)
                dst, src = (stream[c % 3], w["fc2_w"][c]) if c < 10 else (stream[1][0:4, :], w["fc2_b"])
                sp.dma_start(dst, src).then_inc(s_str[c % 3], 16)
            sp.wait_ge(s_rd, 1)
            for r_ in range(4):
                sp.dma_start(route[:, r_, :], route_sm[r_:r_ + 1, :]).then_inc(s_rt, 16)
            for b in range(B):
                for t in range(WT):
                    sp.wait_ge(s_i2e, WT * b + t + 1)
                    rows = w["bounce"][1, b].rearrange("s w c -> (s w) c")[t * P:(t + 1) * P, :]
                    sp.dma_start(rows, U[b][:, t, :]).then_inc(s_uo[b], 16)
                sp.wait_ge(s_uo[b], 32 * WT)
                for t in range(WT):
                    sp.dma_start(V[b][:, t, :], w["bounce"][1, b, :, t, :]).then_inc(s_vi[WT * b + t], 16)
            if LAST >= 2:
                sp.wait_ge(s_x_new, 16)
                sp.dma_start(qkvw, w["qkv_w"].rearrange("(k p) c -> p k c", p=P)).then_inc(s_w2, 16)
                sp.dma_start(pwm.rearrange("p t m -> p (t m)"), w["pointwise_w"]).then_inc(s_w2b, 16)
                sp.dma_start(projw, w["proj_w"].rearrange("(k p) c -> p k c", p=P)).then_inc(s_w2b, 16)
                sp.dma_start(head_cols, w["head_cols"]).then_inc(s_w2b, 16)
                sp.dma_start(head_rows, w["head_rows"]).then_inc(s_w2b, 16)
            if LAST >= 3:
                sp.wait_ge(s_x_new, 24)
                sp.dma_start(pw3w, w["pw3_w"].rearrange("(k p) c -> p k c", p=P)).then_inc(s_w3, 16)
            for n, i in enumerate((0, 2, 1, 3)):
                h, b = divmod(i, 2)
                sp.wait_ge(s_x_new, 8 * (LAST + 1) if LAST < 3 else 24 + n + 1)
                sp.dma_start(out[b, h * P:(h + 1) * P], X[:, h, b, :]).then_inc(s_out, 16)
            sp.wait_ge(s_out, 64)

        @block.tensor
        def _(pe):
            def group_means(layer):
                pe.wait_ge(s_gn_stats, layer + 1)
                pe.matmul(psum[:, 7, 0:8], gmean, small[:, 56:64], start=True, stop=True).then_inc(s_gn_means, 1)

            pe.wait_ge(s_const, 80)
            group_means(0)
            pe.wait_ge(s_zc, 4)
            pe.wait_ge(s_w0, 112)
            for n in range(8):
                for u in range(2):
                    for k in range(HALVES):
                        lhs = Zc[:, 2 * k:2 * k + 2, :].rearrange("p b q -> p (b q)")[:, 2 * n + u::XX]
                        m = pe.matmul(psum[:, n, u * C:(u + 1) * C], lhs, inw[:, k], start=(k == 0 and u == 0),
                                      stop=(k == 1), skip_group_check=True)
                m.then_inc(s_xp, 1)
            for t in range(8):
                if t == 0:
                    pe.wait_ge(s_x1, 2)
                    pe.wait_ge(s_xpe, 8)
                for u in range(2):
                    for k in range(HALVES):
                        m = pe.transpose(psum[:, t, u * C + k * P:u * C + (k + 1) * P],
                                         x1cm[:, k, 2 * t + u::XX], ident)
                m.then_inc(s_x1t, 1)
            for t in range(8):
                q, k = divmod(t, 2)
                pe.wait_ge(s_x1n, 4 * (q + 1))
                for u in range(4):
                    m = pe.transpose(psum[:, t, u * P:(u + 1) * P], x1n[:, 4 * q + u, k * P:(k + 1) * P], ident)
                m.then_inc(s_back, 1)
            for t in range(XX):
                pe.wait_ge(s_g1, max(2 * (t // 4 + 1), t % 8 + 1))
                if t >= 8:
                    pe.wait_ge(s_ome, t - 7)
                for k in range(HALVES):
                    m = pe.matmul(psum[:, t % 8, 0:NOM], g1cm[:, k, t, :], omw[:, k], start=(k == 0), stop=(k == 1))
                m.then_inc(s_om, 1)
            pe.wait_ge(s_ome, XX)
            opened = set()
            for n in range(9):
                ky, kx = divmod(n, 3)
                pe.wait_ge(s_wk, n + 1)
                for i in range(3):
                    for j in range(3):
                        bank, at = divmod((kx + i) * ND + ky + j, 4)
                        m = pe.matmul(psum[:, bank, at * XG:(at + 1) * XG], ident, wk[n % 2][:, (3 * i + j) * XG:(3 * i + j + 1) * XG],
                                      start=(bank not in opened), stop=(n == 8), skip_group_check=True)
                        opened.add(bank)
                m.then_inc(s_wka, 1)
            pe.wait_ge(s_wd[0], 2)
            for n, (hf, j, i) in enumerate(plan):
                first, last = n % (ND * ND) == 0, n % (ND * ND) == ND * ND - 1
                if by_pool[n]:
                    pe.wait_ge(s_pp, upto_pool[n])
                else:
                    pe.wait_ge(s_pd, upto_dve[n])
                for xx in range(XX):
                    m = pe.matmul(psum[:, 4 * hf + xx // 4, xx % 4 * P:(xx % 4 + 1) * P], prods[n % NB][:, xx * P:(xx + 1) * P],
                                  ident, start=(first and xx % 4 == 0), stop=last, is_transpose=True, skip_group_check=True)
                m.then_inc(s_acc, 1)
            pe.wait_ge(s_outT, 8)
            for t in range(8):
                q, mh = divmod(t, 2)
                for k in range(HALVES):
                    m = pe.matmul(psum[:, t, :], outw[:, k, mh * P:(mh + 1) * P],
                                  outT[:, k, 4 * q:4 * q + 4, :], start=(k == 0), stop=(k == 1))
                m.then_inc(s_op, 1)

            if LAST < 1:
                return
            group_means(1)
            pe.wait_ge(s_zc, 8)
            pe.wait_ge(s_w1, 64)
            z2 = Zc1.rearrange("p (k b) q -> p k (b q)", k=2)
            for c in range(CHUNKS):
                for k in range(HALVES):
                    m = pe.matmul(psum[:, c, :], fc1w[:, k], z2[:, k, c * BANK:(c + 1) * BANK], start=(k == 0), stop=(k == 1))
                m.then_inc(s_fc1, 1)
            for c in range(CHUNKS):
                pe.wait_ge(s_fc1r, c + 1)
                pe.matmul(psum[:, 4 + c, :], convw, sr_act[:, c * BANK:(c + 1) * BANK], start=True, stop=True).then_inc(s_cv, 1)
            for i in range(TILES + 3):
                if i < TILES:
                    if i < 4:
                        pe.wait_ge(s_fc1r, i + 1)
                    else:
                        pe.wait_ge(s_pw1r, i - 3)
                    b, t = divmod(i, WT)
                    for k in range(HALVES):
                        m = pe.matmul(psum[:, i % 4, :], Zc1[:, 2 * k + b, t::WT], pw1w[:, k], start=(k == 0), stop=(k == 1))
                    m.then_inc(s_pw1, 1)
                if i >= 3:
                    n = i - 3
                    pe.wait_ge(s_xpd, n + 1)
                    if n < 4:
                        pe.wait_ge(s_cvr, 4)
                    else:
                        pe.wait_ge(s_f1e, n - 3)
                    pe.matmul(psum[:, 4 + n % 4, :], dft[:, 0], xp[:, n, :], start=True, stop=True).then_inc(s_f1, 1)
            pe.wait_ge(s_z, 8)
            pe.wait_ge(s_zb, 2)
            pe.wait_ge(s_w1b, 48)
            pe.wait_ge(s_pw1r, TILES)
            for c in range(CHUNKS):
                b, yh = divmod(c, 2)
                for k in range(HALVES):
                    for tap in range(9):
                        dy, dx = divmod(tap, 3)
                        y0 = PAD - 1 + dy + 16 * yh
                        m = pe.matmul(psum[:, c, :], sp1w[:, k, tap], Z[:, 2 * k + b, y0:y0 + 16, PAD - 1 + dx:PAD - 1 + dx + W],
                                      start=(k == 0 and tap == 0), stop=(k == 1 and tap == 8))
                m.then_inc(s_sp, 1)
            for c in range(10):
                pe.wait_ge(s_str[c % 3], 16 * (c // 3 + 1))
                if c == 0:
                    pe.wait_ge(s_rmean, 1)
                    pe.wait_ge(s_f1e, TILES)
                if c == 1:
                    pe.wait_ge(s_u, 1)
                for f in range(4):
                    m = pe.matmul(psum[0:4, 4 + f, :], rmean if c == 0 else lhs_u[:, c - 1, :],
                                  stream[c % 3][:, f * BANK:(f + 1) * BANK], start=(c == 0), stop=(c == 9))
                m.then_inc(s_fc2c, 1)
            for i in range(TILES + 1):
                if i < TILES:
                    b, t = divmod(i, WT)
                    sel = 1 if t == 0 else 2
                    pe.wait_ge(s_vi[i], 16)
                    if i == 0:
                        pe.wait_ge(s_spr, 4)
                    if i >= 2:
                        pe.wait_ge(s_f2e, i - 1)
                    pe.matmul(psum[:, 2 * (i % 2), :], dft[:, sel], V[b][:, t, :], start=True, stop=True)
                    pe.matmul(psum[:, 2 * (i % 2) + 1, :], dft[:, sel + 2], V[b][:, t, :], start=True, stop=True).then_inc(s_f2, 1)
                    if i == 0:
                        pe.wait_ge(s_rt, 64)
                        pe.wait_ge(s_cwe, 1)
                    else:
                        pe.wait_ge(s_ya, i)
                        pe.wait_ge(s_yb, i)
                    pe.matmul(psum[:, 4, :], cwe[:, 0, t * P:(t + 1) * P], route[:, b, :], start=True, stop=True)
                    pe.matmul(psum[:, 5, :], cwe[:, 1, t * P:(t + 1) * P], route[:, b, :], start=True, stop=True).then_inc(s_wri, 1)
                if i >= 1:
                    n = i - 1
                    pe.wait_ge(s_y, n + 1)
                    if n >= 2:
                        pe.wait_ge(s_i2e, n - 1)
                    pe.matmul(psum[:, 6 + n % 2, :], dft[:, 5 if n % WT == 0 else 6], y_w[n % 2], start=True, stop=True).then_inc(s_i2, 1)
            for i in range(TILES + 1):
                if i < TILES:
                    b, t = divmod(i, WT)
                    if i == 0:
                        pe.wait_ge(s_f2e, TILES)
                    if i >= 2:
                        pe.wait_ge(s_xw, i - 1)
                    pe.matmul(psum[:, i % 2, :], spw[:, t * P:(t + 1) * P], route[:, 2 + b, :], start=True, stop=True).then_inc(s_sw, 1)
                if i >= 1:
                    n = i - 1
                    b, t = divmod(n, WT)
                    pe.wait_ge(s_vi[n], 32)
                    pe.wait_ge(s_xw, n + 1)
                    if n < 2:
                        pe.wait_ge(s_yb, TILES)
                    else:
                        pe.wait_ge(s_o1e, n - 1)
                    for k in range(KM):
                        pe.matmul(psum[:, 2 + n % 2, k * P:(k + 1) * P], V[b][:, t, k * P:(k + 1) * P], dft[:, 7],
                                  start=(k == 0), stop=False, skip_group_check=True)
                    for k in range(KM):
                        m = pe.matmul(psum[:, 2 + n % 2, k * P:(k + 1) * P], xp[:, n, k * P:(k + 1) * P], ident,
                                      start=False, stop=True, is_transpose=True, skip_group_check=True)
                    m.then_inc(s_o1, 1)
                    if n % 4 == 3:
                        pe.wait_ge(s_o1e, n + 1)
                        pe.wait_ge(s_i2e, TILES)
                        for mh in range(HALVES):
                            j = n // 4 * 2 + mh
                            if j >= 4:
                                pe.wait_ge(s_x_new, 8 + j - 3)
                            for k in range(KM):
                                m = pe.matmul(psum[:, 4 + j % 4, :], pw2w[:, k, mh * P:(mh + 1) * P],
                                              OT[b][:, k, t - 3:t + 1, :], start=(k == 0), stop=(k == KM - 1))
                            m.then_inc(s_p2, 1)

            if LAST < 2:
                return
            group_means(2)
            pe.wait_ge(s_zc, 12)
            pe.wait_ge(s_w2, 16)
            z2 = Zc2.rearrange("p (k b) q -> p k (b q)", k=2)
            for i in range(QKV_TILES * CHUNKS):
                t, c = Q_ORDER[i // CHUNKS], i % CHUNKS
                if i >= 4:
                    pe.wait_ge(s_qp, i - 3)
                    pe.wait_ge(s_qf, i - 3)
                for k in range(HALVES):
                    m = pe.matmul(psum[:, i % 4, :], qkvw[:, k, t * P:(t + 1) * P], z2[:, k, c * BANK:(c + 1) * BANK],
                                  start=(k == 0), stop=(k == 1))
                m.then_inc(s_qkv, 1)

            def key_value_products(src, tiles):
                for i in range(TILES + 1):
                    if i < TILES:
                        b, t = divmod(i, WT)
                        n = src * TILES + i
                        if n >= 2:
                            pe.wait_ge(s_trc, n - 1)
                        for u in range(4):
                            m = pe.transpose(psum[:, 4 + n % 2, u * P:(u + 1) * P], tiles[u][:, i * P:(i + 1) * P], ident)
                        m.then_inc(s_tr, 1)
                    if i >= 1:
                        b, t = divmod(i - 1, WT)
                        n = src * TILES + i - 1
                        pe.wait_ge(s_trc, n + 1)
                        if src and t == 0:
                            pe.wait_ge(s_vkm, 2)
                        for gr in range(2):
                            tk, tv = 2 * gr, 2 * gr + 1
                            m = pe.matmul(psum[:, 6 + b, gr * P:(gr + 1) * P], turned[n % 2][:, tk * P:(tk + 1) * P],
                                          turned[n % 2][:, tv * P:(tv + 1) * P], start=(t == 0 and gr == 0), stop=(t == WT - 1),
                                          skip_group_check=True)
                        m.then_inc(s_vk, 1)

            def denominators(src, queries):
                pe.wait_ge(s_dnw, src + 1)
                for c in range(2):
                    for b in range(B):
                        for gr in range(2):
                            j = 2 * gr + b
                            m = pe.matmul(psum[32 * j:32 * j + 32, c, :], denw[:, src, b, gr, :],
                                          queries[gr][:, b * PIX + c * BANK:b * PIX + (c + 1) * BANK], start=True, stop=True)
                    m.then_inc(s_den, 1)

            def numerator(src, queries, s_):
                b, c, gr = ATTEND_ORDER[s_]
                n = 8 * src + s_
                if n >= 2:
                    pe.wait_ge(s_ns, n - 1)
                pe.matmul(psum[:, 2 + n % 2, :], vkm[:, src, b, gr, :], queries[gr][:, b * PIX + c * BANK:b * PIX + (c + 1) * BANK],
                          start=True, stop=True).then_inc(s_num, 1)

            def spread(src, s_):
                b, c, gr = ATTEND_ORDER[s_]
                n, j = 8 * src + s_, 2 * gr + b
                if s_ == 0:
                    pe.wait_ge(s_rc, src + 1)
                if n >= 2:
                    pe.wait_ge(s_att, n - 1)
                pe.matmul(psum[:, 4 + n % 2, :], head_rows[32 * j:32 * j + 32, :],
                          rden[32 * j:32 * j + 32, c * BANK:(c + 1) * BANK], start=True, stop=True).then_inc(s_rb, 1)

            def local_taps(a):
                t = Y_ORDER[a]
                if t == QKV_TILES - 1:
                    pe.wait_ge(s_pwt, 1)
                for c in range(CHUNKS):
                    if a:
                        pe.wait_ge(s_yqe, min(4 * a + c - 3, local_free[a]))
                    else:
                        pe.wait_ge(s_pwm, 1)
                    b, yh = divmod(c, 2)
                    for tap in range(TENSOR_TAPS[t]):
                        dy, dx = divmod(tap, 5)
                        pe.matmul(psum[:, y_bank[a] + c, :], pwt[t][:, tap, :], padq[:, t, b, dy + 16 * yh:dy + 16 * yh + 16, dx:dx + W],
                                  start=(tap == 0), stop=False)

            def local_rest(a):
                t = Y_ORDER[a]
                if t in POOL_TILES:
                    pe.wait_ge(s_ta, len([p for p in pool_taps if p[0] <= t]))
                else:
                    pe.wait_ge(s_dwd, 2 * (DVE_TILES.index(t) + 1))
                for c in range(CHUNKS):
                    pe.matmul(psum[:, y_bank[a] + c, :], pwm[:, t, :], local[t][:, c * BANK:(c + 1) * BANK],
                              start=False, stop=True).then_inc(s_yq, 1)

            pe.wait_ge(s_qf, 24)
            pe.wait_ge(s_qp, 24)
            key_value_products(0, flat[0:4])
            pe.wait_ge(s_w2b, 64)
            local_taps(0)
            local_rest(0)
            pe.wait_ge(s_yqe, 4)
            denominators(0, flat[4:6])
            pe.wait_ge(s_vkm, 2)
            for s_ in range(8):
                numerator(0, flat[4:6], s_)
                spread(0, s_)
            pe.wait_ge(s_ns, 8)
            for a in range(1, 4):
                local_taps(a)
                local_rest(a)
            pe.wait_ge(s_att, 8)
            local_taps(4)
            local_taps(5)
            local_rest(4)
            local_rest(5)
            pe.wait_ge(s_yqe, 24)
            denominators(1, local[4:6])
            key_value_products(1, local[0:4])
            pe.wait_ge(s_vkm, 4)
            for s_ in range(8):
                numerator(1, local[4:6], s_)
            pe.wait_ge(s_ns, 16)
            for j in range(5):
                if j < 4:
                    for s_ in (2 * j, 2 * j + 1):
                        spread(1, s_)
                if j >= 1:
                    c = j - 1
                    pe.wait_ge(s_att, 8 + 2 * j)
                    for mh in range(HALVES):
                        i = 2 * c + mh
                        if i >= 4:
                            pe.wait_ge(s_pje, i - 3)
                        for k in range(4):
                            m = pe.matmul(psum[:, i % 4, :], projw[:, k, mh * P:(mh + 1) * P], att[k][:, c * BANK:(c + 1) * BANK],
                                          start=(k == 0), stop=(k == 3))
                        m.then_inc(s_pj, 1)
            if LAST < 3:
                return
            group_means(3)
            pe.wait_ge(s_z, 16 - 4)
            pe.wait_ge(s_zb, 3)
            pe.wait_ge(s_d3, 1)
            for c in range(2):
                for tap in range(9):
                    dy, dx = divmod(tap, 3)
                    y0 = PAD - 1 + dy + 16 * c
                    m = pe.matmul(psum[:, c, :], tap3[:, tap, :], Z[:, 3, y0:y0 + 16, PAD - 1 + dx:PAD - 1 + dx + W],
                                  start=(tap == 0), stop=(tap == 8))
            m.then_inc(s_dw3t, 1)
            pe.wait_ge(s_w3, 16)
            for b in range(B):
                pe.wait_ge(s_kept, 2 * (b + 1))
                for mh in range(HALVES):
                    for c in range(2):
                        for k in range(HALVES):
                            m = pe.matmul(psum[:, (2 + 4 * b + 2 * mh + c) % 8, :], pw3w[:, k, mh * P:(mh + 1) * P],
                                          h3[:, 2 * k + b, c * BANK:(c + 1) * BANK], start=(k == 0), stop=(k == 1))
                    m.then_inc(s_pw3, 1)

        @block.vector
        def _(dve):
            v = nc.vector
            me = Steps(dve, s_dve)

            def group_norm(layer):
                for i in range(4):
                    for c in range(2):
                        n = me.add(v.bn_stats(st[:, i, c, :], X.rearrange("p h b q -> p (h b) q")[:, i, c * BANK:(c + 1) * BANK]))
                me.upto(n)
                for i in range(4):
                    n = me.add(v.bn_aggr(mv[:, i, :], st[:, i, :, :]))
                me.upto(n)
                me.link(v.tensor_tensor(gq[:, 1, :], mv[:, :, 0], mv[:, :, 0], ALU.mult))
                me.link(v.tensor_tensor(gq[:, 1, :], gq[:, 1, :], mv[:, :, 1], ALU.add))
                v.tensor_copy(gq[:, 0, :], mv[:, :, 0]).then_inc(s_gn_stats, 1)
                dve.wait_ge(s_gn_means, layer + 1)
                me.link(v.tensor_copy(small[:, 64:72], psum[:, 7, 0:8]))
                me.link(v.tensor_tensor(gt, gm[:, 0, :], gm[:, 0, :], ALU.mult))
                me.link(v.tensor_tensor(gvar, gm[:, 1, :], gt, ALU.subtract))
                v.tensor_scalar(gvar, gvar, GN_EPS, None, ALU.add).then_inc(s_gn_var, 1)
                dve.wait_ge(s_gn_sd, layer + 1)
                me.link(v.reciprocal(grs, gsd))
                newton(grs, gvar, gt)
                me.link(v.tensor_tensor(gnb, gm[:, 0, :], grs, ALU.mult))
                v.tensor_scalar(gnb, gnb, -1.0, None, ALU.mult).then_inc(s_gn_coef, 1)
                dve.wait_ge(s_gn_coef, layer + 1)
                if layer == 2:
                    return
                for i in range(4):
                    v.tensor_scalar(z_inner(i), Xi[:, i], grs[:, i:i + 1], gnb[:, i:i + 1], ALU.mult, ALU.add).then_inc(s_z, 1)

            def newton(r, var, t):
                me.link(v.tensor_tensor(t, r, r, ALU.mult))
                me.link(v.tensor_tensor(t, t, var, ALU.mult))
                me.link(v.tensor_scalar(t, t, -0.5, 1.5, ALU.mult, ALU.add))
                me.link(v.tensor_tensor(r, r, t, ALU.mult))

            dve.wait_ge(s_x, 64)
            dve.wait_ge(s_const, 80)
            group_norm(0)
            v.tensor_scalar(bnv, col("bn_v", 0, 6), GN_EPS, None, ALU.add).then_inc(s_bnv, 1)
            dve.wait_ge(s_z, 4)
            dve.wait_ge(s_zb, 1)
            dve.wait_ge(s_w0, 112)
            dve.wait_ge(s_bnsd, 1)
            me.link(v.reciprocal(bn_inv, bnsd))
            newton(bn_inv, bnv, bnt)
            me.link(v.tensor_tensor(bn_inv, bn_inv, col("bn_g", 0, 6), ALU.mult))
            me.link(v.tensor_tensor(bn_off, col("bn_m", 0, 6), bn_inv, ALU.mult))
            me.link(v.tensor_tensor(bn_off, col("bn_b", 0, 6), bn_off, ALU.subtract))
            me.link(v.tensor_tensor(bnt[:, 0:4], col("l3_b", 0, 4), bn_inv[:, 2:6], ALU.mult))
            v.tensor_tensor(bn_off[:, 2:6], bn_off[:, 2:6], bnt[:, 0:4], ALU.add).then_inc(s_bn, 1)

            def depthwise3(k, acc, tap, wname, bname, last):
                dy, dx = divmod(tap, 3)
                for b in range(B):
                    src = Z[:, 2 * k + b, PAD - 1 + dy:PAD - 1 + dy + H, PAD - 1 + dx:PAD - 1 + dx + W]
                    dst = acc[:, k, b * PIX:(b + 1) * PIX].rearrange("p (y x) -> p y x", y=H)
                    wt = col(wname, k * 9 + tap)
                    if tap == 0:
                        ins = v.tensor_scalar(dst, src, wt, col(bname, k), ALU.mult, ALU.add)
                    else:
                        ins = v.scalar_tensor_tensor(dst, src, wt, dst, ALU.mult, ALU.add)
                    n = me.add(ins)
                return n

            def evacuate_xproj(n):
                dve.wait_ge(s_xp, n + 1)
                v.tensor_tensor(XSc[:, PAD + 2 * n:PAD + 2 * n + 2, :], psum[:, n, :].rearrange("p (x c) -> p x c", c=C),
                                inb.unsqueeze(1).to_broadcast([P, 2, C]), ALU.add).then_inc(s_xpe, 1)

            tap_done = [0, 0]
            for tap in range(DW_TAPS):
                for k in range(HALVES):
                    if tap:
                        me.upto(tap_done[k])
                    tap_done[k] = depthwise3(k, x1cm, tap, "dw0_w", "dw0_b", s_x1)
                if tap:
                    for n in range(2 * tap - 2, 2 * tap):
                        evacuate_xproj(n)
            for k in range(HALVES):
                me.upto(tap_done[k])
                dve.wait_ge(s_dwa, (8 - DW_TAPS) * (k + 1))
                v.tensor_tensor(x1cm[:, k], x1cm[:, k], x1_rest[:, k], ALU.add).then_inc(s_x1, 1)
            tiles = psum[:].rearrange("p t (u c) -> p (t u) c", c=C)
            for t in range(XX):
                dve.wait_ge(s_x1t, t // 2 + 1)
                n = me.add(v.bn_stats(ln_st[:, t, :], tiles[:, t, :]))
            me.upto(n)
            for t in range(XX):
                n = me.add(v.bn_aggr(ln_mv[:, t, :], ln_st[:, t, :]))
            me.upto(n)
            v.tensor_scalar(ln_var, ln_mv[:, :, 1], GN_EPS, None, ALU.add).then_inc(s_lnv, 1)
            dve.wait_ge(s_lnsd, 1)
            me.link(v.reciprocal(ln_rs, ln_sd))
            newton(ln_rs, ln_var, ln_t)
            me.link(v.tensor_tensor(ln_nb, ln_mv[:, :, 0], ln_rs, ALU.mult))
            me.link(v.tensor_scalar(ln_nb, ln_nb, -1.0, None, ALU.mult))
            for t in range(XX):
                v.tensor_scalar(x1n[:, t, :], tiles[:, t, :], ln_rs[:, t:t + 1], ln_nb[:, t:t + 1],
                                ALU.mult, ALU.add).then_inc(s_x1n, 1)
            for t in range(XX):
                dve.wait_ge(s_om, t + 1)
                v.tensor_tensor(OM[:, t, :], psum[:, t % 8, 0:NOM], omb, ALU.add).then_inc(s_ome, 1)
            dve.wait_ge(s_ome, XX)
            logits = OM[:, :, 2 * G * K2:].rearrange("p x (h g k) -> p h x g k", h=2, k=K2)
            for hf in range(2):
                n = me.add(v.tensor_reduce(sm_t[:, hf].rearrange("p (x g) -> p x g", g=GH), logits[:, hf], AX.X, ALU.max))
            me.upto(n)
            for hf in range(2):
                v.tensor_tensor(mask[:, hf].rearrange("p k (x g) -> p k x g", g=GH), logits[:, hf].rearrange("p x g k -> p k x g"),
                                sm_t[:, hf].rearrange("p (x g) -> p x g", g=GH).unsqueeze(1).to_broadcast([P, K2, XX, GH]),
                                ALU.subtract).then_inc(s_lgs, 1)
            v.tensor_reduce(amax, OM[:, :, 0:2 * G * K2], AX.XY, ALU.max, apply_absolute_value=True).then_inc(s_amax, 1)
            for hf in range(2):
                dve.wait_ge(s_exp, hf + 1)
                me.link(v.tensor_reduce(sm_r[:, hf], mask[:, hf].rearrange("p k g -> p g k"), AX.X, ALU.add))
                me.link(v.reciprocal(sm_t[:, hf], sm_r[:, hf]))
                v.tensor_tensor(mask[:, hf], mask[:, hf], sm_t[:, hf].unsqueeze(1).to_broadcast([P, K2, XG]), ALU.mult).then_inc(s_mask, 1)
            dve.wait_ge(s_mask, 2)

            dve.wait_ge(s_hat[0], 1)
            dve.wait_ge(s_general, 1)
            for ky in range(3):
                n = me.add(v.scalar_tensor_tensor(hats[:, 3 + ky], hats[:, 3 + ky], within, mask[:, 0], ALU.mult, ALU.mult))
            me.upto(n)
            for n in range(9):
                ky, kx = divmod(n, 3)
                if n >= 2:
                    dve.wait_ge(s_wka, n - 1)
                v.tensor_tensor(wk[n % 2], hats[:, 3 + ky].rearrange("p k g -> p (k g)"),
                                hats[:, kx].rearrange("p k g -> p (k g)"), ALU.mult).then_inc(s_wk, 1)
            dve.wait_ge(s_wka, 9)
            v.tensor_copy(Wd.rearrange("p i j g -> p (i j g)")[:, COLS:], psum[:, 4:8, :].rearrange("p t q -> p (t q)")[:, 0:ND * ND * XG - COLS]).then_inc(s_wd[0], 1)
            for n in range(len(plan)):
                if not by_pool[n]:
                    await_product_inputs(dve, n)
                    product(v, n).then_inc(s_pd, 1)
            for t in range(8):
                q, mh = divmod(t, 2)
                dve.wait_ge(s_op, t + 1)
                xv = X[:, mh].rearrange("p b (r x) -> p x (b r)", x=XX)[:, 4 * q:4 * q + 4, :]
                v.scalar_tensor_tensor(xv, psum[:, t, :].rearrange("p (x r) -> p x r", x=4), col("out_b", mh), xv,
                                       ALU.add, ALU.add).then_inc(s_x_new, 1)

            if LAST < 1:
                return
            dve.wait_ge(s_x_new, 8)
            group_norm(1)
            for i in range(TILES):
                dve.wait_ge(s_pw1r, i + 1)
                v.tensor_tensor(xp[:, i, :], xp[:, i, :], xp[:, i, :], ALU.mult).then_inc(s_sq, 1)
                if i == 3:
                    dve.wait_ge(s_cvr, 4)
                    me.link(v.tensor_tensor(rmean[:, 0:2], racc[:, 0:4:2], racc[:, 1:4:2], ALU.add))
                    n = me.add(v.tensor_scalar(rmean[:, 0:2], rmean[:, 0:2], 1.0 / PIX, None, ALU.mult))
                    v.memset(rmean[:, 2:4], 0.0).then_inc(s_rmean, 1)
                    me.link(v.memset(small[:, 330:366], 0.0))
            dve.wait_ge(s_spr, 4)
            hidden = sr_act.rearrange("p (b y x) -> p b y x", b=B, y=H)
            span = [(0, 31), (0, 32), (1, 32)]
            for dx, (lo, hi) in enumerate(span):
                n = me.add(v.tensor_reduce(rsums[:, dx], hidden[:, :, :, lo:hi], AX.X, ALU.add))
            me.upto(n)
            for dy, (lo, hi) in enumerate(span):
                n = me.add(v.tensor_reduce(lhs_u[:, 3 * dy:3 * dy + 3, 2:4], rsums[:, :, :, lo:hi], AX.X, ALU.add))
            me.upto(n)
            v.tensor_scalar(lhs_u[:, :, 2:4], lhs_u[:, :, 2:4], 1.0 / PIX, None, ALU.mult).then_inc(s_u, 1)
            dve.wait_ge(s_fc2c, 10)
            dve.wait_ge(s_str[1], 64)
            me.link(v.tensor_tensor(route_sm, psum[0:4, 4:8, :].rearrange("p f c -> p (f c)"), stream[1][0:4, :], ALU.add))
            rs_f = route_sm.rearrange("p (f c) -> p f c", f=NF)
            me.link(v.tensor_reduce(sm_tmp[:, 0], rs_f.rearrange("p f c -> p c f"), AX.X, ALU.max))
            v.tensor_tensor(rs_f, rs_f, sm_tmp[:, 0].unsqueeze(1).to_broadcast([4, NF, MED]), ALU.subtract).then_inc(s_rl, 1)
            dve.wait_ge(s_re, 1)
            me.link(v.tensor_reduce(sm_tmp[:, 0], rs_f.rearrange("p f c -> p c f"), AX.X, ALU.add))
            me.link(v.reciprocal(sm_tmp[:, 1], sm_tmp[:, 0]))
            v.tensor_tensor(rs_f, rs_f, sm_tmp[:, 1].unsqueeze(1).to_broadcast([4, NF, MED]), ALU.mult).then_inc(s_rd, 1)
            for i in range(TILES):
                dve.wait_ge(s_f2e, i + 1)
                dve.wait_ge(s_wri, i + 1)
                if i >= 2:
                    dve.wait_ge(s_y, i - 1)
                v.tensor_tensor(ya[i % 2], spec[i % 2][:, 0], psum[:, 4, :], ALU.mult).then_inc(s_ya, 1)
                v.tensor_tensor(yb[i % 2], spec[i % 2][:, 1], psum[:, 5, :], ALU.mult).then_inc(s_yb, 1)

            def update_x1(m):
                b, q = divmod(m, 2)
                for mh in range(HALVES):
                    j = 2 * m + mh
                    dve.wait_ge(s_p2, j + 1)
                    xv = X[:, mh, b].rearrange("p (j o) -> p o j", o=WT)[:, 4 * q:4 * q + 4, :]
                    v.tensor_tensor(xv, psum[:, 4 + j % 4, :].rearrange("p (o j) -> p o j", o=4), xv, ALU.add).then_inc(s_x_new, 1)

            for i in range(TILES):
                dve.wait_ge(s_sw, i + 1)
                v.tensor_tensor(xp[:, i, :], xp[:, i, :], psum[:, i % 2, :], ALU.mult).then_inc(s_xw, 1)
                if i % 4 == 1 and i >= 5:
                    update_x1(i // 4 - 1)
            update_x1(3)

            if LAST < 2:
                return
            dve.wait_ge(s_x_new, 16)
            group_norm(2)
            dve.wait_ge(s_w2b, 64)
            me.link(v.tensor_tensor(pwm, pwm, head_mask.unsqueeze(1).to_broadcast([P, QKV_TILES, P]), ALU.mult))
            for t in range(QKV_TILES - 1):
                for a_ in range(TENSOR_TAPS[t]):
                    ins = v.tensor_scalar(pwt[t][:, a_, :], pwm[:, t, :], col("dw2_w", t * K5 + a_), None, ALU.mult)
                    n = me.add(ins) if (t, a_) != (QKV_TILES - 2, TENSOR_TAPS[-2] - 1) else ins.then_inc(s_pwm, 1)

            def denominator_weights(src):
                me.link(v.tensor_tensor(ksum[:, src], kacc[:, src, :, 0:4:2], kacc[:, src, :, 1:4:2], ALU.add))
                for b in range(B):
                    for gr in range(2):
                        ins = v.tensor_scalar(denw[:, src, b, gr, :], head_cols, ksum[:, src, gr, b:b + 1], None, ALU.mult)
                        if (b, gr) != (1, 1):
                            me.add(ins)
                ins.then_inc(s_dnw, 1)

            def mask_products(src):
                for b in range(B):
                    dve.wait_ge(s_vk, src * TILES + WT * (b + 1))
                    v.tensor_tensor(vkm[:, src, b], psum[:, 6 + b, 0:2 * P].rearrange("p (g m) -> p g m", g=2),
                                    head_mask.unsqueeze(1).to_broadcast([P, 2, P]), ALU.mult).then_inc(s_vkm, 1)

            def invert_denominators(src):
                dve.wait_ge(s_den, 2 * src + 2)
                if src == 0:
                    dve.wait_ge(s_ta, EARLY_PRODUCTS)
                me.link(v.tensor_scalar(rden, psum[:, 0:2, :].rearrange("p c q -> p (c q)"), ATT_EPS, None, ALU.add))
                v.reciprocal(rden, rden).then_inc(s_rc, 1)

            def divide(src, s_):
                b, c, gr = ATTEND_ORDER[s_]
                n = 8 * src + s_
                dve.wait_ge(s_ns, n + 1)
                dve.wait_ge(s_rb, n + 1)
                v.tensor_tensor(att[2 * src + gr][:, b * PIX + c * BANK:b * PIX + (c + 1) * BANK], (num_s1 if src else num_s)[s_ % (8 if src else 2)],
                                psum[:, 4 + n % 2, :], ALU.mult).then_inc(s_att, 1)

            for t in DVE_TILES:
                dve.wait_ge(s_qp, CHUNKS * (Q_ORDER.index(t) + 1))
                if t == 2:
                    dve.wait_ge(s_ta, EARLY_PRODUCTS)
                if t == 1:
                    dve.wait_ge(s_tr, TILES)
                if t == DVE_TILES[1]:
                    dve.wait_ge(s_qf, CHUNKS * (Q_ORDER.index(2) + 1))
                    denominator_weights(0)
                for tap in range(TENSOR_TAPS[t], K5):
                    if tap > TENSOR_TAPS[t]:
                        me.upto(tap_n)
                    tap_n = filter_tap(v, me, t, tap)
                    at = tap - TENSOR_TAPS[t]
                    if t == DVE_TILES[1] and at == 4:
                        mask_products(0)
                    if t == DVE_TILES[1] and at == 7:
                        invert_denominators(0)
                    if t == DVE_TILES[1] and 9 <= at < 17:
                        divide(0, at - 9)
            dve.wait_ge(s_yqe, 4 * (max(Y_ORDER.index(0), Y_ORDER.index(2)) + 1))
            denominator_weights(1)
            invert_denominators(1)
            mask_products(1)
            for j in range(5):
                if j < 4:
                    for s_ in (2 * j, 2 * j + 1):
                        divide(1, s_)
                if j >= 1:
                    b, q = divmod(j - 1, 2)
                    for mh in range(HALVES):
                        i = 2 * (j - 1) + mh
                        dve.wait_ge(s_pje, i + 1)
                        xv = X[:, mh, b, q * BANK:(q + 1) * BANK]
                        v.tensor_tensor(xv, xv, proj_s[i % 2], ALU.add).then_inc(s_x_new, 1)
            if LAST < 3:
                return
            dve.wait_ge(s_x_new, 24)
            group_norm(3)
            for tap in range(9):
                ins = v.tensor_scalar(tap3[:, tap, :], ident, col("dw3_w", 9 + tap), None, ALU.mult)
                n = me.add(ins) if tap < 8 else ins.then_inc(s_d3, 1)
            dve.wait_ge(s_z, 12)
            dve.wait_ge(s_zb, 3)
            for tap in range(9):
                if tap:
                    me.upto(tap_n)
                for i in (0, 2):
                    tap_n = filter3(v, me, i, tap, s_dw3)

            def keep_flags(a_, i, data, thresh):
                me.link(v.tensor_reduce(pk[:, 2 * a_, i:i + 1], data, AX.X, ALU.max))
                me.link(v.tensor_scalar(pk[:, 2 * a_ + 1, i:i + 1], pk[:, 2 * a_, i:i + 1], thresh, None, ALU.is_ge))
                return pk[:, 2 * a_ + 1, i:i + 1]

            for a_, i in enumerate((0, 2, 1, 3)):
                dve.wait_ge(s_h3, a_ + 1)
                keep = keep_flags(0, i, h3[:, i, :], DW_THRESH)
                v.tensor_scalar(h3[:, i, :], h3[:, i, :], keep, None, ALU.mult).then_inc(s_kept, 1)
            for a_, i in enumerate((0, 2, 1, 3)):
                dve.wait_ge(s_o3, a_ + 1)
                keep = keep_flags(1, i, o3[:, i, :], PW_THRESH)
                xv = X.rearrange("p h b q -> p (h b) q")[:, i, :]
                v.scalar_tensor_tensor(xv, o3[:, i, :], keep, xv, ALU.mult, ALU.add).then_inc(s_x_new, 1)

        @block.scalar
        def _(act):
            a = nc.scalar

            def group_norm(layer, zc):
                act.wait_ge(s_gn_var, layer + 1)
                a.activation(gsd, gvar, ACT.Sqrt).then_inc(s_gn_sd, 1)
                if layer == 0:
                    act.wait_ge(s_bnv, 1)
                    a.activation(bnsd, bnv, ACT.Sqrt).then_inc(s_bnsd, 1)
                if zc is None:
                    return
                act.wait_ge(s_gn_coef, layer + 1)
                for i in range(4):
                    a.activation(zc[:, i], X.rearrange("p h b q -> p (h b) q")[:, i], ACT.Identity, scale=grs[:, i:i + 1],
                                 bias=gnb[:, i:i + 1]).then_inc(s_zc, 1)

            act.wait_ge(s_const, 80)
            group_norm(0, Zc)
            act.wait_ge(s_z, 4)
            act.wait_ge(s_zb, 1)
            for n in range(HALVES * (9 - DW_TAPS)):
                k, tap = n // (9 - DW_TAPS), DW_TAPS + n % (9 - DW_TAPS)
                dy, dx = divmod(tap, 3)
                if n % (9 - DW_TAPS) == 0:
                    dst = x1_rest[:, k]
                else:
                    dst = dw_tmp[n % 3]
                    if n >= 4:
                        act.wait_ge(s_dwa, sum(1 for m in range(n - 2) if m % (9 - DW_TAPS)))
                for b in range(B):
                    ins = a.activation(dst[:, b * PIX:(b + 1) * PIX].rearrange("p (y x) -> p y x", y=H),
                                       Z[:, 2 * k + b, PAD - 1 + dy:PAD - 1 + dy + H, PAD - 1 + dx:PAD - 1 + dx + W],
                                       ACT.Copy, scale=col("dw0_w", 9 * k + tap))
                ins.then_inc(s_dwp, 1)
            act.wait_ge(s_lnv, 1)
            a.activation(ln_sd, ln_var, ACT.Sqrt).then_inc(s_lnsd, 1)
            for t in range(8):
                q, k = divmod(t, 2)
                act.wait_ge(s_back, t + 1)
                a.activation(g1cm[:, k, 4 * q:4 * q + 4, :], psum[:, t, :].rearrange("p (x q) -> p x q", x=4), ACT.Gelu,
                             scale=col("ln_g", k), bias=col("ln_b", k)).then_inc(s_g1, 1)
            for hf in range(2):
                act.wait_ge(s_lgs, hf + 1)
                a.activation(mask[:, hf], mask[:, hf], ACT.Exp).then_inc(s_exp, 1)
            offs = OM[:, :, 0:2 * G * K2].rearrange("p x (h g k a) -> p h a k x g", h=2, g=GH, k=K2)

            def hat_values(dst, at):
                at_dst = [dst[:, k].rearrange("p k (x g) -> p k x g", g=GH) for k in range(3)]
                a.activation(at_dst[1], at, ACT.Abs)
                a.activation(at_dst[0], at, ACT.Relu, scale=-1.0)
                a.activation(at_dst[2], at, ACT.Relu).then_inc(s_habs, 1)

            act.wait_ge(s_om, XX)
            act.wait_ge(s_ome, XX)
            hat_values(hats[:, 0:3], offs[:, 0, 0])
            hat_values(hats[:, 3:6], offs[:, 0, 1])
            for ax in range(2):
                act.wait_ge(s_habs, ax + 1)
                ins = a.activation(hats[:, 3 * ax + 1], hats[:, 3 * ax + 1], ACT.Identity, scale=-1.0, bias=hat_shift[:, 0:1])
            ins.then_inc(s_hat[0], 1)
            act.wait_ge(s_general, 1)
            offs1_x = wk1.rearrange("p (k x g) -> p k x g", k=K2, g=GH)
            a.activation(offs1_x, offs[:, 1, 0], ACT.Copy).then_inc(s_offx, 1)
            hat_values(hats1_y, offs[:, 1, 1])
            act.wait_ge(s_offx, 1)
            act.wait_ge(s_habs, 3)
            act.wait_ge(s_lgs, 2)
            act.wait_ge(s_amax, 1)
            hat_values(hats1_x, offs1_x)
            for ax, h_ in enumerate((hats1_y, hats1_x)):
                act.wait_ge(s_habs, ax + 3)
                ins = a.activation(h_[:, 1], h_[:, 1], ACT.Identity, scale=-1.0, bias=hat_shift[:, 0:1])
            ins.then_inc(s_hat[1], 1)
            act.wait_ge(s_wka, 9)
            a.activation(Wd.rearrange("p i j g -> p (i j g)")[:, 0:COLS], psum[:, 0:4, :].rearrange("p t q -> p (t q)"), ACT.Copy).then_inc(s_wd[0], 1)
            act.wait_ge(s_wd[0], 2)
            for hf in range(2):
                act.wait_ge(s_acc, ND * ND * (hf + 1))
                for q in range(4):
                    a.activation(outT[:, hf, 4 * q:4 * q + 4, :], psum[:, 4 * hf + q, :].rearrange("p (x q) -> p x q", x=4),
                                 ACT.Copy).then_inc(s_outT, 1)

            if LAST < 1:
                return
            group_norm(1, Zc1)
            for c in range(CHUNKS):
                act.wait_ge(s_fc1, c + 1)
                a.activation(sr_act[:, c * BANK:(c + 1) * BANK], psum[:, c, :], ACT.Relu, bias=col("fc1_b")).then_inc(s_fc1r, 1)
            for c in range(CHUNKS):
                act.wait_ge(s_cv, c + 1)
                a.activation(sr_act[:, c * BANK:(c + 1) * BANK], psum[:, 4 + c, :], ACT.Relu, bias=col("conv_b"),
                             accum_out=racc[:, c:c + 1]).then_inc(s_cvr, 1)
            for i in range(TILES + 4):
                if i < TILES:
                    act.wait_ge(s_pw1, i + 1)
                    a.activation(xp[:, i, :], psum[:, i % 4, :], ACT.Relu).then_inc(s_pw1r, 1)
                if i >= 4:
                    n = i - 4
                    b, t = divmod(n, WT)
                    act.wait_ge(s_f1, n + 1)
                    if n == 0:
                        act.wait_ge(s_cwe, 1)
                    a.activation(U[b][:, t, :], psum[:, 4 + n % 4, :], ACT.Copy).then_inc(s_f1e, 1)
            for c in range(CHUNKS):
                act.wait_ge(s_sp, c + 1)
                if c == 0:
                    act.wait_ge(s_cvr, 4)
                a.activation(sr_act[:, c * BANK:(c + 1) * BANK], psum[:, c, :], ACT.Relu, bias=col("sp1_b")).then_inc(s_spr, 1)
            act.wait_ge(s_rl, 1)
            a.activation(route_sm, route_sm, ACT.Exp).then_inc(s_re, 1)
            for i in range(TILES + 2):
                if i < TILES:
                    act.wait_ge(s_f2, i + 1)
                    if i >= 2:
                        act.wait_ge(s_ya, i - 1)
                        act.wait_ge(s_yb, i - 1)
                    a.activation(spec[i % 2], psum[:, 2 * (i % 2):2 * (i % 2) + 2, :], ACT.Copy).then_inc(s_f2e, 1)
                if i >= 2:
                    n = i - 2
                    b, t = divmod(n, WT)
                    act.wait_ge(s_i2, n + 1)
                    if n == 0:
                        act.wait_ge(s_uo[0], 16 * WT)
                        act.wait_ge(s_uo[1], 16 * WT)
                    a.activation(U[b][:, t, :], psum[:, 6 + n % 2, :], ACT.Copy).then_inc(s_i2e, 1)
            for n in range(TILES):
                b, t = divmod(n, WT)
                act.wait_ge(s_o1, n + 1)
                if t == 0:
                    act.wait_ge(s_uo[b], 32 * WT)
                a.activation(OT[b][:, :, t, :], psum[:, 2 + n % 2, :].rearrange("p (k j) -> p k j", k=KM), ACT.Copy).then_inc(s_o1e, 1)

            if LAST < 2:
                return
            group_norm(2, Zc2)
            made = [0]

            def tap_products(count):
                for n in range(made[0], min(count, len(pool_taps))):
                    t, tap, b = pool_taps[n]
                    act.wait_ge(s_qp, CHUNKS * (Q_ORDER.index(t) + 1))
                    if n >= 3:
                        act.wait_ge(s_ta, n - 2)
                    a.activation(tap_tmp(n).rearrange("p (y x) -> p y x", y=H), tap_view(t, tap, b), ACT.Copy,
                                 scale=col("dw2_w", t * K5 + tap)).then_inc(s_tp, 1)
                    made[0] = n + 1

            act.wait_ge(s_qb, 1)
            for i in range(QKV_TILES * CHUNKS):
                t, c = Q_ORDER[i // CHUNKS], i % CHUNKS
                b, yh = divmod(c, 2)
                act.wait_ge(s_qkv, i + 1)
                a.activation(padq[:, t, b, 2 + 16 * yh:18 + 16 * yh, 2:2 + W], psum[:, i % 4, :].rearrange("p (y x) -> p y x", y=16),
                             ACT.Copy).then_inc(s_qp, 1)
                dst = flat[t][:, c * BANK:(c + 1) * BANK]
                if t in (1, 3):
                    a.activation(dst, psum[:, i % 4, :], ACT.Copy).then_inc(s_qf, 1)
                elif t in (0, 2):
                    a.activation(dst, psum[:, i % 4, :], ACT.Relu, accum_out=kacc[:, 0, t // 2, c:c + 1]).then_inc(s_qf, 1)
                else:
                    a.activation(dst, psum[:, i % 4, :], ACT.Relu).then_inc(s_qf, 1)
                if i >= 9:
                    tap_products(i - 8)

            def copy_turned(src, made=0):
                for i in range(TILES):
                    n = src * TILES + i
                    act.wait_ge(s_tr, n + 1)
                    if n >= 2:
                        act.wait_ge(s_vk, n - 1)
                    a.activation(turned[n % 2], psum[:, 4 + n % 2, :], ACT.Copy).then_inc(s_trc, 1)
                    if i % 2 == 1:
                        tap_products(made + i // 2)

            def copy_numerators(src, made=0):
                for s_ in range(8):
                    n = 8 * src + s_
                    act.wait_ge(s_num, n + 1)
                    if src == 0 and s_ >= 2:
                        act.wait_ge(s_att, s_ - 1)
                    a.activation((num_s1[s_] if src else num_s[s_ % 2]), psum[:, 2 + n % 2, :], ACT.Copy).then_inc(s_ns, 1)
                    if src == 0 and s_ >= 1:
                        tap_products(made + 3 + s_)

            def copy_local(tiles):
                for n_ in tiles:
                    t = Y_ORDER[n_]
                    for c in range(CHUNKS):
                        act.wait_ge(s_yq, 4 * n_ + c + 1)
                        bank = psum[:, y_bank[n_] + c, :]
                        dst = local[t][:, c * BANK:(c + 1) * BANK]
                        if t in (1, 3):
                            a.activation(dst, bank, ACT.Copy).then_inc(s_yqe, 1)
                        elif t in (0, 2):
                            a.activation(dst, bank, ACT.Relu, accum_out=kacc[:, 1, t // 2, c:c + 1]).then_inc(s_yqe, 1)
                        else:
                            a.activation(dst, bank, ACT.Relu).then_inc(s_yqe, 1)

            copy_turned(0, 16)
            act.wait_ge(s_pwm, 1)
            for tap in range(TENSOR_TAPS[-1]):
                ins = a.activation(pwt[-1][:, tap, :], pwm[:, QKV_TILES - 1, :], ACT.Copy, scale=col("dw2_w", (QKV_TILES - 1) * K5 + tap))
            ins.then_inc(s_pwt, 1)
            tap_products(26)
            copy_local([0])
            copy_numerators(0, 27)
            tap_products(46)
            copy_local([1])
            tap_products(54)
            copy_local([2])
            tap_products(68)
            copy_local([3])
            tap_products(len(pool_taps))
            copy_local([4])
            copy_local([5])
            copy_turned(1)
            copy_numerators(1)
            act.wait_ge(s_bn, 1)
            act.wait_ge(s_vk, 2 * TILES)
            for i in range(8):
                mh = i % 2
                act.wait_ge(s_pj, i + 1)
                if i >= 2:
                    act.wait_ge(s_x_new, 16 + i - 1)
                a.activation(proj_s[i % 2], psum[:, i % 4, :], ACT.Identity, scale=bn_inv[:, mh:mh + 1], bias=bn_off[:, mh:mh + 1]).then_inc(s_pje, 1)
            if LAST < 3:
                return
            group_norm(3, None)
            act.wait_ge(s_z, 10)
            act.wait_ge(s_zb, 3)
            for tap in range(9):
                dy, dx = divmod(tap, 3)
                if tap >= 2:
                    act.wait_ge(s_dw3p, tap - 1)
                a.activation(tap3_tmp[tap % 2].rearrange("p (y x) -> p y x", y=H), Z[:, 1, PAD - 1 + dy:PAD - 1 + dy + H, PAD - 1 + dx:PAD - 1 + dx + W],
                             ACT.Copy, scale=col("dw3_w", tap)).then_inc(s_tp3, 1)
            for n, i in enumerate((0, 2, 1, 3)):
                h = i // 2
                scale, bias = bn_inv[:, 2 + h:3 + h], bn_off[:, 2 + h:3 + h]
                if i == 3:
                    act.wait_ge(s_dw3t, 1)
                    a.activation(h3[:, i, :].rearrange("p (c q) -> p c q", c=2), psum[:, 0:2, :], ACT.Relu, scale=scale, bias=bias).then_inc(s_h3, 1)
                else:
                    if i == 1:
                        act.wait_ge(s_dw3p, 9)
                    else:
                        act.wait_ge(s_dw3, n + 1)
                    a.activation(h3[:, i, :], h3[:, i, :], ACT.Relu, scale=scale, bias=bias).then_inc(s_h3, 1)
            for n, i in enumerate((0, 2, 1, 3)):
                h, b = divmod(i, 2)
                act.wait_ge(s_pw3, n + 1)
                bank = (2 + 4 * b + 2 * h) % 8
                a.activation(o3[:, i, :].rearrange("p (c q) -> p c q", c=2), psum[:, bank:bank + 2, :], ACT.Relu,
                             scale=bn_inv[:, 4 + h:5 + h], bias=bn_off[:, 4 + h:5 + h]).then_inc(s_o3, 1)

        @block.gpsimd
        def _(pool):
            g = nc.gpsimd
            me = Steps(pool, s_pool)

            def zero_border():
                g.memset(Z[:, :, 0:PAD, :], 0.0)
                g.memset(Z[:, :, PAD + H:, :], 0.0)
                g.memset(Z[:, :, PAD:PAD + H, 0:PAD], 0.0)
                return g.memset(Z[:, :, PAD:PAD + H, PAD + W:], 0.0)

            zero_border().then_inc(s_zb, 1)
            g.memset(XSc[:, 0:PAD], 0.0)
            g.memset(XSc[:, PAD + XX:], 0.0).then_inc(s_shz, 1)
            g.memset(XSd, 0.0).then_inc(s_shz, 1)
            added = 0
            for n in range(HALVES * (9 - DW_TAPS)):
                k = n // (9 - DW_TAPS)
                if n % (9 - DW_TAPS) == 0:
                    continue
                pool.wait_ge(s_dwp, n + 1)
                if added:
                    pool.wait_ge(s_dwa, added)
                g.tensor_tensor(x1_rest[:, k], x1_rest[:, k], dw_tmp[n % 3], ALU.add).then_inc(s_dwa, 1)
                added += 1
            pool.wait_ge(s_amax, 1)
            me.link(g.partition_all_reduce(amax_all, amax, P, bass.bass_isa.ReduceOp.max))
            me.add(g.tensor_scalar(within, amax_all, 1.0, None, ALU.is_le))
            me.link(g.tensor_scalar(beyond, amax_all, 1.0, None, ALU.is_gt))
            pool.wait_ge(s_mask, 2)
            any_beyond = pool.value_load(beyond[0:1, 0:1], min_val=0, max_val=1)
            general_path(pool, g, any_beyond)
            g.memset(small[:, 442:443], 0.0).then_inc(s_general, 1)
            me.link(g.tensor_scalar(mask[:, 1], mask[:, 1], within, None, ALU.mult))
            pool.wait_ge(s_hat[1], 1)
            me.add(g.memset(Wds[1], 0.0))
            for ky in range(3):
                me.link(g.tensor_tensor(hats1_y[:, ky], hats1_y[:, ky], mask[:, 1], ALU.mult))
            for ky in range(3):
                for kx in range(3):
                    me.link(g.tensor_tensor(wk1, hats1_y[:, ky].rearrange("p k g -> p (k g)"),
                                            hats1_x[:, kx].rearrange("p k g -> p (k g)"), ALU.mult))
                    window = Wds[1][:, kx:kx + 3, ky:ky + 3, :]
                    ins = g.tensor_tensor(window, window, wk1.rearrange("p (i j g) -> p i j g", i=3, j=3), ALU.add)
                    if ky == 2 and kx == 2:
                        ins.then_inc(s_wd[1], 1)
                    else:
                        me.link(ins)
            for n in range(len(plan)):
                if by_pool[n]:
                    await_product_inputs(pool, n)
                    if n in last_of_half:
                        me.link(product(g, n))
                        add_general(pool, g, any_beyond, n)
                        g.memset(small[:, 443:444], 0.0).then_inc(s_pp, 1)
                    else:
                        product(g, n).then_inc(s_pp, 1)
            if LAST < 1:
                return
            pool.wait_ge(s_acc, len(plan))
            pool.wait_ge(s_mask, 2)
            zero_border().then_inc(s_zb, 1)
            pool.wait_ge(s_craw, 32)
            n = me.add(g.tensor_tensor(cwe[:, 0], craw[:, 0], craw[:, 1], ALU.add))
            me.add(g.tensor_tensor(craw[:, 2], craw[:, 2], ccoef[:, 0], ALU.mult))
            me.link(g.tensor_tensor(craw[:, 3], craw[:, 3], ccoef[:, 1], ALU.mult))
            me.link(g.tensor_scalar(cwe[:, 0], cwe[:, 0], 0.5, None, ALU.mult))
            g.tensor_tensor(cwe[:, 1], craw[:, 2], craw[:, 3], ALU.add).then_inc(s_cwe, 1)
            for i in range(TILES):
                pool.wait_ge(s_sq, i + 1)
                g.tensor_scalar(xp[:, i, :], xp[:, i, :], col("star_scale"), col("star_bias"), ALU.mult, ALU.add).then_inc(s_xpd, 1)
            for i in range(TILES):
                pool.wait_ge(s_ya, i + 1)
                pool.wait_ge(s_yb, i + 1)
                if i >= 2:
                    pool.wait_ge(s_i2, i - 1)
                g.tensor_tensor(y_w[i % 2], ya[i % 2], yb[i % 2], ALU.add).then_inc(s_y, 1)
            if LAST < 2:
                return
            pool.wait_ge(s_x_new, 16)
            borders = padq.rearrange("p t b y x -> p (t b) y x")
            g.memset(borders[:, :, 0:2, :], 0.0)
            g.memset(borders[:, :, 2 + H:, :], 0.0)
            g.memset(borders[:, :, 2:2 + H, 0:2], 0.0)
            g.memset(borders[:, :, 2:2 + H, 2 + W:], 0.0).then_inc(s_qb, 1)
            for n, (t, tap, b) in enumerate(pool_taps):
                if tap == TENSOR_TAPS[t] and t == 5:
                    pool.wait_ge(s_yq, 4)
                pool.wait_ge(s_tp, n + 1)
                dst = local[t][:, b * PIX:(b + 1) * PIX]
                if tap == TENSOR_TAPS[t]:
                    g.tensor_copy(dst, tap_tmp(n)).then_inc(s_ta, 1)
                else:
                    pool.wait_ge(s_ta, n - 1)
                    g.tensor_tensor(dst, dst, tap_tmp(n), ALU.add).then_inc(s_ta, 1)
            if LAST < 3:
                return
            pool.wait_ge(s_x_new, 24)
            zero_border().then_inc(s_zb, 1)
            for tap in range(9):
                pool.wait_ge(s_tp3, tap + 1)
                if tap == 0:
                    g.tensor_copy(h3[:, 1, :], tap3_tmp[0]).then_inc(s_dw3p, 1)
                else:
                    pool.wait_ge(s_dw3p, tap)
                    g.tensor_tensor(h3[:, 1, :], h3[:, 1, :], tap3_tmp[tap % 2], ALU.add).then_inc(s_dw3p, 1)


def host_arrays(**i):
    at, n = channel_columns()
    cv = np.zeros((P, n), np.float32)

    def put(name, a):
        a = np.asarray(a, np.float32).reshape(-1, P, *np.shape(a)[1:]).reshape(-1, P, int(np.prod(np.shape(a)[1:]) or 1))
        lo, hi = at[name]
        cv[:, lo:hi] = a.transpose(1, 0, 2).reshape(P, hi - lo)

    put("dw0_w", i["L0_conv_dw_w"].reshape(C, 9))
    for name, src in (("dw0_b", "dw_b"), ("ln_g", "ln_g"), ("ln_b", "ln_b"), ("out_b", "out_b")):
        put(name, i["L0_conv_" + src])
    r = {"chan_vecs": cv, "ident": np.eye(P, dtype=np.float32)}
    blocks = np.kron(np.eye(16, dtype=np.float32), np.ones((8, 8), np.float32))
    r["gmean"] = blocks / 8
    r["head_mask"] = blocks
    sc = np.zeros((P, 7), np.float32)
    sc[:, 0:3] = [1, 0, -1]
    xh = np.arange(P) % 2
    sc[:, 3:5] = (xh == 1)[:, None]
    sc[:, 5:7] = (xh == 0)[:, None]
    r["small_consts"] = sc
    for name in ("in_w", "in_b", "off_w", "off_b", "mask_w", "mask_b", "out_w"):
        r[name] = np.ascontiguousarray(i["L0_conv_" + name])
    put("star_scale", np.broadcast_to(i["L1_conv_star_scale"], (P,)))
    put("star_bias", np.broadcast_to(i["L1_conv_star_bias"], (P,)))
    put("fc1_b", i["L1_conv_rw_fc1_b"])
    put("conv_b", i["L1_conv_rw_conv_b"])
    put("sp1_b", i["L1_conv_sp_fc1_b"])
    r["fc1_w"] = i["L1_conv_rw_fc1_w"][:, :, 0, 0].T
    r["conv_w"] = i["L1_conv_rw_conv_w"][:, :, 0, 0].T
    r["pw1_w"] = i["L1_conv_w_pw1"].T
    r["pw2_w"] = i["L1_conv_w_pw2"].T
    r["sp1_w"] = i["L1_conv_sp_fc1_w"].reshape(P, C, 9).transpose(1, 2, 0)
    r["fc2_w"] = np.concatenate([i["L1_conv_rw_fc2_w"][:, :, 0, 0].T[None], i["L1_conv_sp_fc2_w"].reshape(-1, P, 9).transpose(2, 1, 0)])
    r["fc2_b"] = np.stack([i["L1_conv_rw_fc2_b"]] * 2 + [i["L1_conv_sp_fc2_b"]] * 2)
    r["dft"] = dft_constants()
    first, second, sign = spectra_maps()
    cw = i["L1_conv_complex_weights"].transpose(2, 3, 0, 1)
    r["spectra"] = np.stack([cw[:, part, m[:, 0], m[:, 1]] for part in (0, 1) for m in (first, second)], 1)
    r["spectra_coef"] = np.broadcast_to(sign, (NF, 2, 1024))
    r["spatial_w"] = i["L1_conv_spatial_weights"].reshape(P, WT, NF).transpose(2, 1, 0).reshape(NF, PIX)
    chan = np.concatenate([[24 * (16 * gr + m // 8) + off + m % 8 for m in range(P)]
                           for gr, off in ((0, 8), (0, 16), (1, 8), (1, 16), (0, 0), (1, 0))])
    r["qkv_w"] = i["L2_conv_w_qkv"][chan].T
    put("dw2_w", i["L2_conv_w_dw"].reshape(-1, K5)[chan])
    r["pointwise_w"] = np.tile(i["L2_conv_w_pw"].reshape(-1, 8)[chan].T, (16, 1))
    r["proj_w"] = i["L2_conv_w_proj"].T
    hc = np.zeros((P, 32), np.float32)
    hc[np.arange(P), np.arange(P) // 8] = 1
    r["head_cols"] = hc
    hr = np.zeros((4, 32, P), np.float32)
    hr[:, np.arange(P) // 8, np.arange(P)] = 1
    r["head_rows"] = hr.reshape(P, P)
    for name, l2, l3 in (("bn_g", "gamma", "g"), ("bn_b", "beta", "b"), ("bn_m", "mean", "m"), ("bn_v", "var", "v")):
        put(name, np.concatenate([i["L2_conv_bn_" + l2], i["L3_conv_bn1_" + l3], i["L3_conv_bn2_" + l3]]))
    put("dw3_w", i["L3_conv_dw_w"].reshape(C, 9))
    put("l3_b", np.concatenate([i["L3_conv_dw_b"], i["L3_conv_pw_b"]]))
    r["pw3_w"] = i["L3_conv_pw_w"][:, :, 0, 0].T
    return {k: np.ascontiguousarray(a) for k, a in r.items()}


def dft_rows():
    rows = []
    for t in range(WT):
        if t == 0:
            for ky in (0, H // 2):
                rows += [(ky, kx, 0) for kx in range(17)] + [(ky, kx, 1) for kx in range(1, 16)]
        for ky in ([1] if t == 0 else [2 * t, 2 * t + 1]):
            rows += [(ky, kx, part) for part in (0, 1) for kx in range(W)]
    return rows


def dft_constants():
    comps = []
    for t in range(WT):
        comps.append([(0, 0), (H // 2, 0), (1, 0), (1, 1)] if t == 0 else [(2 * t, 0), (2 * t, 1), (2 * t + 1, 0), (2 * t + 1, 1)])
    f1 = np.zeros((P, P))
    for t in range(WT):
        for j, (ky, part) in enumerate(comps[t]):
            for y in range(H):
                ang = 2 * np.pi * ky * y / H
                val = (np.cos(ang) if part == 0 else -np.sin(ang)) / np.sqrt(H)
                for i in range(4):
                    f1[16 * t + 4 * j + i, 4 * y + i] = val
    rows = dft_rows()
    f2, f2s = np.zeros((2, P, P)), np.zeros((2, P, P))
    for a, t in enumerate((0, 1)):
        for m in range(P):
            ky, kx, part = rows[t * P + m]
            for j, (cy, cpart) in enumerate(comps[t]):
                if cy != ky:
                    continue
                for x in range(W):
                    q = 8 * (4 * j + x // 8) + x % 8
                    e = np.exp(-2j * np.pi * kx * x / W) / np.sqrt(W) * (1j if cpart else 1)
                    f2[a, m, q] = e.imag if part else e.real
                    f2s[a, m, q] = e.real if part else -e.imag
    mats = [f1.T, f2[0].T, f2[1].T, f2s[0].T, f2s[1].T, np.linalg.inv(f2[0]).T, np.linalg.inv(f2[1]).T,
            np.linalg.inv(f1).T]
    return np.stack(mats, 1).astype(np.float32)


def spectra_maps():
    first, second, sign = [], [], np.zeros((2, 1024), np.float32)
    for n, (ky, kx, part) in enumerate(dft_rows()):
        if kx in (0, W // 2):
            first.append((ky, kx)); second.append((-ky % H, kx)); sign[:, n] = 0.5, -0.5
        elif kx < W // 2:
            first.append((ky, kx)); second.append((ky, kx)); sign[:, n] = 0.5, 0.5
        else:
            first.append((-ky % H, W - kx)); second.append(first[-1]); sign[:, n] = -0.5, -0.5
    return np.array(first), np.array(second), sign


def kernel(**inputs):
    import concourse.bacc as bacc
    from concourse.bass_utils import run_bass_kernel_spmd

    inputs = {k: np.asarray(a) for k, a in inputs.items()}
    nc = bacc.Bacc("TRN2", target_bir_lowering=False, num_devices=1)
    arrays = {"x_dram": np.ascontiguousarray(inputs.pop("x").reshape(B, C, PIX))}
    arrays.update({k + "_dram": a for k, a in host_arrays(**inputs).items()})
    aps = {k[:-5]: nc.dram_tensor(k, a.shape, mybir.dt.from_np(a.dtype), kind="ExternalInput").ap() for k, a in arrays.items()}
    out = nc.dram_tensor("out_dram", (B, C, PIX), F32, kind="ExternalOutput").ap()
    pad_image = nc.dram_tensor("xproj_padded", (B, PADDED, PADDED, C), F32).ap()
    general = nc.dram_tensor("general_sample", (HALVES, P, XX * P), F32).ap()
    aps["bounce"] = nc.dram_tensor("bounce", (2, B, P, WT, MED), F32).ap()
    mixer_kernel(nc, aps.pop("x"), out, aps, pad_image, general, LAST_LAYER)
    r = run_bass_kernel_spmd(nc, [arrays], core_ids=[0])
    return r.results[0]["out_dram"].reshape(B, C, H, W)
```

```python
from contextlib import ExitStack

import numpy as np
import concourse.bass as bass
from concourse import mybir

F32 = mybir.dt.float32
I32 = mybir.dt.int32
BF16 = mybir.dt.bfloat16
ALU = mybir.AluOpType
ACT = mybir.ActivationFunctionType
AX = mybir.AxisListType

B, C, H, W = 2, 256, 32, 32
PIX = H * W
P = 128
HALVES = C // P
COLS = B * PIX
PAD = 2
HP = H + 2 * PAD
BANK = 512
CHUNKS = COLS // BANK
G, K2 = 16, 9
XX = W // 2
NOM = 3 * G * K2
GH = G // HALVES
CG = C // G
XG = XX * GH
NPT = K2 * XG
ND = 5
MED, NF = 2 * C, 4
KM = MED // P
WT = 8
TILES = B * WT
FILTER_PART = [0, 0, 0, 1, 1, 2]
ROUTE_PART = [0, 1, 2, 0, 1, 0]
PARTS = len(FILTER_PART)
QKV_TILES = 6
K5 = 25
TENSOR_TAPS = [4, 4, 4, 5, 5, 5]
MASK_AT, INVERT_AT = 4, 6
DIVIDE_AT = 12
AHEAD, BETWEEN = 30, 2
EARLY_PRODUCTS = 14
QROW = H + 4
ATT_EPS = 1e-15
DW_THRESH, PW_THRESH = 4.0, 0.001
GN_EPS = 1e-5
DW_TAPS = [5, 6]
POOL_FROM = 25
REACH = H
PADDED = H + 2 * REACH


class Steps:

    def __init__(self, engine, sem):
        self.engine, self.sem, self.n = engine, sem, 0

    def add(self, ins):
        ins.then_inc(self.sem, 1)
        self.n += 1
        return self.n

    def link(self, ins):
        self.add(ins)
        self.engine.wait_ge(self.sem, self.n)

    def upto(self, n):
        self.engine.wait_ge(self.sem, n)


def channel_columns():
    names, at = {}, 0
    for name, width in (("dw0_w", 18), ("dw0_b", 2), ("ln_g", 2), ("ln_b", 2), ("out_b", 2),
                        ("star_scale", 1), ("star_bias", 1), ("fc1_b", 1), ("conv_b", 1), ("sp1_b", 1),
                        ("dw2_w", 150), ("dw3_w", 18), ("bn_g", 6), ("bn_b", 6), ("bn_m", 6), ("bn_v", 6),
                        ("l3_b", 4)):
        names[name] = (at, at + width)
        at += width
    return names, at


def mixer_kernel(nc, x_in, out, w, xpad_dram, general_dram):
    cv_at, cv_n = channel_columns()
    with ExitStack() as ctx:
        def sem(name):
            return ctx.enter_context(nc.semaphore(name))

        arena_words = 53000
        arena = ctx.enter_context(nc.sbuf_tensor("arena", [P, arena_words], F32))
        psum = ctx.enter_context(nc.psum_tensor("psum", [P, 8, BANK], F32))

        def words(at, n):
            assert at + n <= arena_words, (at, n)
            return arena[:, at:at + n]

        top = [0]

        def take(n):
            top[0] += n
            return words(top[0] - n, n)

        X = take(HALVES * COLS).rearrange("p (h b q) -> p h b q", h=HALVES, b=B)
        Z = take(HALVES * B * HP * HP).rearrange("p (i y x) -> p i y x", y=HP, x=HP)
        z_base = HALVES * COLS
        ident = take(P)
        gmean = take(P)
        head_mask = take(P)
        cv = take(cv_n)
        small = take(512)
        L = top[0]

        def col(name, i=0, n=1):
            a, _ = cv_at[name]
            return cv[:, a + i:a + i + n]

        Xi = X.rearrange("p h b (y x) -> p (h b) y x", y=H)

        def z_inner(i):
            return Z[:, i, PAD:PAD + H, PAD:PAD + W]

        st = small[:, 0:48].rearrange("p (i c s) -> p i c s", i=4, c=2)
        mv = small[:, 48:56].rearrange("p (i s) -> p i s", s=2)
        gq = small[:, 56:64].rearrange("p (s i) -> p s i", s=2)
        gm = small[:, 64:72].rearrange("p (s i) -> p s i", s=2)
        gvar, gsd, grs, gt, gnb = (small[:, 72 + 4 * j:76 + 4 * j] for j in range(5))
        amax, amax_all, within = (small[:, 92 + j:93 + j] for j in range(3))
        beyond = small[:, 95:96].bitcast(I32)
        hat_shift = small[:, 96:99]
        part_mask = small[0:PARTS * NF, 99:101]
        ln_st = small[:, 104:200].rearrange("p (x s) -> p x s", s=6)
        ln_mv = small[:, 200:232].rearrange("p (x s) -> p x s", s=2)
        ln_var, ln_sd, ln_rs, ln_t, ln_nb = (small[:, 232 + 16 * j:248 + 16 * j] for j in range(5))

        s_x, s_const, s_w0 = sem("x_loaded"), sem("consts_loaded"), sem("l0_weights_loaded")
        s_gn_stats, s_gn_means, s_gn_var = sem("gn_stats"), sem("gn_group_means"), sem("gn_var")
        s_gn_sd, s_gn_coef, s_z = sem("gn_sd"), sem("gn_coef"), sem("z_padded_written")
        s_zc = sem("z_unpadded_written")
        s_zb = sem("z_border_zero")
        s_x_new = sem("x_updated")
        s_dve, s_pool = sem("dve_steps"), sem("pool_steps")
        s_out = sem("output_stored")

        o = L
        inw = words(o, 512).rearrange("p (k c) -> p k c", k=2); o += 512
        omw = words(o, 2 * NOM).rearrange("p (k c) -> p k c", k=2); o += 2 * NOM
        outw = words(o, 512).rearrange("p (k c) -> p k c", k=2); o += 512
        inb = words(o, C); o += C
        omb = words(o, NOM); o += NOM
        XSc = words(o, (XX + 4) * C).rearrange("p (x c) -> p x c", c=C); o += (XX + 4) * C
        XSd = words(o, 4 * (XX + 4) * P).rearrange("p (d x c) -> p d x c", d=4, c=P); o += 4 * (XX + 4) * P
        r1 = o; o += 2 * HALVES * COLS
        Zc = words(o, HALVES * COLS).rearrange("p (i q) -> p i q", q=PIX)
        OM = words(o, XX * NOM).rearrange("p (x o) -> p x o", o=NOM); o += XX * NOM
        mask = words(o, 2 * NPT).rearrange("p (h k g) -> p h k g", h=2, k=K2); o += 2 * NPT
        mask_x = mask.rearrange("p h k (x g) -> p h k x g", g=GH)
        amax_part = small[:, 444:446]
        wd_at = o
        Wd = words(o, ND * ND * XG).rearrange("p (i j g) -> p i j g", i=ND, j=ND); o += ND * ND * XG
        hats1_y = words(o, 3 * NPT).rearrange("p (a k g) -> p a k g", a=3, k=K2); o += 3 * NPT
        x1cm = words(r1, HALVES * COLS).rearrange("p (h q) -> p h q", h=HALVES)
        x1n = words(r1 + HALVES * COLS, HALVES * COLS).rearrange("p (x c) -> p x c", c=C)
        x1_rest = words(r1 + HALVES * COLS, HALVES * COLS).rearrange("p (h q) -> p h q", h=HALVES)
        dw_tmp = [words(wd_at + COLS * j, COLS) for j in range(3)]
        rest_taps = [(k, tap) for k in range(HALVES) for tap in range(DW_TAPS[k], 9)]
        rest_sums = [8 - DW_TAPS[0], 16 - sum(DW_TAPS)]
        s_dwp, s_dwa = sem("dw_tap_products"), sem("dw_tap_products_added")
        g1cm = words(r1, HALVES * COLS).rearrange("p (h x q) -> p h x q", h=HALVES, x=XX)
        hats = words(r1, 6 * NPT).rearrange("p (a k g) -> p a k g", a=6, k=K2)
        wk = [words(r1 + 6 * NPT, NPT), mask[:, 0].rearrange("p k g -> p (k g)")]
        s_wk, s_wka = sem("weight_terms"), sem("weight_terms_added")
        wk1 = words(L, NPT)
        hats1_x = OM.rearrange("p x o -> p (x o)")[:, XX * NOM - 3 * NPT:].rearrange("p (a k g) -> p a k g", a=3, k=K2)
        prods = [words(at, COLS) for at in (z_base, z_base + COLS, r1 + HALVES * COLS, r1 + (HALVES + 1) * COLS)]
        NB = len(prods)
        sm_t = words(z_base + 4096, 2 * XG).rearrange("p (h g) -> p h g", h=2)
        sm_r = words(z_base + 4096 + 2 * XG, 2 * XG).rearrange("p (h g) -> p h g", h=2)
        Wds = [Wd, OM.rearrange("p x o -> p (x o)")[:, 0:ND * ND * XG].rearrange("p (i j g) -> p i j g", i=ND, j=ND)]
        outT = words(r1, HALVES * COLS).rearrange("p (h x q) -> p h x q", h=HALVES, x=XX)

        s_xp, s_xpe = sem("xproj_ready"), sem("xproj_evacuated")
        s_shift = [sem(f"xproj_shifted_{j}") for j in range(4)]
        s_shz = sem("shift_border_zero")
        s_x1 = sem("x1_ready")
        s_lnv, s_lnsd = sem("ln_var"), sem("ln_sd")
        s_x1t, s_x1n = sem("x1_turned"), sem("x1_normalised")
        s_back, s_g1 = sem("x1n_turned_back"), sem("gelu_done")
        s_om, s_ome = sem("offset_mask_ready"), sem("offset_mask_evacuated")
        s_lgs, s_exp = sem("mask_logits_shifted"), sem("mask_exp")
        s_amax = sem("offset_amax")
        s_habs, s_mask, s_general = sem("hat_values"), sem("mask_ready"), sem("general_path_done")
        s_hat = [sem(f"hats_ready_{hf}") for hf in range(2)]
        s_wd = [sem(f"displacement_weights_{hf}") for hf in range(2)]
        s_pd, s_pp = sem("product_by_dve"), sem("product_by_pool")
        s_acc = sem("product_accumulated")
        s_outT, s_op, s_halo = sem("sampled_evacuated"), sem("out_projected"), sem("halo_columns")
        s_gen, s_gstep = sem("general_dma"), sem("general_step")

        o = L
        fc1w = words(o, 2 * P).rearrange("p (k c) -> p k c", k=2); o += 2 * P
        convw = words(o, P); o += P
        pw1w = words(o, 2 * MED).rearrange("p (k c) -> p k c", k=2); o += 2 * MED + P
        filters = words(L, 1536)[0:PARTS * NF].bitcast(BF16)
        sp1w = words(o, 18 * P).rearrange("p (k t c) -> p k t c", k=2, t=9)
        logits1 = words(o, 64).rearrange("p (f n) -> p f n", f=NF)
        lg_max, lg_sum, lg_rec = (words(o + 64 + 16 * j, 16) for j in range(3))
        lg_rows = words(o + 600, MED)
        spare_spec = words(o + 1112, 1024)
        rpart = [words(o + 112 + 32 * j, 32).bitcast(BF16).rearrange("p (f n) -> p f n", f=NF) for j in range(3)]
        rparts = words(o + 208, 16 * PARTS * NF).rearrange("p (n g f) -> p n g f", n=16, g=PARTS); o += 18 * P
        pw2w = words(o, KM * C).rearrange("p (k c) -> p k c", k=KM); o += KM * C
        dft = words(o, 8 * P).rearrange("p (a m) -> p a m", a=8); o += 8 * P
        filters32 = words(o, 3 * 1024)[0:PARTS * NF]
        cwe = words(o, 2 * 1024)[0:PARTS * NF].rearrange("p (a m) -> p a m", a=2); o += 2048
        spw = words(o, 1024)[0:PARTS * NF]; o += 1024
        stream = [words(o + 2048 * j, 2048) for j in range(3)]; o += 3 * 2048
        route = stream[2][0:PARTS * NF, 0:1024].bitcast(BF16).rearrange("p (r c) -> p r c", r=4)
        sr_act = words(o, COLS); o += COLS
        Zc1 = words(o, HALVES * COLS).rearrange("p (i q) -> p i q", q=PIX)
        V = [words(o + 4096 * b, 4096).rearrange("p (t c) -> p t c", t=WT) for b in range(B)]; o += 8192
        craw = words(o, 4096)[0:PARTS * NF].rearrange("p (a m) -> p a m", a=4)
        ccoef = words(o + 4096, 2048)[0:PARTS * NF].rearrange("p (a m) -> p a m", a=2)
        U = [words(o + 4096 * b, 4096).rearrange("p (t c) -> p t c", t=WT) for b in range(B)]; o += 8192
        chunk_at = stream + [U[j // 2].rearrange("p t c -> p (t c)")[:, j % 2 * 2048:(j % 2 + 1) * 2048] for j in range(4)]
        NCB = len(chunk_at)
        OT = [u.rearrange("p t c -> p (t c)").rearrange("p (k t j) -> p k t j", k=KM, t=WT) for u in U]
        xp = words(o, TILES * MED).rearrange("p (t c) -> p t c", t=TILES); o += TILES * MED
        racc = small[:, 322:326]
        means = words(o, 10 * 32).rearrange("p (c m) -> p c m", c=10); o += 320
        rsum2 = words(o, 256); o += 256
        fc2b = words(o, 64).rearrange("p (f n) -> p f n", f=NF); o += 64
        rsums = rsum2[:, 0:192].rearrange("p (v b y) -> p v b y", v=3, b=2)

        s_w1, s_w1b, s_craw = sem("l1_weights_loaded"), sem("l1_late_weights"), sem("l1_spectra_loaded")
        s_cwe = sem("l1_spectra_ready")
        s_str = [sem(f"l1_stream_{j}") for j in range(NCB)]
        s_fc1, s_fc1r, s_cv, s_cvr = sem("fc1"), sem("fc1_relu"), sem("conv"), sem("conv_relu")
        s_pw1, s_pw1r, s_sq, s_xpd = sem("pw1"), sem("pw1_relu"), sem("pw1_squared"), sem("xp_ready")
        s_f1, s_f1e = sem("rows_dft"), sem("rows_dft_evacuated")
        s_uo = [sem(f"bounce_out_{b}") for b in range(B)]
        s_vi = [sem(f"bounce_in_{j}") for j in range(TILES)]
        s_sp, s_spr, s_u = sem("sp_conv"), sem("sp_relu"), sem("sp_tap_means")
        s_fc2c, s_rmean = sem("fc2_chunk"), sem("route_mean")
        s_lgc, s_lgt = sem("logits_copied"), sem("logits_turned")
        s_rl, s_re, s_rd, s_rt, s_rtc = sem("route_logits"), sem("route_exp"), sem("route_parts"), sem("route_turned"), sem("route_copied")
        s_fil = sem("filters_in_parts")
        s_f2, s_f2e, s_wri = sem("spectrum"), sem("spectrum_evacuated"), sem("spectrum_weights")
        s_ya, s_yb, s_y = sem("weighted_a"), sem("weighted_b"), sem("weighted")
        s_i2, s_i2e = sem("columns_inverse"), sem("columns_inverse_evacuated")
        s_sw, s_xw, s_o1, s_o1e = sem("spatial_weight"), sem("spatially_weighted"), sem("filtered"), sem("filtered_evacuated")
        s_p2 = sem("pw2")
        ya = [words(z_base + 512 * j, 512) for j in range(2)]
        yb = [words(z_base + 1024 + 512 * j, 512) for j in range(2)]
        y_w = [words(z_base + 2048 + 512 * j, 512) for j in range(2)]
        spec = [at.rearrange("p (a c) -> p a c", a=2) for at in
                (words(z_base + 3072, 1024), words(z_base + 4096, 1024), sr_act[:, 0:1024], sr_act[:, 1024:2048],
                 spare_spec)]
        NS = len(spec)

        o = L
        Zc2 = words(z_base, HALVES * COLS).rearrange("p (i q) -> p i q", q=PIX)
        rden = words(z_base + HALVES * COLS, 1024)
        qkvw = words(o, 2 * 768).rearrange("p (k c) -> p k c", k=2)
        num_s = [words(at, BANK) for at in (o, o + BANK)]; o += 1536
        num_s1 = num_s + [words(z_base + BANK * j, BANK) for j in range(6)]
        pwm = words(o, 768).rearrange("p (t m) -> p t m", t=QKV_TILES); o += 768
        pwt_at = [o + sum(TENSOR_TAPS[:t]) * P for t in range(QKV_TILES - 1)] + [z_base + 3 * PIX]
        pwt = [words(pwt_at[t], TENSOR_TAPS[t] * P).rearrange("p (a m) -> p a m", m=P) for t in range(QKV_TILES)]
        o += sum(TENSOR_TAPS[:-1]) * P
        projw = words(o, 1024).rearrange("p (k c) -> p k c", k=4); o += 1024
        head_cols = words(o, 32); o += 32
        head_rows = words(o, P); o += P
        vkm = words(o, 1024).rearrange("p (s b g m) -> p s b g m", s=2, b=B, g=2); o += 1024
        denw = words(o, 256).rearrange("p (s b g m) -> p s b g m", s=2, b=B, g=2); o += 256
        turned = [words(o + 512 * j, 512) for j in range(2)]
        proj_s = turned; o += 1024
        padq_at = o
        padq = words(o, QKV_TILES * B * QROW * QROW).rearrange("p (t b y x) -> p t b y x", t=QKV_TILES, b=B, y=QROW); o += QKV_TILES * B * QROW * QROW
        flat = [words(o + COLS * t, COLS) for t in range(QKV_TILES)]; o += QKV_TILES * COLS
        tile_pad = B * QROW * QROW
        local = [words(o, COLS), flat[0], words(o + COLS, COLS), flat[1], words(o + 2 * COLS, COLS),
                 words(padq_at, COLS)]; o += 3 * COLS
        att = [flat[2], flat[3], words(padq_at + 2 * tile_pad, COLS), words(padq_at + 3 * tile_pad, COLS)]
        kacc = small[:, 370:386].rearrange("p (s g c) -> p s g c", s=2, g=2)
        ksum = small[:, 386:394].rearrange("p (s g b) -> p s g b", s=2, g=2)
        bnv, bnsd, bn_inv, bnt, bn_off = (small[:, 394 + 6 * j:400 + 6 * j] for j in range(5))
        s_w2, s_w2b, s_bnv, s_bnsd, s_bn = sem("l2_weights_loaded"), sem("l2_late_weights"), sem("bn_var"), sem("bn_sd"), sem("bn_ready")
        s_qb, s_qkv, s_qp, s_qf = sem("qkv_border_zero"), sem("qkv"), sem("qkv_padded"), sem("qkv_flat")
        s_dnw = sem("denominator_weights")
        s_pwm, s_pwt = sem("pointwise_ready"), sem("late_tap_weights")
        s_tr, s_trc, s_vk, s_vkm = sem("kv_turned"), sem("kv_turned_copied"), sem("vk"), sem("vk_masked")
        s_den, s_rc, s_num, s_rb, s_ns, s_att = (sem("denominators"), sem("denominators_inverted"), sem("numerators"),
                                                 sem("inverse_spread"), sem("numerators_copied"), sem("attended"))
        s_dwd, s_yq, s_yqe = sem("filtered_by_dve"), sem("local_qkv"), sem("local_qkv_copied")
        s_pj, s_pje = sem("proj"), sem("proj_scaled")
        Q_ORDER = [0, 4, 1, 2, 3, 5]
        Y_ORDER = [0, 2, 4, 1, 3, 5]
        y_bank = [4, 0, 0, 0, 4, 0]
        local_free = [0, 4, 8, 12, 16, 16]
        ATTEND_ORDER = [(b, c, gr) for b in range(B) for c in range(2) for gr in range(2)]
        POOL_TILES = [4, 5]
        DVE_TILES = [0, 2, 1, 3]

        pool_taps = [(t, a, b) for t in POOL_TILES for a in range(TENSOR_TAPS[t], K5) for b in range(B)]
        early_tmp = [local[2][:, 0:PIX], local[2][:, PIX:COLS], rden]
        late_tmp = [Zc2[:, j, :] for j in range(3)]

        def tap_tmp(n):
            return (early_tmp if n < EARLY_PRODUCTS else late_tmp)[n % 3]

        s_tp = sem("tap_product")
        s_ta = sem("tap_product_added")

        def tap_view(t, a, b):
            dy, dx = divmod(a, 5)
            return padq[:, t, b, dy:dy + H, dx:dx + W]

        def filter_tap(eng, step, t, a):
            for b in range(B):
                dst = local[t][:, b * PIX:(b + 1) * PIX].rearrange("p (y x) -> p y x", y=H)
                wt = col("dw2_w", t * K5 + a)
                if a == TENSOR_TAPS[t]:
                    ins = eng.tensor_scalar(dst, tap_view(t, a, b), wt, None, ALU.mult)
                else:
                    ins = eng.scalar_tensor_tensor(dst, tap_view(t, a, b), wt, dst, ALU.mult, ALU.add)
                if a == K5 - 1:
                    ins.then_inc(s_dwd, 1)
                    n = step.n
                else:
                    n = step.add(ins)
            return n

        o = L
        pw3w = words(o, 512).rearrange("p (k c) -> p k c", k=2); o += 512
        tap3 = words(o, 9 * P).rearrange("p (a m) -> p a m", a=9); o += 9 * P
        h3 = words(o, HALVES * COLS).rearrange("p (i q) -> p i q", q=PIX); o += HALVES * COLS
        o3 = words(o, HALVES * COLS).rearrange("p (i q) -> p i q", q=PIX); o += HALVES * COLS
        pk = small[:, 424:440].rearrange("p (a i) -> p a i", a=4)
        tap3_tmp = [words(o + 1024 * j, 1024) for j in range(2)]; o += 2048
        s_tp3 = sem("l3_tap_product")
        s_w3, s_d3, s_dw3, s_dw3p, s_h3 = sem("l3_weights_loaded"), sem("l3_taps_ready"), sem("l3_dw_by_dve"), sem("l3_dw_by_pool"), sem("l3_hidden")
        s_dw3t, s_kept, s_pw3, s_o3 = sem("l3_dw_by_tensor"), sem("l3_pruned"), sem("l3_pointwise"), sem("l3_result")

        def filter3(eng, step, i, tap, last):
            dy, dx = divmod(tap, 3)
            src = Z[:, i, PAD - 1 + dy:PAD - 1 + dy + H, PAD - 1 + dx:PAD - 1 + dx + W]
            dst = h3[:, i, :].rearrange("p (y x) -> p y x", y=H)
            wt = col("dw3_w", i // 2 * 9 + tap)
            if tap == 0:
                ins = eng.tensor_scalar(dst, src, wt, None, ALU.mult)
            else:
                ins = eng.scalar_tensor_tensor(dst, src, wt, dst, ALU.mult, ALU.add)
            if tap < 8:
                return step.add(ins)
            ins.then_inc(last, 1)
            return step.n

        ORDER = [2, 1, 3, 0, 4]
        plan = []
        for hf in range(HALVES):
            for a, j in enumerate(ORDER):
                for i in range(ND):
                    plan.append((hf, j, i))
        by_pool = [n >= POOL_FROM and n % 3 == 1 for n in range(len(plan))]
        last_of_half = [len(plan) // 2 - 1, len(plan) - 1]
        for n in last_of_half:
            by_pool[n] = True
        upto_dve = np.cumsum([not b for b in by_pool]).tolist()
        upto_pool = np.cumsum(by_pool).tolist()

        def shifted(hf, j, i):
            src = XSc[:, i:i + XX, hf * P:(hf + 1) * P] if j == 2 else XSd[:, j - (j > 2), i:i + XX, :]
            return src.rearrange("p x (g c) -> p x g c", c=CG)

        def product(eng, n):
            hf, j, i = plan[n]
            weight = Wds[hf][:, i, j, :].rearrange("p (x g) -> p x g", g=GH).unsqueeze(3).to_broadcast([P, XX, GH, CG])
            return eng.tensor_tensor(prods[n % NB].rearrange("p (x g c) -> p x g c", g=GH, c=CG),
                                     shifted(hf, j, i), weight, ALU.mult)

        def await_product_inputs(eng, n):
            hf, j, i = plan[n]
            eng.wait_ge(s_wd[hf], (2, 1)[hf])
            if j == 2:
                eng.wait_ge(s_halo, 32)
            else:
                eng.wait_ge(s_shift[j - (j > 2)], 32 * (hf + 1))
            if n >= NB:
                eng.wait_ge(s_acc, n - NB + 1)

        gen_x, gen_y, gen_hy, gen_w = (words(wd_at + NPT * j, NPT).rearrange("p (k g) -> p k g", k=K2) for j in range(4))
        gen_src, gen_acc = prods[0], prods[1]
        gen_tmp = gen_src[:, 0:NPT].rearrange("p (k g) -> p k g", k=K2)
        gen_dy, gen_dx = small[:, 440:441], small[:, 441:442]

        def restart(pool):
            pool.dma_reset(range(s_gen.num, s_gen.num + 1))
            pool.sem_clear(s_gen)

        def hat(me, g, out_, at, centre):
            me.link(g.tensor_scalar(out_, at, centre, None, ALU.subtract))
            me.link(g.tensor_scalar(gen_tmp, out_, 0.0, None, ALU.max))
            me.link(g.tensor_scalar(out_, out_, 0.0, None, ALU.min))
            me.link(g.tensor_tensor(out_, out_, gen_tmp, ALU.subtract))
            me.link(g.tensor_scalar(out_, out_, 1.0, 0.0, ALU.add, ALU.max))

        def general_path(pool, g, any_beyond):
            with pool.If(any_beyond > 0):
                pool.wait_ge(s_mask, 2)
                me = Steps(pool, s_gstep)
                me.link(g.memset(gen_acc, 0.0))
                blank = xpad_dram.rearrange("b y x c -> (b y x c)").rearrange("(n p q) -> n p q", p=P, q=XX * P)
                for n in range(blank.shape[0]):
                    g.dma_start(blank[n], gen_acc).then_inc(s_gen, 16)
                    pool.wait_ge(s_gen, 16 * (n + 1))
                for b in range(B):
                    for s_ in range(2):
                        rows = XSc[b * 64 + s_:(b + 1) * 64:2, PAD:PAD + XX, :]
                        g.dma_start(xpad_dram[b, REACH:REACH + H, REACH + XX * s_:REACH + XX * (s_ + 1), :], rows).then_inc(s_gen, 16)
                        pool.wait_ge(s_gen, 16 * (blank.shape[0] + 1 + 2 * b + s_))
                restart(pool)
                pool.sem_clear(s_gstep)
                offs = OM[:, :, 0:2 * G * K2].rearrange("p x (h g k a) -> p h a k x g", h=2, g=GH, k=K2)
                for hf in range(HALVES):
                    me = Steps(pool, s_gstep)
                    for k in range(K2):
                        for a_, dst in ((0, gen_x), (1, gen_y)):
                            shift = float((k // 3, k % 3)[a_] - 1)
                            me.add(g.tensor_scalar(dst[:, k].rearrange("p (x g) -> p x g", g=GH), offs[:, hf, a_, k], shift, None, ALU.add))
                    me.add(g.memset(gen_acc, 0.0))
                    me.link(g.memset(gen_dy, -float(REACH)))
                    pool.sem_clear(s_gstep)
                    with pool.Fori(0, 2 * REACH) as i:
                        me = Steps(pool, s_gstep)
                        hat(me, g, gen_hy, gen_y, gen_dy)
                        me.link(g.tensor_tensor(gen_hy, gen_hy, mask[:, hf], ALU.mult))
                        me.add(g.tensor_scalar(gen_dy, gen_dy, 1.0, None, ALU.add))
                        me.link(g.memset(gen_dx, -float(REACH)))
                        pool.sem_clear(s_gstep)
                        with pool.Fori(0, 2 * REACH) as j:
                            me = Steps(pool, s_gstep)
                            hat(me, g, gen_w, gen_x, gen_dx)
                            me.link(g.tensor_tensor(gen_w, gen_w, gen_hy, ALU.mult))
                            me.add(g.tensor_scalar(gen_dx, gen_dx, 1.0, None, ALU.add))
                            for k in range(1, K2):
                                me.link(g.tensor_tensor(gen_w[:, 0], gen_w[:, 0], gen_w[:, k], ALU.add))
                            for b in range(B):
                                for s_ in range(2):
                                    src = xpad_dram[b, bass.ds(i, H), bass.ds(j + XX * s_, XX), hf * P:(hf + 1) * P]
                                    dst = gen_src.rearrange("p (x c) -> p x c", c=P)[b * 64 + s_:(b + 1) * 64:2]
                                    g.dma_start(dst, src).then_inc(s_gen, 16)
                                    pool.wait_ge(s_gen, 16 * (2 * b + s_ + 1))
                            weight = gen_w[:, 0].rearrange("p (x g) -> p x g", g=GH).unsqueeze(3).to_broadcast([P, XX, GH, CG])
                            term = gen_src.rearrange("p (x g c) -> p x g c", g=GH, c=CG)
                            me.link(g.tensor_tensor(term, term, weight, ALU.mult))
                            me.link(g.tensor_tensor(gen_acc, gen_acc, gen_src, ALU.add))
                            restart(pool)
                            pool.sem_clear(s_gstep)
                    g.dma_start(general_dram[hf], gen_acc).then_inc(s_gen, 16)
                    pool.wait_ge(s_gen, 16)
                    restart(pool)

        def add_general(pool, g, any_beyond, n):
            with pool.If(any_beyond > 0):
                g.dma_start(prods[n % NB], general_dram[plan[n][0]], accum_op=ALU.add).then_inc(s_gen, 16)
                pool.wait_ge(s_gen, 16)
                restart(pool)

        block = ctx.enter_context(nc.Block())

        @block.sync
        def _(sp):
            for i in range(4):
                h, b = divmod(i, 2)
                sp.dma_start(X[:, h, b, :], x_in[b, h * P:(h + 1) * P]).then_inc(s_x, 16)
            sp.dma_start(cv, w["chan_vecs"]).then_inc(s_const, 16)
            sp.dma_start(ident, w["ident"]).then_inc(s_const, 16)
            sp.dma_start(gmean, w["gmean"]).then_inc(s_const, 16)
            sp.dma_start(head_mask, w["head_mask"]).then_inc(s_const, 16)
            sp.dma_start(small[:, 96:103], w["small_consts"]).then_inc(s_const, 16)
            sp.dma_start(inw, w["in_w"].rearrange("(k p) c -> p k c", p=P)).then_inc(s_w0, 16)
            sp.dma_start(inb, w["in_b"].partition_broadcast(P)).then_inc(s_w0, 16)
            sp.dma_start(omw[:, :, 0:2 * G * K2], w["off_w"].rearrange("(k p) c -> p k c", p=P)).then_inc(s_w0, 16)
            sp.dma_start(omw[:, :, 2 * G * K2:], w["mask_w"].rearrange("(k p) c -> p k c", p=P)).then_inc(s_w0, 16)
            sp.dma_start(omb[:, 0:2 * G * K2], w["off_b"].partition_broadcast(P)).then_inc(s_w0, 16)
            sp.dma_start(omb[:, 2 * G * K2:], w["mask_b"].partition_broadcast(P)).then_inc(s_w0, 16)
            sp.dma_start(outw, w["out_w"].rearrange("(k p) c -> p k c", p=P)).then_inc(s_w0, 16)
            sp.wait_ge(s_xpe, 8)
            sp.wait_ge(s_shz, 2)
            sp.dma_start(XSc[1::2, 0:PAD], XSc[0::2, XX:XX + PAD]).then_inc(s_halo, 16)
            sp.dma_start(XSc[0::2, PAD + XX:], XSc[1::2, PAD:2 * PAD]).then_inc(s_halo, 16)
            sp.wait_ge(s_halo, 32)
            for hf in range(HALVES):
                for a, j in enumerate(ORDER[1:]):
                    if hf:
                        sp.wait_ge(s_acc, ND * (a + 2))
                    d = 2 * (j - 2)
                    for b in range(B):
                        lo, hi = b * 64 + max(0, -d), b * 64 + 64 - max(0, d)
                        sp.dma_start(XSd[lo:hi, j - (j > 2)], XSc[lo + d:hi + d, :, hf * P:(hf + 1) * P]).then_inc(s_shift[j - (j > 2)], 16)
            sp.wait_ge(s_x_new, 8)
            for dst, name in ((fc1w, "fc1_w"), (pw1w, "pw1_w")):
                sp.dma_start(dst, w[name].rearrange("(k p) c -> p k c", p=P)).then_inc(s_w1, 16)
            sp.dma_start(convw, w["conv_w"]).then_inc(s_w1, 16)
            sp.dma_start(dft, w["dft"]).then_inc(s_w1, 16)
            sp.dma_start(craw, w["spectra"]).then_inc(s_craw, 16)
            sp.dma_start(ccoef, w["spectra_coef"]).then_inc(s_craw, 16)
            sp.dma_start(sp1w, w["sp1_w"].rearrange("(k p) t c -> p k t c", p=P)).then_inc(s_w1b, 16)
            sp.dma_start(spw, w["spatial_w"]).then_inc(s_w1b, 16)
            sp.dma_start(fc2b.rearrange("p f n -> p (f n)"), w["fc2_b"]).then_inc(s_w1b, 16)
            sp.dma_start(pw2w, w["pw2_w"].rearrange("(k p) c -> p k c", p=P)).then_inc(s_w1b, 16)
            for c in range(3):
                sp.dma_start(chunk_at[c], w["fc2_w"][c]).then_inc(s_str[c], 16)
            for b in range(B):
                for t in range(WT):
                    sp.wait_ge(s_f1e, WT * b + t + 1)
                    sp.dma_start(w["bounce"][0, b, :, t, :], U[b][:, t, :]).then_inc(s_uo[b], 16)
            for b in range(B):
                sp.wait_ge(s_uo[b], 16 * WT)
                if b == 0:
                    sp.wait_ge(s_pw1, TILES)
                for t in range(WT):
                    rows = w["bounce"][0, b].rearrange("s w c -> (s w) c")[t * P:(t + 1) * P, :]
                    sp.dma_start(V[b][:, t, :], rows).then_inc(s_vi[WT * b + t], 16)
            for c in range(3, 10):
                if c >= NCB:
                    sp.wait_ge(s_fc2c, c - NCB + 1)
                sp.dma_start(chunk_at[c % NCB], w["fc2_w"][c]).then_inc(s_str[c % NCB], 16)
            for b in range(B):
                for t in range(WT):
                    sp.wait_ge(s_i2e, WT * b + t + 1)
                    rows = w["bounce"][1, b].rearrange("s w c -> (s w) c")[t * P:(t + 1) * P, :]
                    sp.dma_start(rows, U[b][:, t, :]).then_inc(s_uo[b], 16)
                sp.wait_ge(s_uo[b], 32 * WT)
                for t in range(WT):
                    sp.dma_start(V[b][:, t, :], w["bounce"][1, b, :, t, :]).then_inc(s_vi[WT * b + t], 16)
            sp.wait_ge(s_x_new, 16)
            sp.dma_start(qkvw, w["qkv_w"].rearrange("(k p) c -> p k c", p=P)).then_inc(s_w2, 16)
            sp.dma_start(pwm.rearrange("p t m -> p (t m)"), w["pointwise_w"]).then_inc(s_w2b, 16)
            sp.dma_start(projw, w["proj_w"].rearrange("(k p) c -> p k c", p=P)).then_inc(s_w2b, 16)
            sp.dma_start(head_cols, w["head_cols"]).then_inc(s_w2b, 16)
            sp.dma_start(head_rows, w["head_rows"]).then_inc(s_w2b, 16)
            sp.wait_ge(s_x_new, 24)
            sp.dma_start(pw3w, w["pw3_w"].rearrange("(k p) c -> p k c", p=P)).then_inc(s_w3, 16)
            for n, i in enumerate((0, 2, 1, 3)):
                h, b = divmod(i, 2)
                sp.wait_ge(s_x_new, 24 + n + 1)
                sp.dma_start(out[b, h * P:(h + 1) * P], X[:, h, b, :]).then_inc(s_out, 16)
            sp.wait_ge(s_out, 64)

        @block.tensor
        def _(pe):
            def group_means(layer):
                pe.wait_ge(s_gn_stats, layer + 1)
                pe.matmul(psum[:, 7, 0:8], gmean, small[:, 56:64], start=True, stop=True).then_inc(s_gn_means, 1)

            pe.wait_ge(s_const, 80)
            group_means(0)
            pe.wait_ge(s_zc, 4)
            pe.wait_ge(s_w0, 112)
            for n in range(8):
                for u in range(2):
                    for k in range(HALVES):
                        lhs = Zc[:, 2 * k:2 * k + 2, :].rearrange("p b q -> p (b q)")[:, 2 * n + u::XX]
                        m = pe.matmul(psum[:, n, u * C:(u + 1) * C], lhs, inw[:, k], start=(k == 0 and u == 0),
                                      stop=(k == 1), skip_group_check=True)
                m.then_inc(s_xp, 1)
            for t in range(8):
                if t == 0:
                    pe.wait_ge(s_x1, 2)
                    pe.wait_ge(s_xpe, 8)
                for u in range(2):
                    for k in range(HALVES):
                        m = pe.transpose(psum[:, t, u * C + k * P:u * C + (k + 1) * P],
                                         x1cm[:, k, 2 * t + u::XX], ident)
                m.then_inc(s_x1t, 1)
            for t in range(8):
                q, k = divmod(t, 2)
                pe.wait_ge(s_x1n, 4 * (q + 1))
                for u in range(4):
                    m = pe.transpose(psum[:, t, u * P:(u + 1) * P], x1n[:, 4 * q + u, k * P:(k + 1) * P], ident)
                m.then_inc(s_back, 1)
            for t in range(XX):
                pe.wait_ge(s_g1, max(2 * (t // 4 + 1), t % 8 + 1))
                if t >= 8:
                    pe.wait_ge(s_ome, t - 7)
                for k in range(HALVES):
                    m = pe.matmul(psum[:, t % 8, 0:NOM], g1cm[:, k, t, :], omw[:, k], start=(k == 0), stop=(k == 1))
                m.then_inc(s_om, 1)
            pe.wait_ge(s_ome, XX)
            opened = set()
            for n in range(9):
                ky, kx = divmod(n, 3)
                pe.wait_ge(s_wk, n + 1)
                for i in range(3):
                    for j in range(3):
                        bank, at = divmod((kx + i) * ND + ky + j, 4)
                        m = pe.matmul(psum[:, bank, at * XG:(at + 1) * XG], ident, wk[n % 2][:, (3 * i + j) * XG:(3 * i + j + 1) * XG],
                                      start=(bank not in opened), stop=(n == 8), skip_group_check=True)
                        opened.add(bank)
                m.then_inc(s_wka, 1)
            pe.wait_ge(s_wd[0], 2)
            for n, (hf, j, i) in enumerate(plan):
                first, last = n % (ND * ND) == 0, n % (ND * ND) == ND * ND - 1
                if by_pool[n]:
                    pe.wait_ge(s_pp, upto_pool[n])
                else:
                    pe.wait_ge(s_pd, upto_dve[n])
                for xx in range(XX):
                    m = pe.matmul(psum[:, 4 * hf + xx // 4, xx % 4 * P:(xx % 4 + 1) * P], prods[n % NB][:, xx * P:(xx + 1) * P],
                                  ident, start=(first and xx % 4 == 0), stop=last, is_transpose=True, skip_group_check=True)
                m.then_inc(s_acc, 1)
            pe.wait_ge(s_outT, 8)
            for t in range(8):
                mh, q = divmod(t, 4)
                for k in range(HALVES):
                    m = pe.matmul(psum[:, t, :], outw[:, k, mh * P:(mh + 1) * P],
                                  outT[:, k, 4 * q:4 * q + 4, :], start=(k == 0), stop=(k == 1))
                m.then_inc(s_op, 1)

            group_means(1)
            pe.wait_ge(s_zc, 8)
            pe.wait_ge(s_w1, 64)
            z2 = Zc1.rearrange("p (k b) q -> p k (b q)", k=2)
            for c in range(CHUNKS):
                for k in range(HALVES):
                    m = pe.matmul(psum[:, c, :], fc1w[:, k], z2[:, k, c * BANK:(c + 1) * BANK], start=(k == 0), stop=(k == 1))
                m.then_inc(s_fc1, 1)
            for c in range(CHUNKS):
                pe.wait_ge(s_fc1r, c + 1)
                pe.matmul(psum[:, 4 + c, :], convw, sr_act[:, c * BANK:(c + 1) * BANK], start=True, stop=True).then_inc(s_cv, 1)
            for i in range(TILES + 3):
                if i < TILES:
                    if i < 4:
                        pe.wait_ge(s_fc1r, i + 1)
                    else:
                        pe.wait_ge(s_pw1r, i - 3)
                    b, t = divmod(i, WT)
                    for k in range(HALVES):
                        m = pe.matmul(psum[:, i % 4, :], Zc1[:, 2 * k + b, t::WT], pw1w[:, k], start=(k == 0), stop=(k == 1))
                    m.then_inc(s_pw1, 1)
                if i >= 3:
                    n = i - 3
                    pe.wait_ge(s_xpd, n + 1)
                    if n < 4:
                        pe.wait_ge(s_cvr, 4)
                    else:
                        pe.wait_ge(s_f1e, n - 3)
                    pe.matmul(psum[:, 4 + n % 4, :], dft[:, 0], xp[:, n, :], start=True, stop=True).then_inc(s_f1, 1)
            pe.wait_ge(s_z, 8)
            pe.wait_ge(s_zb, 2)
            pe.wait_ge(s_w1b, 64)
            pe.wait_ge(s_pw1r, TILES)
            def fc2_chunk(c):
                pe.wait_ge(s_str[c % NCB], 16 * (c // NCB + 1))
                for f in range(NF):
                    m = pe.matmul(psum[32 * f:32 * (f + 1), 4, :], means[:, c, :], chunk_at[c % NCB][:, f * MED:(f + 1) * MED],
                                  start=(c == 0), stop=(c == 9))
                m.then_inc(s_fc2c, 1)

            for c in range(CHUNKS):
                b, yh = divmod(c, 2)
                for k in range(HALVES):
                    for tap in range(9):
                        dy, dx = divmod(tap, 3)
                        y0 = PAD - 1 + dy + 16 * yh
                        m = pe.matmul(psum[:, c, :], sp1w[:, k, tap], Z[:, 2 * k + b, y0:y0 + 16, PAD - 1 + dx:PAD - 1 + dx + W],
                                      start=(k == 0 and tap == 0), stop=(k == 1 and tap == 8))
                m.then_inc(s_sp, 1)
                if c == 0:
                    pe.wait_ge(s_rmean, 1)
                    pe.wait_ge(s_f1e, TILES)
                    fc2_chunk(0)

            def spectrum(i):
                b, t = divmod(i, WT)
                sel = 1 if t == 0 else 2
                pe.wait_ge(s_vi[i], 16)
                if i >= 2:
                    pe.wait_ge(s_f2e, i - 1)
                pe.matmul(psum[:, 2 * (i % 2), :], dft[:, sel], V[b][:, t, :], start=True, stop=True)
                pe.matmul(psum[:, 2 * (i % 2) + 1, :], dft[:, sel + 2], V[b][:, t, :], start=True, stop=True).then_inc(s_f2, 1)

            pe.wait_ge(s_spr, 4)
            for i in range(3):
                spectrum(i)
            pe.wait_ge(s_u, 1)
            for c in range(1, 10):
                if c == NCB + 1:
                    spectrum(3)
                fc2_chunk(c)
            pe.wait_ge(s_lgc, 1)
            for km in range(KM):
                m = pe.transpose(psum[:, 5, km * P:(km + 1) * P], lg_rows[:, km * P:(km + 1) * P], ident)
            m.then_inc(s_lgt, 1)
            for i in range(4, NS):
                spectrum(i)
            pe.wait_ge(s_rd, 1)
            for n in range(KM * 4):
                km, r_ = divmod(n, 4)
                m = pe.transpose(psum[0:PARTS * NF, 4 + r_, km * P:(km + 1) * P], rparts[:, n].rearrange("p g f -> p (g f)"), ident)
            m.then_inc(s_rt, 1)
            def spatial_weight(i):
                b, t = divmod(i, WT)
                pe.wait_ge(s_f2e, TILES)
                if i >= 2:
                    pe.wait_ge(s_xw, i - 1)
                pe.matmul(psum[:, i % 2, :], filters[:, 2 * PIX + t * P:2 * PIX + (t + 1) * P], route[:, 2 + b, :],
                          start=True, stop=True).then_inc(s_sw, 1)

            for i in range(TILES + 1):
                if i < TILES:
                    b, t = divmod(i, WT)
                    if i == 0:
                        pe.wait_ge(s_rtc, 2)
                        pe.wait_ge(s_fil, 1)
                    else:
                        pe.wait_ge(s_ya, i)
                        pe.wait_ge(s_yb, i)
                    pe.matmul(psum[:, 4, :], filters[:, t * P:(t + 1) * P], route[:, b, :], start=True, stop=True)
                    pe.matmul(psum[:, 5, :], filters[:, PIX + t * P:PIX + (t + 1) * P], route[:, b, :], start=True, stop=True).then_inc(s_wri, 1)
                    if i + NS < TILES:
                        spectrum(i + NS)
                    if i >= TILES - 2:
                        spatial_weight(i - TILES + 2)
                if i >= 1:
                    n = i - 1
                    pe.wait_ge(s_y, n + 1)
                    if n >= 2:
                        pe.wait_ge(s_i2e, n - 1)
                    pe.matmul(psum[:, 6 + n % 2, :], dft[:, 5 if n % WT == 0 else 6], y_w[n % 2], start=True, stop=True).then_inc(s_i2, 1)
            for i in range(TILES + 1):
                if 2 <= i < TILES:
                    spatial_weight(i)
                if i >= 1:
                    n = i - 1
                    b, t = divmod(n, WT)
                    pe.wait_ge(s_vi[n], 32)
                    pe.wait_ge(s_xw, n + 1)
                    if n < 2:
                        pe.wait_ge(s_yb, TILES)
                    else:
                        pe.wait_ge(s_o1e, n - 1)
                    for k in range(KM):
                        pe.matmul(psum[:, 2 + n % 2, k * P:(k + 1) * P], V[b][:, t, k * P:(k + 1) * P], dft[:, 7],
                                  start=(k == 0), stop=False, skip_group_check=True)
                    for k in range(KM):
                        m = pe.matmul(psum[:, 2 + n % 2, k * P:(k + 1) * P], xp[:, n, k * P:(k + 1) * P], ident,
                                      start=False, stop=True, is_transpose=True, skip_group_check=True)
                    m.then_inc(s_o1, 1)
                    if n % 4 == 3:
                        pe.wait_ge(s_o1e, n + 1)
                        pe.wait_ge(s_i2e, TILES)
                        for mh in range(HALVES):
                            j = n // 4 * 2 + mh
                            if j >= 4:
                                pe.wait_ge(s_x_new, 8 + j - 3)
                            for k in range(KM):
                                m = pe.matmul(psum[:, 4 + j % 4, :], pw2w[:, k, mh * P:(mh + 1) * P],
                                              OT[b][:, k, t - 3:t + 1, :], start=(k == 0), stop=(k == KM - 1))
                            m.then_inc(s_p2, 1)

            group_means(2)
            pe.wait_ge(s_zc, 12)
            pe.wait_ge(s_w2, 16)
            z2 = Zc2.rearrange("p (k b) q -> p k (b q)", k=2)
            for i in range(QKV_TILES * CHUNKS):
                t, c = Q_ORDER[i // CHUNKS], i % CHUNKS
                if i >= 4:
                    pe.wait_ge(s_qp, i - 3)
                    pe.wait_ge(s_qf, i - 3)
                for k in range(HALVES):
                    m = pe.matmul(psum[:, i % 4, :], qkvw[:, k, t * P:(t + 1) * P], z2[:, k, c * BANK:(c + 1) * BANK],
                                  start=(k == 0), stop=(k == 1))
                m.then_inc(s_qkv, 1)

            def key_value_products(src, tiles):
                for i in range(TILES + 1):
                    if i < TILES:
                        b, t = divmod(i, WT)
                        n = src * TILES + i
                        if n >= 2:
                            pe.wait_ge(s_trc, n - 1)
                        for u in range(4):
                            m = pe.transpose(psum[:, 4 + n % 2, u * P:(u + 1) * P], tiles[u][:, i * P:(i + 1) * P], ident)
                        m.then_inc(s_tr, 1)
                    if i >= 1:
                        b, t = divmod(i - 1, WT)
                        n = src * TILES + i - 1
                        pe.wait_ge(s_trc, n + 1)
                        if src and t == 0:
                            pe.wait_ge(s_vkm, 2)
                        for gr in range(2):
                            tk, tv = 2 * gr, 2 * gr + 1
                            m = pe.matmul(psum[:, 6 + b, gr * P:(gr + 1) * P], turned[n % 2][:, tk * P:(tk + 1) * P],
                                          turned[n % 2][:, tv * P:(tv + 1) * P], start=(t == 0 and gr == 0), stop=(t == WT - 1),
                                          skip_group_check=True)
                        m.then_inc(s_vk, 1)

            def denominators(src, queries):
                pe.wait_ge(s_dnw, src + 1)
                for c in range(2):
                    for b in range(B):
                        for gr in range(2):
                            j = 2 * gr + b
                            m = pe.matmul(psum[32 * j:32 * j + 32, c, :], denw[:, src, b, gr, :],
                                          queries[gr][:, b * PIX + c * BANK:b * PIX + (c + 1) * BANK], start=True, stop=True)
                    m.then_inc(s_den, 1)

            def numerator(src, queries, s_):
                b, c, gr = ATTEND_ORDER[s_]
                n = 8 * src + s_
                if n >= 2:
                    pe.wait_ge(s_ns, n - 1)
                pe.matmul(psum[:, 2 + n % 2, :], vkm[:, src, b, gr, :], queries[gr][:, b * PIX + c * BANK:b * PIX + (c + 1) * BANK],
                          start=True, stop=True).then_inc(s_num, 1)

            def spread(src, s_):
                b, c, gr = ATTEND_ORDER[s_]
                n, j = 8 * src + s_, 2 * gr + b
                if s_ == 0:
                    pe.wait_ge(s_rc, src + 1)
                if n >= 2:
                    pe.wait_ge(s_att, n - 1)
                pe.matmul(psum[:, 4 + n % 2, :], head_rows[32 * j:32 * j + 32, :],
                          rden[32 * j:32 * j + 32, c * BANK:(c + 1) * BANK], start=True, stop=True).then_inc(s_rb, 1)

            def local_taps(a):
                t = Y_ORDER[a]
                if t == QKV_TILES - 1:
                    pe.wait_ge(s_pwt, 1)
                for c in range(CHUNKS):
                    if a:
                        pe.wait_ge(s_yqe, min(4 * a + c - 3, local_free[a]))
                    else:
                        pe.wait_ge(s_pwm, 1)
                    b, yh = divmod(c, 2)
                    for tap in range(TENSOR_TAPS[t]):
                        dy, dx = divmod(tap, 5)
                        pe.matmul(psum[:, y_bank[a] + c, :], pwt[t][:, tap, :], padq[:, t, b, dy + 16 * yh:dy + 16 * yh + 16, dx:dx + W],
                                  start=(tap == 0), stop=False)

            def local_rest(a):
                t = Y_ORDER[a]
                if t in POOL_TILES:
                    pe.wait_ge(s_ta, len([p for p in pool_taps if p[0] <= t]))
                else:
                    pe.wait_ge(s_dwd, 2 * (DVE_TILES.index(t) + 1))
                for c in range(CHUNKS):
                    pe.matmul(psum[:, y_bank[a] + c, :], pwm[:, t, :], local[t][:, c * BANK:(c + 1) * BANK],
                              start=False, stop=True).then_inc(s_yq, 1)

            pe.wait_ge(s_qf, 24)
            pe.wait_ge(s_qp, 24)
            key_value_products(0, flat[0:4])
            pe.wait_ge(s_w2b, 64)
            denominators(0, flat[4:6])
            pe.wait_ge(s_vkm, 2)
            for s_ in range(2):
                numerator(0, flat[4:6], s_)
            local_taps(0)
            local_rest(0)
            pe.wait_ge(s_yqe, 4)
            for s_ in range(8):
                if s_ >= 2:
                    numerator(0, flat[4:6], s_)
                spread(0, s_)
            pe.wait_ge(s_ns, 8)
            for a in range(1, 4):
                local_taps(a)
                local_rest(a)
            pe.wait_ge(s_att, 8)
            local_taps(4)
            local_taps(5)
            local_rest(4)
            local_rest(5)
            pe.wait_ge(s_yqe, 24)
            denominators(1, local[4:6])
            key_value_products(1, local[0:4])
            pe.wait_ge(s_vkm, 4)
            for s_ in range(8):
                numerator(1, local[4:6], s_)

            def spread_pair(c):
                for s_ in (2 * c, 2 * c + 1):
                    spread(1, s_)

            def project(c, ks):
                for mh in range(HALVES):
                    i = 2 * c + mh
                    if 0 in ks and i >= 4:
                        pe.wait_ge(s_pje, i - 3)
                    for k in ks:
                        m = pe.matmul(psum[:, i % 4, :], projw[:, k, mh * P:(mh + 1) * P], att[k][:, c * BANK:(c + 1) * BANK],
                                      start=(k == 0), stop=(k == 3))
                    if 3 in ks:
                        m.then_inc(s_pj, 1)

            pe.wait_ge(s_rc, 2)
            project(0, (0, 1))
            spread_pair(0)
            pe.wait_ge(s_ns, 16)
            project(1, (0, 1))
            for c in range(4):
                if c < 3:
                    spread_pair(c + 1)
                pe.wait_ge(s_att, 8 + 2 * (c + 1))
                project(c, (2, 3))
                if 1 <= c < 3:
                    project(c + 1, (0, 1))
            group_means(3)
            pe.wait_ge(s_z, 12)
            pe.wait_ge(s_zb, 3)
            pe.wait_ge(s_d3, 1)
            for c in range(2):
                for tap in range(9):
                    dy, dx = divmod(tap, 3)
                    y0 = PAD - 1 + dy + 16 * c
                    m = pe.matmul(psum[:, c, :], tap3[:, tap, :], Z[:, 3, y0:y0 + 16, PAD - 1 + dx:PAD - 1 + dx + W],
                                  start=(tap == 0), stop=(tap == 8))
            m.then_inc(s_dw3t, 1)
            pe.wait_ge(s_w3, 16)
            for b in range(B):
                pe.wait_ge(s_kept, 2 * (b + 1))
                for mh in range(HALVES):
                    for c in range(2):
                        for k in range(HALVES):
                            m = pe.matmul(psum[:, (2 + 4 * b + 2 * mh + c) % 8, :], pw3w[:, k, mh * P:(mh + 1) * P],
                                          h3[:, 2 * k + b, c * BANK:(c + 1) * BANK], start=(k == 0), stop=(k == 1))
                    m.then_inc(s_pw3, 1)

        @block.vector
        def _(dve):
            v = nc.vector
            me = Steps(dve, s_dve)

            def moments(chunks):
                for i, c in chunks:
                    n = me.add(v.bn_stats(st[:, i, c, :], X.rearrange("p h b q -> p (h b) q")[:, i, c * BANK:(c + 1) * BANK]))
                return n

            ALL_CHUNKS = [(i, c) for i in range(4) for c in range(2)]

            def group_norm(layer, missing=ALL_CHUNKS):
                me.upto(moments(missing))
                for i in range(4):
                    n = me.add(v.bn_aggr(mv[:, i, :], st[:, i, :, :]))
                me.upto(n)
                me.link(v.tensor_tensor(gq[:, 1, :], mv[:, :, 0], mv[:, :, 0], ALU.mult))
                me.link(v.tensor_tensor(gq[:, 1, :], gq[:, 1, :], mv[:, :, 1], ALU.add))
                v.tensor_copy(gq[:, 0, :], mv[:, :, 0]).then_inc(s_gn_stats, 1)
                dve.wait_ge(s_gn_means, layer + 1)
                me.link(v.tensor_copy(small[:, 64:72], psum[:, 7, 0:8]))
                me.link(v.tensor_tensor(gt, gm[:, 0, :], gm[:, 0, :], ALU.mult))
                v.scalar_tensor_tensor(gvar, gm[:, 1, :], GN_EPS, gt, ALU.add, ALU.subtract).then_inc(s_gn_var, 1)
                dve.wait_ge(s_gn_sd, layer + 1)
                me.link(v.reciprocal(grs, gsd))
                newton(grs, gvar, gt)
                v.scalar_tensor_tensor(gnb, gm[:, 0, :], -1.0, grs, ALU.mult, ALU.mult).then_inc(s_gn_coef, 1)
                dve.wait_ge(s_gn_coef, layer + 1)
                if layer in (1, 2):
                    for i in (0, 2):
                        v.tensor_scalar((Zc1, Zc2)[layer - 1][:, i], X.rearrange("p h b q -> p (h b) q")[:, i], grs[:, i:i + 1],
                                        gnb[:, i:i + 1], ALU.mult, ALU.add).then_inc(s_zc, 1)
                if layer == 2:
                    return
                for i in range(4) if layer < 3 else (0, 2):
                    v.tensor_scalar(z_inner(i), Xi[:, i], grs[:, i:i + 1], gnb[:, i:i + 1], ALU.mult, ALU.add).then_inc(s_z, 1)

            def newton(r, var, t):
                me.link(v.tensor_tensor(t, r, r, ALU.mult))
                me.link(v.scalar_tensor_tensor(t, t, -0.5, var, ALU.mult, ALU.mult))
                me.link(v.scalar_tensor_tensor(r, t, 1.5, r, ALU.add, ALU.mult))

            dve.wait_ge(s_x, 64)
            dve.wait_ge(s_const, 80)
            group_norm(0)
            v.tensor_scalar(bnv, col("bn_v", 0, 6), GN_EPS, None, ALU.add).then_inc(s_bnv, 1)
            dve.wait_ge(s_z, 4)
            dve.wait_ge(s_zb, 1)
            dve.wait_ge(s_w0, 112)
            dve.wait_ge(s_bnsd, 1)
            me.link(v.reciprocal(bn_inv, bnsd))
            newton(bn_inv, bnv, bnt)
            me.link(v.tensor_tensor(bn_inv, bn_inv, col("bn_g", 0, 6), ALU.mult))
            me.link(v.tensor_tensor(bn_off, col("bn_m", 0, 6), bn_inv, ALU.mult))
            me.link(v.tensor_tensor(bn_off, col("bn_b", 0, 6), bn_off, ALU.subtract))
            me.link(v.tensor_tensor(bnt[:, 0:4], col("l3_b", 0, 4), bn_inv[:, 2:6], ALU.mult))
            v.tensor_tensor(bn_off[:, 2:6], bn_off[:, 2:6], bnt[:, 0:4], ALU.add).then_inc(s_bn, 1)

            def depthwise3(k, tap):
                dy, dx = divmod(tap, 3)
                for b in range(B):
                    src = Z[:, 2 * k + b, PAD - 1 + dy:PAD - 1 + dy + H, PAD - 1 + dx:PAD - 1 + dx + W]
                    dst = x1cm[:, k, b * PIX:(b + 1) * PIX].rearrange("p (y x) -> p y x", y=H)
                    wt = col("dw0_w", k * 9 + tap)
                    if tap == 0:
                        ins = v.tensor_scalar(dst, src, wt, col("dw0_b", k), ALU.mult, ALU.add)
                    else:
                        ins = v.scalar_tensor_tensor(dst, src, wt, dst, ALU.mult, ALU.add)
                    n = me.add(ins)
                return n

            def evacuate_xproj(n):
                dve.wait_ge(s_xp, n + 1)
                v.tensor_tensor(XSc[:, PAD + 2 * n:PAD + 2 * n + 2, :], psum[:, n, :].rearrange("p (x c) -> p x c", c=C),
                                inb.unsqueeze(1).to_broadcast([P, 2, C]), ALU.add).then_inc(s_xpe, 1)

            tap_done = [0, 0]
            for tap in range(max(DW_TAPS)):
                for k in range(HALVES):
                    if tap >= DW_TAPS[k]:
                        continue
                    if tap:
                        me.upto(tap_done[k])
                    tap_done[k] = depthwise3(k, tap)
                if 1 <= tap <= 4:
                    for n in range(2 * tap - 2, 2 * tap):
                        evacuate_xproj(n)
            for k in range(HALVES):
                me.upto(tap_done[k])
                dve.wait_ge(s_dwa, rest_sums[k])
                v.tensor_tensor(x1cm[:, k], x1cm[:, k], x1_rest[:, k], ALU.add).then_inc(s_x1, 1)
            tiles = psum[:].rearrange("p t (u c) -> p (t u) c", c=C)
            for t in range(XX):
                dve.wait_ge(s_x1t, t // 2 + 1)
                n = me.add(v.bn_stats(ln_st[:, t, :], tiles[:, t, :]))
            me.upto(n)
            for t in range(XX):
                n = me.add(v.bn_aggr(ln_mv[:, t, :], ln_st[:, t, :]))
            me.upto(n)
            v.tensor_scalar(ln_var, ln_mv[:, :, 1], GN_EPS, None, ALU.add).then_inc(s_lnv, 1)
            dve.wait_ge(s_lnsd, 1)
            me.link(v.reciprocal(ln_rs, ln_sd))
            newton(ln_rs, ln_var, ln_t)
            me.link(v.scalar_tensor_tensor(ln_nb, ln_mv[:, :, 0], -1.0, ln_rs, ALU.mult, ALU.mult))
            for t in range(XX):
                v.tensor_scalar(x1n[:, t, :], tiles[:, t, :], ln_rs[:, t:t + 1], ln_nb[:, t:t + 1],
                                ALU.mult, ALU.add).then_inc(s_x1n, 1)
            logits = OM[:, :, 2 * G * K2:].rearrange("p x (h g k) -> p h x g k", h=2, k=K2)
            for part in range(2):
                xs = slice(8 * part, 8 * part + 8)
                for t in range(8 * part, 8 * part + 8):
                    dve.wait_ge(s_om, t + 1)
                    v.tensor_tensor(OM[:, t, :], psum[:, t % 8, 0:NOM], omb, ALU.add).then_inc(s_ome, 1)
                dve.wait_ge(s_ome, 8 * (part + 1))
                me.add(v.tensor_reduce(amax_part[:, part:part + 1], OM[:, xs, 0:2 * G * K2], AX.XY, ALU.max, apply_absolute_value=True))
                for hf in range(2):
                    n = me.add(v.tensor_reduce(sm_t[:, hf].rearrange("p (x g) -> p x g", g=GH)[:, xs], logits[:, hf, xs], AX.X, ALU.max))
                me.upto(n)
                if part == 1:
                    v.tensor_tensor(amax, amax_part[:, 0:1], amax_part[:, 1:2], ALU.max).then_inc(s_amax, 1)
                for hf in range(2):
                    v.tensor_tensor(mask_x[:, hf, :, xs], logits[:, hf, xs].rearrange("p x g k -> p k x g"),
                                    sm_t[:, hf].rearrange("p (x g) -> p x g", g=GH)[:, xs].unsqueeze(1).to_broadcast([P, K2, 8, GH]),
                                    ALU.subtract).then_inc(s_lgs, 1)
            for hf in range(2):
                dve.wait_ge(s_exp, hf + 3)
                me.link(v.tensor_reduce(sm_r[:, hf], mask[:, hf].rearrange("p k g -> p g k"), AX.X, ALU.add))
                me.link(v.reciprocal(sm_t[:, hf], sm_r[:, hf]))
                v.tensor_tensor(mask[:, hf], mask[:, hf], sm_t[:, hf].unsqueeze(1).to_broadcast([P, K2, XG]), ALU.mult).then_inc(s_mask, 1)
            dve.wait_ge(s_mask, 2)

            dve.wait_ge(s_hat[0], 1)
            dve.wait_ge(s_general, 1)
            for ky in range(3):
                n = me.add(v.scalar_tensor_tensor(hats[:, 3 + ky], hats[:, 3 + ky], within, mask[:, 0], ALU.mult, ALU.mult))
            me.upto(n)
            for n in range(9):
                ky, kx = divmod(n, 3)
                if n >= 2:
                    dve.wait_ge(s_wka, n - 1)
                v.tensor_tensor(wk[n % 2], hats[:, 3 + ky].rearrange("p k g -> p (k g)"),
                                hats[:, kx].rearrange("p k g -> p (k g)"), ALU.mult).then_inc(s_wk, 1)
            dve.wait_ge(s_wka, 9)
            v.tensor_copy(Wd.rearrange("p i j g -> p (i j g)")[:, COLS:], psum[:, 4:8, :].rearrange("p t q -> p (t q)")[:, 0:ND * ND * XG - COLS]).then_inc(s_wd[0], 1)
            for n in range(len(plan)):
                if not by_pool[n]:
                    await_product_inputs(dve, n)
                    product(v, n).then_inc(s_pd, 1)
            for t in range(8):
                mh, q = divmod(t, 4)
                if t == 5:
                    dve.wait_ge(s_x_new, 4)
                    moments(ALL_CHUNKS[0:4])
                dve.wait_ge(s_op, t + 1)
                xv = X[:, mh].rearrange("p b (r x) -> p x (b r)", x=XX)[:, 4 * q:4 * q + 4, :]
                v.scalar_tensor_tensor(xv, psum[:, t, :].rearrange("p (x r) -> p x r", x=4), col("out_b", mh), xv,
                                       ALU.add, ALU.add).then_inc(s_x_new, 1)

            dve.wait_ge(s_x_new, 8)
            group_norm(1, ALL_CHUNKS[4:8])
            for i in range(TILES):
                if i == 0:
                    me.link(v.memset(means, 0.0))
                dve.wait_ge(s_pw1r, i + 1)
                v.tensor_tensor(xp[:, i, :], xp[:, i, :], xp[:, i, :], ALU.mult).then_inc(s_sq, 1)
                if i == 3:
                    dve.wait_ge(s_cvr, 4)
                    me.link(v.tensor_tensor(means[:, 0, 0:2], racc[:, 0:4:2], racc[:, 1:4:2], ALU.add))
                    v.tensor_scalar(means[:, 0, 0:2], means[:, 0, 0:2], 1.0 / PIX, None, ALU.mult).then_inc(s_rmean, 1)
            dve.wait_ge(s_cwe, 1)
            dve.wait_ge(s_w1b, 64)
            dve.wait_ge(s_pw1, TILES)
            for j in range(2):
                me.link(v.tensor_copy(filters, filters32))
                me.link(v.scalar_tensor_tensor(filters32, filters, part_mask[:, j:j + 1], filters32, ALU.mult, ALU.add))
            v.tensor_copy(filters, filters32).then_inc(s_fil, 1)
            hidden = sr_act.rearrange("p (b y x) -> p b y x", b=B, y=H)
            span = [(0, 31), (0, 32), (1, 32)]
            for c in range(CHUNKS):
                b, yh = divmod(c, 2)
                rows = slice(16 * yh, 16 * yh + 16)
                dve.wait_ge(s_spr, c + 1)
                for dx, (lo, hi) in enumerate(span):
                    n = me.add(v.tensor_reduce(rsums[:, dx, b, rows], hidden[:, b, rows, lo:hi], AX.X, ALU.add))
            me.upto(n)
            for dy, (lo, hi) in enumerate(span):
                n = me.add(v.tensor_reduce(means[:, 1 + 3 * dy:4 + 3 * dy, 2:4], rsums[:, :, :, lo:hi], AX.X, ALU.add))
            me.upto(n)
            v.tensor_scalar(means[:, 1:, 2:4], means[:, 1:, 2:4], 1.0 / PIX, None, ALU.mult).then_inc(s_u, 1)
            dve.wait_ge(s_lgt, 1)
            turned_logits = psum[:, 5, :].rearrange("p (k f r) -> p f k r", k=KM, f=NF)[:, :, :, 0:4]
            me.link(v.tensor_tensor(logits1.rearrange("p f (k r) -> p f k r", k=KM), turned_logits,
                                    fc2b.rearrange("p f (k r) -> p f k r", k=KM), ALU.add))
            by_filter = logits1.rearrange("p f n -> p n f")
            me.link(v.tensor_reduce(lg_max, by_filter, AX.X, ALU.max))
            v.tensor_tensor(logits1, logits1, lg_max.unsqueeze(1).to_broadcast([P, NF, 16]), ALU.subtract).then_inc(s_rl, 1)
            dve.wait_ge(s_re, 1)
            me.link(v.tensor_reduce(lg_sum, by_filter, AX.X, ALU.add))
            me.link(v.reciprocal(lg_rec, lg_sum))
            me.link(v.tensor_tensor(logits1, logits1, lg_rec.unsqueeze(1).to_broadcast([P, NF, 16]), ALU.mult))
            for j in range(3):
                me.link(v.tensor_copy(rpart[j], logits1))
                if j < 2:
                    me.link(v.tensor_tensor(logits1, logits1, rpart[j], ALU.subtract))
            for g_, j in enumerate(ROUTE_PART):
                ins = v.tensor_copy(rparts[:, :, g_, :], rpart[j].rearrange("p f n -> p n f"))
                if g_ < PARTS - 1:
                    me.add(ins)
            ins.then_inc(s_rd, 1)
            dve.wait_ge(s_rt, 1)
            v.tensor_copy(route[:, 2:4, :], psum[0:PARTS * NF, 6:8, :]).then_inc(s_rtc, 1)
            for i in range(TILES):
                dve.wait_ge(s_f2e, i + 1)
                dve.wait_ge(s_wri, i + 1)
                if i >= 2:
                    dve.wait_ge(s_y, i - 1)
                v.tensor_tensor(ya[i % 2], spec[i % NS][:, 0], psum[:, 4, :], ALU.mult).then_inc(s_ya, 1)
                v.tensor_tensor(yb[i % 2], spec[i % NS][:, 1], psum[:, 5, :], ALU.mult).then_inc(s_yb, 1)

            def update_x1(m):
                b, q = divmod(m, 2)
                for mh in range(HALVES):
                    j = 2 * m + mh
                    dve.wait_ge(s_p2, j + 1)
                    xv = X[:, mh, b].rearrange("p (j o) -> p o j", o=WT)[:, 4 * q:4 * q + 4, :]
                    v.tensor_tensor(xv, psum[:, 4 + j % 4, :].rearrange("p (o j) -> p o j", o=4), xv, ALU.add).then_inc(s_x_new, 1)

            for i in range(TILES):
                dve.wait_ge(s_sw, i + 1)
                v.tensor_tensor(xp[:, i, :], xp[:, i, :], psum[:, i % 2, :], ALU.mult).then_inc(s_xw, 1)
                if i % 4 == 1 and i >= 5:
                    update_x1(i // 4 - 1)
                if i == TILES - 2:
                    dve.wait_ge(s_x_new, 12)
                    moments([(0, 0), (0, 1), (2, 0), (2, 1)])
            update_x1(3)

            dve.wait_ge(s_x_new, 16)
            group_norm(2, [(1, 0), (1, 1), (3, 0), (3, 1)])
            dve.wait_ge(s_w2b, 64)
            me.link(v.tensor_tensor(pwm, pwm, head_mask.unsqueeze(1).to_broadcast([P, QKV_TILES, P]), ALU.mult))
            for t in range(QKV_TILES - 1):
                for a_ in range(TENSOR_TAPS[t]):
                    ins = v.tensor_scalar(pwt[t][:, a_, :], pwm[:, t, :], col("dw2_w", t * K5 + a_), None, ALU.mult)
                    n = me.add(ins) if (t, a_) != (QKV_TILES - 2, TENSOR_TAPS[-2] - 1) else ins.then_inc(s_pwm, 1)

            def denominator_weights(src):
                me.link(v.tensor_tensor(ksum[:, src], kacc[:, src, :, 0:4:2], kacc[:, src, :, 1:4:2], ALU.add))
                for b in range(B):
                    for gr in range(2):
                        ins = v.tensor_scalar(denw[:, src, b, gr, :], head_cols, ksum[:, src, gr, b:b + 1], None, ALU.mult)
                        if (b, gr) != (1, 1):
                            me.add(ins)
                ins.then_inc(s_dnw, 1)

            def mask_products(src):
                for b in range(B):
                    dve.wait_ge(s_vk, src * TILES + WT * (b + 1))
                    v.tensor_tensor(vkm[:, src, b], psum[:, 6 + b, 0:2 * P].rearrange("p (g m) -> p g m", g=2),
                                    head_mask.unsqueeze(1).to_broadcast([P, 2, P]), ALU.mult).then_inc(s_vkm, 1)

            def invert_denominators(src):
                dve.wait_ge(s_den, 2 * src + 2)
                if src == 0:
                    dve.wait_ge(s_ta, EARLY_PRODUCTS)
                me.link(v.tensor_scalar(rden, psum[:, 0:2, :].rearrange("p c q -> p (c q)"), ATT_EPS, None, ALU.add))
                v.reciprocal(rden, rden).then_inc(s_rc, 1)

            def divide(src, s_):
                b, c, gr = ATTEND_ORDER[s_]
                n = 8 * src + s_
                dve.wait_ge(s_ns, n + 1)
                dve.wait_ge(s_rb, n + 1)
                v.tensor_tensor(att[2 * src + gr][:, b * PIX + c * BANK:b * PIX + (c + 1) * BANK], (num_s1 if src else num_s)[s_ % (8 if src else 2)],
                                psum[:, 4 + n % 2, :], ALU.mult).then_inc(s_att, 1)

            for t in DVE_TILES:
                dve.wait_ge(s_qp, CHUNKS * (Q_ORDER.index(t) + 1))
                if t == 2:
                    dve.wait_ge(s_ta, EARLY_PRODUCTS)
                if t == 1:
                    dve.wait_ge(s_tr, TILES)
                if t == DVE_TILES[1]:
                    dve.wait_ge(s_qf, CHUNKS * (Q_ORDER.index(2) + 1))
                    denominator_weights(0)
                for tap in range(TENSOR_TAPS[t], K5):
                    if tap > TENSOR_TAPS[t]:
                        me.upto(tap_n)
                    tap_n = filter_tap(v, me, t, tap)
                    at = tap - TENSOR_TAPS[t]
                    if t == DVE_TILES[1] and at == MASK_AT:
                        mask_products(0)
                    if t == DVE_TILES[1] and at == INVERT_AT:
                        invert_denominators(0)
                    if t == DVE_TILES[1] and DIVIDE_AT <= at < DIVIDE_AT + 8:
                        divide(0, at - DIVIDE_AT)
            dve.wait_ge(s_yqe, 4 * (max(Y_ORDER.index(0), Y_ORDER.index(2)) + 1))
            denominator_weights(1)
            invert_denominators(1)
            mask_products(1)
            for j in range(5):
                if j < 4:
                    for s_ in (2 * j, 2 * j + 1):
                        divide(1, s_)
                if j >= 2:
                    b, q = divmod(j - 2, 2)
                    dve.wait_ge(s_x_new, 16 + 2 * (j - 1))
                    moments([(b, q), (2 + b, q)])
                if j >= 1:
                    b, q = divmod(j - 1, 2)
                    for mh in range(HALVES):
                        i = 2 * (j - 1) + mh
                        dve.wait_ge(s_pje, i + 1)
                        xv = X[:, mh, b, q * BANK:(q + 1) * BANK]
                        v.tensor_tensor(xv, xv, proj_s[i % 2], ALU.add).then_inc(s_x_new, 1)
            dve.wait_ge(s_x_new, 24)
            group_norm(3, [(1, 1), (3, 1)])
            for tap in range(9):
                ins = v.tensor_scalar(tap3[:, tap, :], ident, col("dw3_w", 9 + tap), None, ALU.mult)
                n = me.add(ins) if tap < 8 else ins.then_inc(s_d3, 1)
            dve.wait_ge(s_z, 12)
            dve.wait_ge(s_zb, 3)
            for tap in range(9):
                if tap:
                    me.upto(tap_n)
                for i in (0, 2):
                    tap_n = filter3(v, me, i, tap, s_dw3)

            def keep_flags(a_, i, data, thresh):
                me.link(v.tensor_reduce(pk[:, 2 * a_, i:i + 1], data, AX.X, ALU.max))
                me.link(v.tensor_scalar(pk[:, 2 * a_ + 1, i:i + 1], pk[:, 2 * a_, i:i + 1], thresh, None, ALU.is_ge))
                return pk[:, 2 * a_ + 1, i:i + 1]

            for a_, i in enumerate((0, 2, 1, 3)):
                dve.wait_ge(s_h3, a_ + 1)
                keep = keep_flags(0, i, h3[:, i, :], DW_THRESH)
                v.tensor_scalar(h3[:, i, :], h3[:, i, :], keep, None, ALU.mult).then_inc(s_kept, 1)
            for a_, i in enumerate((0, 2, 1, 3)):
                dve.wait_ge(s_o3, a_ + 1)
                keep = keep_flags(1, i, o3[:, i, :], PW_THRESH)
                xv = X.rearrange("p h b q -> p (h b) q")[:, i, :]
                v.scalar_tensor_tensor(xv, o3[:, i, :], keep, xv, ALU.mult, ALU.add).then_inc(s_x_new, 1)

        @block.scalar
        def _(act):
            a = nc.scalar

            warmed = [0]

            def load_table(function):
                a.activation(small[:, 448 + warmed[0]:449 + warmed[0]], hat_shift[:, 0:1], function)
                warmed[0] += 1

            def group_norm(layer, zc):
                load_table(ACT.Sqrt)
                act.wait_ge(s_gn_var, layer + 1)
                a.activation(gsd, gvar, ACT.Sqrt).then_inc(s_gn_sd, 1)
                if layer == 0:
                    act.wait_ge(s_bnv, 1)
                    a.activation(bnsd, bnv, ACT.Sqrt).then_inc(s_bnsd, 1)
                act.wait_ge(s_gn_coef, layer + 1)
                if zc is None:
                    for i in (1, 3):
                        a.activation(z_inner(i), Xi[:, i], ACT.Identity, scale=grs[:, i:i + 1], bias=gnb[:, i:i + 1]).then_inc(s_z, 1)
                    return
                for i in (0, 2, 1, 3) if layer == 0 else (1, 3):
                    a.activation(zc[:, i], X.rearrange("p h b q -> p (h b) q")[:, i], ACT.Identity, scale=grs[:, i:i + 1],
                                 bias=gnb[:, i:i + 1]).then_inc(s_zc, 1)

            act.wait_ge(s_const, 80)
            group_norm(0, Zc)
            act.wait_ge(s_z, 4)
            act.wait_ge(s_zb, 1)
            for n, (k, tap) in enumerate(rest_taps):
                dy, dx = divmod(tap, 3)
                if tap == DW_TAPS[k]:
                    dst = x1_rest[:, k]
                else:
                    dst = dw_tmp[n % 3]
                    if n >= 4:
                        act.wait_ge(s_dwa, sum(1 for k_, t_ in rest_taps[:n - 2] if t_ > DW_TAPS[k_]))
                for b in range(B):
                    ins = a.activation(dst[:, b * PIX:(b + 1) * PIX].rearrange("p (y x) -> p y x", y=H),
                                       Z[:, 2 * k + b, PAD - 1 + dy:PAD - 1 + dy + H, PAD - 1 + dx:PAD - 1 + dx + W],
                                       ACT.Copy, scale=col("dw0_w", 9 * k + tap))
                ins.then_inc(s_dwp, 1)
            load_table(ACT.Sqrt)
            act.wait_ge(s_lnv, 1)
            a.activation(ln_sd, ln_var, ACT.Sqrt).then_inc(s_lnsd, 1)
            load_table(ACT.Gelu)
            for t in range(8):
                q, k = divmod(t, 2)
                act.wait_ge(s_back, t + 1)
                a.activation(g1cm[:, k, 4 * q:4 * q + 4, :], psum[:, t, :].rearrange("p (x q) -> p x q", x=4), ACT.Gelu,
                             scale=col("ln_g", k), bias=col("ln_b", k)).then_inc(s_g1, 1)
            load_table(ACT.Exp)

            def exponentials(part):
                for hf in range(2):
                    act.wait_ge(s_lgs, 2 * part + hf + 1)
                    at = mask_x[:, hf, :, 8 * part:8 * part + 8]
                    a.activation(at, at, ACT.Exp).then_inc(s_exp, 1)

            offs = OM[:, :, 0:2 * G * K2].rearrange("p x (h g k a) -> p h a k x g", h=2, g=GH, k=K2)

            def hat_values(dst, at):
                at_dst = [dst[:, k].rearrange("p k (x g) -> p k x g", g=GH) for k in range(3)]
                a.activation(at_dst[1], at, ACT.Abs)
                a.activation(at_dst[0], at, ACT.Relu, scale=-1.0)
                a.activation(at_dst[2], at, ACT.Relu).then_inc(s_habs, 1)

            exponentials(0)
            act.wait_ge(s_om, XX)
            act.wait_ge(s_ome, XX)
            hat_values(hats[:, 0:3], offs[:, 0, 0])
            exponentials(1)
            hat_values(hats[:, 3:6], offs[:, 0, 1])
            for ax in range(2):
                act.wait_ge(s_habs, ax + 1)
                ins = a.activation(hats[:, 3 * ax + 1], hats[:, 3 * ax + 1], ACT.Identity, scale=-1.0, bias=hat_shift[:, 0:1])
            ins.then_inc(s_hat[0], 1)
            act.wait_ge(s_general, 1)
            offs1_x = wk1.rearrange("p (k x g) -> p k x g", k=K2, g=GH)
            a.activation(offs1_x, offs[:, 1, 0], ACT.Copy).then_inc(s_habs, 1)
            hat_values(hats1_y, offs[:, 1, 1])
            act.wait_ge(s_habs, 4)
            act.wait_ge(s_lgs, 4)
            act.wait_ge(s_amax, 1)
            hat_values(hats1_x, offs1_x)
            for ax, h_ in enumerate((hats1_y, hats1_x)):
                act.wait_ge(s_habs, ax + 4)
                ins = a.activation(h_[:, 1], h_[:, 1], ACT.Identity, scale=-1.0, bias=hat_shift[:, 0:1])
            ins.then_inc(s_hat[1], 1)
            act.wait_ge(s_wka, 9)
            a.activation(Wd.rearrange("p i j g -> p (i j g)")[:, 0:COLS], psum[:, 0:4, :].rearrange("p t q -> p (t q)"), ACT.Copy).then_inc(s_wd[0], 1)
            act.wait_ge(s_wd[0], 2)
            for hf in range(2):
                act.wait_ge(s_acc, ND * ND * (hf + 1))
                for q in range(4):
                    a.activation(outT[:, hf, 4 * q:4 * q + 4, :], psum[:, 4 * hf + q, :].rearrange("p (x q) -> p x q", x=4),
                                 ACT.Copy).then_inc(s_outT, 1)

            group_norm(1, Zc1)
            for c in range(CHUNKS):
                act.wait_ge(s_fc1, c + 1)
                a.activation(sr_act[:, c * BANK:(c + 1) * BANK], psum[:, c, :], ACT.Relu, bias=col("fc1_b")).then_inc(s_fc1r, 1)
            for c in range(CHUNKS):
                act.wait_ge(s_cv, c + 1)
                a.activation(sr_act[:, c * BANK:(c + 1) * BANK], psum[:, 4 + c, :], ACT.Relu, bias=col("conv_b"),
                             accum_out=racc[:, c:c + 1]).then_inc(s_cvr, 1)
            for i in range(TILES + 4):
                if i < TILES:
                    act.wait_ge(s_pw1, i + 1)
                    a.activation(xp[:, i, :], psum[:, i % 4, :], ACT.Relu).then_inc(s_pw1r, 1)
                if i >= 4:
                    n = i - 4
                    b, t = divmod(n, WT)
                    act.wait_ge(s_f1, n + 1)
                    if n == 0:
                        act.wait_ge(s_cwe, 1)
                    a.activation(U[b][:, t, :], psum[:, 4 + n % 4, :], ACT.Copy).then_inc(s_f1e, 1)
            for c in range(CHUNKS):
                act.wait_ge(s_sp, c + 1)
                if c == 0:
                    act.wait_ge(s_cvr, 4)
                a.activation(sr_act[:, c * BANK:(c + 1) * BANK], psum[:, c, :], ACT.Relu, bias=col("sp1_b")).then_inc(s_spr, 1)
            def copy_spectrum(i):
                act.wait_ge(s_f2, i + 1)
                if i >= NS:
                    act.wait_ge(s_ya, i - NS + 1)
                    act.wait_ge(s_yb, i - NS + 1)
                elif i == 2:
                    act.wait_ge(s_u, 1)
                a.activation(spec[i % NS], psum[:, 2 * (i % 2):2 * (i % 2) + 2, :], ACT.Copy).then_inc(s_f2e, 1)

            for i in range(4):
                copy_spectrum(i)
            act.wait_ge(s_fc2c, 10)
            a.activation(lg_rows, psum[:, 4, :], ACT.Copy).then_inc(s_lgc, 1)
            load_table(ACT.Exp)
            act.wait_ge(s_rl, 1)
            a.activation(logits1, logits1, ACT.Exp).then_inc(s_re, 1)
            for i in range(4, NS):
                copy_spectrum(i)
            act.wait_ge(s_rt, 1)
            a.activation(route[:, 0:2, :], psum[0:PARTS * NF, 4:6, :], ACT.Copy).then_inc(s_rtc, 1)
            for i in range(TILES + 2):
                if i + NS < TILES:
                    copy_spectrum(i + NS)
                if i >= 2:
                    n = i - 2
                    b, t = divmod(n, WT)
                    act.wait_ge(s_i2, n + 1)
                    if n == 0:
                        act.wait_ge(s_uo[0], 16 * WT)
                        act.wait_ge(s_uo[1], 16 * WT)
                    a.activation(U[b][:, t, :], psum[:, 6 + n % 2, :], ACT.Copy).then_inc(s_i2e, 1)
            for n in range(TILES):
                b, t = divmod(n, WT)
                act.wait_ge(s_o1, n + 1)
                if t == 0:
                    act.wait_ge(s_uo[b], 32 * WT)
                a.activation(OT[b][:, :, t, :], psum[:, 2 + n % 2, :].rearrange("p (k j) -> p k j", k=KM), ACT.Copy).then_inc(s_o1e, 1)

            group_norm(2, Zc2)
            made = [0]

            def tap_products(count):
                for n in range(made[0], min(count, len(pool_taps))):
                    t, tap, b = pool_taps[n]
                    act.wait_ge(s_qp, CHUNKS * (Q_ORDER.index(t) + 1))
                    if n >= 3:
                        act.wait_ge(s_ta, n - 2)
                    a.activation(tap_tmp(n).rearrange("p (y x) -> p y x", y=H), tap_view(t, tap, b), ACT.Copy,
                                 scale=col("dw2_w", t * K5 + tap)).then_inc(s_tp, 1)
                    made[0] = n + 1

            act.wait_ge(s_qb, 1)
            for i in range(QKV_TILES * CHUNKS):
                t, c = Q_ORDER[i // CHUNKS], i % CHUNKS
                b, yh = divmod(c, 2)
                act.wait_ge(s_qkv, i + 1)
                a.activation(padq[:, t, b, 2 + 16 * yh:18 + 16 * yh, 2:2 + W], psum[:, i % 4, :].rearrange("p (y x) -> p y x", y=16),
                             ACT.Copy).then_inc(s_qp, 1)
                dst = flat[t][:, c * BANK:(c + 1) * BANK]
                if t in (1, 3):
                    a.activation(dst, psum[:, i % 4, :], ACT.Copy).then_inc(s_qf, 1)
                elif t in (0, 2):
                    a.activation(dst, psum[:, i % 4, :], ACT.Relu, accum_out=kacc[:, 0, t // 2, c:c + 1]).then_inc(s_qf, 1)
                else:
                    a.activation(dst, psum[:, i % 4, :], ACT.Relu).then_inc(s_qf, 1)
                if i >= 9:
                    tap_products(min(i - 8, EARLY_PRODUCTS))

            def copy_turned(src, made=0):
                for i in range(TILES):
                    n = src * TILES + i
                    act.wait_ge(s_tr, n + 1)
                    if n >= 2:
                        act.wait_ge(s_vk, n - 1)
                    a.activation(turned[n % 2], psum[:, 4 + n % 2, :], ACT.Copy).then_inc(s_trc, 1)
                    if i % 2 == 1:
                        tap_products(made + i // 2)

            def copy_numerators(src, which=range(8), made=0):
                for s_ in which:
                    n = 8 * src + s_
                    act.wait_ge(s_num, n + 1)
                    if src == 0 and s_ >= 2:
                        act.wait_ge(s_att, s_ - 1)
                    a.activation((num_s1[s_] if src else num_s[s_ % 2]), psum[:, 2 + n % 2, :], ACT.Copy).then_inc(s_ns, 1)
                    if src == 0 and s_ >= 2:
                        tap_products(made + s_)

            def copy_local(tiles):
                for n_ in tiles:
                    t = Y_ORDER[n_]
                    for c in range(CHUNKS):
                        act.wait_ge(s_yq, 4 * n_ + c + 1)
                        bank = psum[:, y_bank[n_] + c, :]
                        dst = local[t][:, c * BANK:(c + 1) * BANK]
                        if t in (1, 3):
                            a.activation(dst, bank, ACT.Copy).then_inc(s_yqe, 1)
                        elif t in (0, 2):
                            a.activation(dst, bank, ACT.Relu, accum_out=kacc[:, 1, t // 2, c:c + 1]).then_inc(s_yqe, 1)
                        else:
                            a.activation(dst, bank, ACT.Relu).then_inc(s_yqe, 1)

            copy_turned(0, 16)
            act.wait_ge(s_pwm, 1)
            for tap in range(TENSOR_TAPS[-1]):
                ins = a.activation(pwt[-1][:, tap, :], pwm[:, QKV_TILES - 1, :], ACT.Copy, scale=col("dw2_w", (QKV_TILES - 1) * K5 + tap))
            ins.then_inc(s_pwt, 1)
            copy_numerators(0, range(2))
            tap_products(AHEAD)
            copy_local([0])
            copy_numerators(0, range(2, 8), AHEAD + BETWEEN)
            tap_products(46)
            copy_local([1])
            tap_products(54)
            copy_local([2])
            tap_products(68)
            copy_local([3])
            tap_products(len(pool_taps))
            copy_local([4])
            copy_local([5])
            copy_turned(1)
            copy_numerators(1)
            act.wait_ge(s_bn, 1)
            act.wait_ge(s_vk, 2 * TILES)
            for i in range(8):
                mh = i % 2
                act.wait_ge(s_pj, i + 1)
                if i >= 2:
                    act.wait_ge(s_x_new, 16 + i - 1)
                a.activation(proj_s[i % 2], psum[:, i % 4, :], ACT.Identity, scale=bn_inv[:, mh:mh + 1], bias=bn_off[:, mh:mh + 1]).then_inc(s_pje, 1)
            group_norm(3, None)
            act.wait_ge(s_z, 12)
            act.wait_ge(s_zb, 3)
            for tap in range(9):
                dy, dx = divmod(tap, 3)
                if tap >= 2:
                    act.wait_ge(s_dw3p, tap - 1)
                a.activation(tap3_tmp[tap % 2].rearrange("p (y x) -> p y x", y=H), Z[:, 1, PAD - 1 + dy:PAD - 1 + dy + H, PAD - 1 + dx:PAD - 1 + dx + W],
                             ACT.Copy, scale=col("dw3_w", tap)).then_inc(s_tp3, 1)
            for n, i in enumerate((0, 2, 1, 3)):
                h = i // 2
                scale, bias = bn_inv[:, 2 + h:3 + h], bn_off[:, 2 + h:3 + h]
                if i == 3:
                    act.wait_ge(s_dw3t, 1)
                    a.activation(h3[:, i, :].rearrange("p (c q) -> p c q", c=2), psum[:, 0:2, :], ACT.Relu, scale=scale, bias=bias).then_inc(s_h3, 1)
                else:
                    if i == 1:
                        act.wait_ge(s_dw3p, 9)
                    else:
                        act.wait_ge(s_dw3, n + 1)
                    a.activation(h3[:, i, :], h3[:, i, :], ACT.Relu, scale=scale, bias=bias).then_inc(s_h3, 1)
            for n, i in enumerate((0, 2, 1, 3)):
                h, b = divmod(i, 2)
                act.wait_ge(s_pw3, n + 1)
                bank = (2 + 4 * b + 2 * h) % 8
                a.activation(o3[:, i, :].rearrange("p (c q) -> p c q", c=2), psum[:, bank:bank + 2, :], ACT.Relu,
                             scale=bn_inv[:, 4 + h:5 + h], bias=bn_off[:, 4 + h:5 + h]).then_inc(s_o3, 1)

        @block.gpsimd
        def _(pool):
            g = nc.gpsimd
            me = Steps(pool, s_pool)

            def zero_border():
                g.memset(Z[:, :, 0:PAD, :], 0.0)
                g.memset(Z[:, :, PAD + H:, :], 0.0)
                g.memset(Z[:, :, PAD:PAD + H, 0:PAD], 0.0)
                return g.memset(Z[:, :, PAD:PAD + H, PAD + W:], 0.0)

            zero_border().then_inc(s_zb, 1)
            g.memset(XSc[:, 0:PAD], 0.0)
            g.memset(XSc[:, PAD + XX:], 0.0).then_inc(s_shz, 1)
            g.memset(XSd, 0.0).then_inc(s_shz, 1)
            added = 0
            for n, (k, tap) in enumerate(rest_taps):
                if tap == DW_TAPS[k]:
                    continue
                pool.wait_ge(s_dwp, n + 1)
                if added:
                    pool.wait_ge(s_dwa, added)
                g.tensor_tensor(x1_rest[:, k], x1_rest[:, k], dw_tmp[n % 3], ALU.add).then_inc(s_dwa, 1)
                added += 1
            pool.wait_ge(s_amax, 1)
            me.link(g.partition_all_reduce(amax_all, amax, P, bass.bass_isa.ReduceOp.max))
            me.add(g.tensor_scalar(within, amax_all, 1.0, None, ALU.is_le))
            me.link(g.tensor_scalar(beyond, amax_all, 1.0, None, ALU.is_gt))
            any_beyond = pool.value_load(beyond[0:1, 0:1], min_val=0, max_val=1)
            general_path(pool, g, any_beyond)
            g.memset(small[:, 442:443], 0.0).then_inc(s_general, 1)
            pool.wait_ge(s_mask, 2)
            me.link(g.tensor_scalar(mask[:, 1], mask[:, 1], within, None, ALU.mult))
            pool.wait_ge(s_hat[1], 1)
            me.add(g.memset(Wds[1], 0.0))
            for ky in range(3):
                me.link(g.tensor_tensor(hats1_y[:, ky], hats1_y[:, ky], mask[:, 1], ALU.mult))
            for ky in range(3):
                for kx in range(3):
                    me.link(g.tensor_tensor(wk1, hats1_y[:, ky].rearrange("p k g -> p (k g)"),
                                            hats1_x[:, kx].rearrange("p k g -> p (k g)"), ALU.mult))
                    window = Wds[1][:, kx:kx + 3, ky:ky + 3, :]
                    ins = g.tensor_tensor(window, window, wk1.rearrange("p (i j g) -> p i j g", i=3, j=3), ALU.add)
                    if ky == 2 and kx == 2:
                        ins.then_inc(s_wd[1], 1)
                    else:
                        me.link(ins)
            for n in range(len(plan)):
                if by_pool[n]:
                    await_product_inputs(pool, n)
                    if n in last_of_half:
                        me.link(product(g, n))
                        add_general(pool, g, any_beyond, n)
                        g.memset(small[:, 443:444], 0.0).then_inc(s_pp, 1)
                    else:
                        product(g, n).then_inc(s_pp, 1)
            pool.wait_ge(s_acc, len(plan))
            pool.wait_ge(s_mask, 2)
            zero_border().then_inc(s_zb, 1)
            pool.wait_ge(s_craw, 32)
            n = me.add(g.tensor_tensor(cwe[:, 0], craw[:, 0], craw[:, 1], ALU.add))
            me.add(g.tensor_tensor(craw[:, 2], craw[:, 2], ccoef[:, 0], ALU.mult))
            me.link(g.tensor_tensor(craw[:, 3], craw[:, 3], ccoef[:, 1], ALU.mult))
            me.link(g.tensor_scalar(cwe[:, 0], cwe[:, 0], 0.5, None, ALU.mult))
            g.tensor_tensor(cwe[:, 1], craw[:, 2], craw[:, 3], ALU.add).then_inc(s_cwe, 1)
            for i in range(TILES):
                pool.wait_ge(s_sq, i + 1)
                g.tensor_scalar(xp[:, i, :], xp[:, i, :], col("star_scale"), col("star_bias"), ALU.mult, ALU.add).then_inc(s_xpd, 1)
            for i in range(TILES):
                pool.wait_ge(s_ya, i + 1)
                pool.wait_ge(s_yb, i + 1)
                if i >= 2:
                    pool.wait_ge(s_i2, i - 1)
                g.tensor_tensor(y_w[i % 2], ya[i % 2], yb[i % 2], ALU.add).then_inc(s_y, 1)
            pool.wait_ge(s_x_new, 16)
            borders = padq.rearrange("p t b y x -> p (t b) y x")
            g.memset(borders[:, :, 0:2, :], 0.0)
            g.memset(borders[:, :, 2 + H:, :], 0.0)
            g.memset(borders[:, :, 2:2 + H, 0:2], 0.0)
            g.memset(borders[:, :, 2:2 + H, 2 + W:], 0.0).then_inc(s_qb, 1)
            for n, (t, tap, b) in enumerate(pool_taps):
                if tap == TENSOR_TAPS[t] and t == 5:
                    pool.wait_ge(s_yq, 4)
                pool.wait_ge(s_tp, n + 1)
                dst = local[t][:, b * PIX:(b + 1) * PIX]
                if tap == TENSOR_TAPS[t]:
                    g.tensor_copy(dst, tap_tmp(n)).then_inc(s_ta, 1)
                else:
                    pool.wait_ge(s_ta, n - 1)
                    g.tensor_tensor(dst, dst, tap_tmp(n), ALU.add).then_inc(s_ta, 1)
            pool.wait_ge(s_x_new, 24)
            zero_border().then_inc(s_zb, 1)
            for tap in range(9):
                pool.wait_ge(s_tp3, tap + 1)
                if tap == 0:
                    g.tensor_copy(h3[:, 1, :], tap3_tmp[0]).then_inc(s_dw3p, 1)
                else:
                    pool.wait_ge(s_dw3p, tap)
                    g.tensor_tensor(h3[:, 1, :], h3[:, 1, :], tap3_tmp[tap % 2], ALU.add).then_inc(s_dw3p, 1)


def host_arrays(**i):
    at, n = channel_columns()
    cv = np.zeros((P, n), np.float32)

    def put(name, a):
        a = np.asarray(a, np.float32).reshape(-1, P, *np.shape(a)[1:]).reshape(-1, P, int(np.prod(np.shape(a)[1:]) or 1))
        lo, hi = at[name]
        cv[:, lo:hi] = a.transpose(1, 0, 2).reshape(P, hi - lo)

    put("dw0_w", i["L0_conv_dw_w"].reshape(C, 9))
    for name, src in (("dw0_b", "dw_b"), ("ln_g", "ln_g"), ("ln_b", "ln_b"), ("out_b", "out_b")):
        put(name, i["L0_conv_" + src])
    r = {"chan_vecs": cv, "ident": np.eye(P, dtype=np.float32)}
    blocks = np.kron(np.eye(16, dtype=np.float32), np.ones((8, 8), np.float32))
    r["gmean"] = blocks / 8
    r["head_mask"] = blocks
    sc = np.zeros((P, 7), np.float32)
    sc[:, 0:3] = [1, 0, -1]
    part = np.repeat(FILTER_PART, NF)
    sc[:len(part), 3] = np.where(part >= 1, -1, 0)
    sc[:len(part), 4] = np.where(part >= 2, -1, 0)
    r["small_consts"] = sc
    for name in ("in_w", "in_b", "off_w", "off_b", "mask_w", "mask_b", "out_w"):
        r[name] = np.ascontiguousarray(i["L0_conv_" + name])
    put("star_scale", np.broadcast_to(i["L1_conv_star_scale"], (P,)))
    put("star_bias", np.broadcast_to(i["L1_conv_star_bias"], (P,)))
    put("fc1_b", i["L1_conv_rw_fc1_b"])
    put("conv_b", i["L1_conv_rw_conv_b"])
    put("sp1_b", i["L1_conv_sp_fc1_b"])
    r["fc1_w"] = i["L1_conv_rw_fc1_w"][:, :, 0, 0].T
    r["conv_w"] = i["L1_conv_rw_conv_w"][:, :, 0, 0].T
    r["pw1_w"] = i["L1_conv_w_pw1"].T
    r["pw2_w"] = i["L1_conv_w_pw2"].T
    r["sp1_w"] = i["L1_conv_sp_fc1_w"].reshape(P, C, 9).transpose(1, 2, 0)
    r["fc2_w"] = np.concatenate([i["L1_conv_rw_fc2_w"][:, :, 0, 0].T[None], i["L1_conv_sp_fc2_w"].reshape(-1, P, 9).transpose(2, 1, 0)])
    bias = np.stack([i["L1_conv_rw_fc2_b"]] * 2 + [i["L1_conv_sp_fc2_b"]] * 2)
    r["fc2_b"] = bias.reshape(4, NF * KM, P).transpose(2, 1, 0).reshape(P, 64)
    r["dft"] = dft_constants()
    first, second, sign = spectra_maps()
    cw = i["L1_conv_complex_weights"].transpose(2, 3, 0, 1)
    r["spectra"] = np.stack([cw[:, part, m[:, 0], m[:, 1]] for part in (0, 1) for m in (first, second)], 1)
    r["spectra"] = np.tile(r["spectra"], (PARTS, 1, 1))
    r["spectra_coef"] = np.broadcast_to(sign, (PARTS * NF, 2, 1024))
    r["spatial_w"] = i["L1_conv_spatial_weights"].reshape(P, WT, NF).transpose(2, 1, 0).reshape(NF, PIX)
    r["spatial_w"] = np.tile(r["spatial_w"], (PARTS, 1))
    chan = np.concatenate([[24 * (16 * gr + m // 8) + off + m % 8 for m in range(P)]
                           for gr, off in ((0, 8), (0, 16), (1, 8), (1, 16), (0, 0), (1, 0))])
    r["qkv_w"] = i["L2_conv_w_qkv"][chan].T
    put("dw2_w", i["L2_conv_w_dw"].reshape(-1, K5)[chan])
    r["pointwise_w"] = np.tile(i["L2_conv_w_pw"].reshape(-1, 8)[chan].T, (16, 1))
    r["proj_w"] = i["L2_conv_w_proj"].T
    hc = np.zeros((P, 32), np.float32)
    hc[np.arange(P), np.arange(P) // 8] = 1
    r["head_cols"] = hc
    hr = np.zeros((4, 32, P), np.float32)
    hr[:, np.arange(P) // 8, np.arange(P)] = 1
    r["head_rows"] = hr.reshape(P, P)
    for name, l2, l3 in (("bn_g", "gamma", "g"), ("bn_b", "beta", "b"), ("bn_m", "mean", "m"), ("bn_v", "var", "v")):
        put(name, np.concatenate([i["L2_conv_bn_" + l2], i["L3_conv_bn1_" + l3], i["L3_conv_bn2_" + l3]]))
    put("dw3_w", i["L3_conv_dw_w"].reshape(C, 9))
    put("l3_b", np.concatenate([i["L3_conv_dw_b"], i["L3_conv_pw_b"]]))
    r["pw3_w"] = i["L3_conv_pw_w"][:, :, 0, 0].T
    return {k: np.ascontiguousarray(a) for k, a in r.items()}


def dft_rows():
    rows = []
    for t in range(WT):
        if t == 0:
            for ky in (0, H // 2):
                rows += [(ky, kx, 0) for kx in range(17)] + [(ky, kx, 1) for kx in range(1, 16)]
        for ky in ([1] if t == 0 else [2 * t, 2 * t + 1]):
            rows += [(ky, kx, part) for part in (0, 1) for kx in range(W)]
    return rows


def dft_constants():
    comps = []
    for t in range(WT):
        comps.append([(0, 0), (H // 2, 0), (1, 0), (1, 1)] if t == 0 else [(2 * t, 0), (2 * t, 1), (2 * t + 1, 0), (2 * t + 1, 1)])
    f1 = np.zeros((P, P))
    for t in range(WT):
        for j, (ky, part) in enumerate(comps[t]):
            for y in range(H):
                ang = 2 * np.pi * ky * y / H
                val = (np.cos(ang) if part == 0 else -np.sin(ang)) / np.sqrt(H)
                for i in range(4):
                    f1[16 * t + 4 * j + i, 4 * y + i] = val
    rows = dft_rows()
    f2, f2s = np.zeros((2, P, P)), np.zeros((2, P, P))
    for a, t in enumerate((0, 1)):
        for m in range(P):
            ky, kx, part = rows[t * P + m]
            for j, (cy, cpart) in enumerate(comps[t]):
                if cy != ky:
                    continue
                for x in range(W):
                    q = 8 * (4 * j + x // 8) + x % 8
                    e = np.exp(-2j * np.pi * kx * x / W) / np.sqrt(W) * (1j if cpart else 1)
                    f2[a, m, q] = e.imag if part else e.real
                    f2s[a, m, q] = e.real if part else -e.imag
    mats = [f1.T, f2[0].T, f2[1].T, f2s[0].T, f2s[1].T, np.linalg.inv(f2[0]).T, np.linalg.inv(f2[1]).T,
            np.linalg.inv(f1).T]
    return np.stack(mats, 1).astype(np.float32)


def spectra_maps():
    first, second, sign = [], [], np.zeros((2, 1024), np.float32)
    for n, (ky, kx, part) in enumerate(dft_rows()):
        if kx in (0, W // 2):
            first.append((ky, kx)); second.append((-ky % H, kx)); sign[:, n] = 0.5, -0.5
        elif kx < W // 2:
            first.append((ky, kx)); second.append((ky, kx)); sign[:, n] = 0.5, 0.5
        else:
            first.append((-ky % H, W - kx)); second.append(first[-1]); sign[:, n] = -0.5, -0.5
    return np.array(first), np.array(second), sign


def kernel(**inputs):
    import concourse.bacc as bacc
    from concourse.bass_utils import run_bass_kernel_spmd

    inputs = {k: np.asarray(a) for k, a in inputs.items()}
    nc = bacc.Bacc("TRN2", target_bir_lowering=False, num_devices=1)
    arrays = {"x_dram": np.ascontiguousarray(inputs.pop("x").reshape(B, C, PIX))}
    arrays.update({k + "_dram": a for k, a in host_arrays(**inputs).items()})
    aps = {k[:-5]: nc.dram_tensor(k, a.shape, mybir.dt.from_np(a.dtype), kind="ExternalInput").ap() for k, a in arrays.items()}
    out = nc.dram_tensor("out_dram", (B, C, PIX), F32, kind="ExternalOutput").ap()
    pad_image = nc.dram_tensor("xproj_padded", (B, PADDED, PADDED, C), F32).ap()
    general = nc.dram_tensor("general_sample", (HALVES, P, XX * P), F32).ap()
    aps["bounce"] = nc.dram_tensor("bounce", (2, B, P, WT, MED), F32).ap()
    mixer_kernel(nc, aps.pop("x"), out, aps, pad_image, general)
    r = run_bass_kernel_spmd(nc, [arrays], core_ids=[0])
    return r.results[0]["out_dram"].reshape(B, C, H, W)
```
